# Optimizing a Trainium2 kernel written in Bass

```python
import numpy as np
import jax
import jax.numpy as jnp

def _softmax(x, axis=-1):
    return jax.nn.softmax(x, axis=axis)

def _gelu(x):
    return jax.nn.gelu(x, approximate=True)

def _silu(x):
    return jax.nn.silu(x)

def _sigmoid(x):
    return jax.nn.sigmoid(x)

def _layernorm(x, axis=-1, eps=1e-05):
    m = jnp.mean(x, axis=axis, keepdims=True)
    v = jnp.var(x, axis=axis, keepdims=True)
    return (x - m) / jnp.sqrt(v + eps)

def _scatter_add(tgt, idx, src, axis=0):
    return tgt.at[idx].add(src)

def _segment_sum(src, seg, n):
    return jax.ops.segment_sum(src, seg, n)
kernel_name = 'mk_audio_tower_d2_tok_audfeat1024_r4_02861c'

def setup_inputs(seed: int=0):
    np.random.seed(seed)
    _w = jnp.asarray

    def _rec_inputs():
        import jax
        import jax.numpy as jnp
        _rk = jax.random.key(seed)
        x = -0.000125008 + 0.999885 * jax.random.normal(jax.random.fold_in(_rk, 1), (4, 128, 750), jnp.float32)
        return x
    x = _rec_inputs()

    def _L0_tok_setup():
        import jax, jax.numpy as jnp
        import numpy as np
        from jax import lax
        ALPHA = 0.1
        B, C_IN, T, D_MODEL = (32, 128, 512, 256)

        def _ewma_scan(xt):

            def step(carry, xi):
                carry = ALPHA * xi + (1.0 - ALPHA) * carry
                return (carry, carry)
            _, ys = lax.scan(step, xt[0], xt[1:])
            return jnp.concatenate([xt[:1], ys], axis=0)
        key = jax.random.key(seed)
        k_x, k_w, k_b = jax.random.split(key, 3)
        x = jax.random.normal(k_x, (B, C_IN, T), dtype=jnp.float32)
        bound = 1.0 / np.sqrt(C_IN)
        W = jax.random.uniform(k_w, (D_MODEL, C_IN), dtype=jnp.float32, minval=-bound, maxval=bound)
        b = jax.random.uniform(k_b, (D_MODEL,), dtype=jnp.float32, minval=-bound, maxval=bound)
        return {'x': x, 'W': W, 'b': b}
    _L0_tok_all = _L0_tok_setup()
    _L0_tok_in = {k: v for k, v in _L0_tok_all.items() if k in ('W', 'b')}
    del _L0_tok_all

    def _L0_attn_setup():
        import jax, jax.numpy as jnp
        import numpy as np
        B, T, H, DK, DV = (4, 512, 256, 256, 256)
        key = jax.random.key(seed)
        ks = jax.random.split(key, 9)
        s = lambda fan_in: 1.0 / np.sqrt(fan_in)
        return {'y_all': jax.random.normal(ks[0], (B, T, H), dtype=jnp.float32), 'Wq': jax.random.uniform(ks[1], (H, DK), jnp.float32, -s(H), s(H)), 'bq': jax.random.uniform(ks[2], (DK,), jnp.float32, -s(H), s(H)), 'Wk': jax.random.uniform(ks[3], (H, DK), jnp.float32, -s(H), s(H)), 'bk': jax.random.uniform(ks[4], (DK,), jnp.float32, -s(H), s(H)), 'Wv': jax.random.uniform(ks[5], (H, DV), jnp.float32, -s(H), s(H)), 'bv': jax.random.uniform(ks[6], (DV,), jnp.float32, -s(H), s(H)), 'Wo': jax.random.uniform(ks[7], (DV, H), jnp.float32, -s(DV), s(DV)), 'bo': jax.random.uniform(ks[8], (H,), jnp.float32, -s(DV), s(DV))}
    _L0_attn_all = _L0_attn_setup()
    _L0_attn_in = {k: v for k, v in _L0_attn_all.items() if k in ('Wq', 'bq', 'Wk', 'bk', 'Wv', 'bv', 'Wo', 'bo')}
    del _L0_attn_all

    def _L0_ffn_setup():
        import jax, jax.numpy as jnp
        import numpy as np
        E = 8
        TOPK = 2
        H = 256
        I = 256
        ISH = I * 2
        B, S = (2, 256)
        key = jax.random.key(seed)
        ks = jax.random.split(key, 7)
        s = 0.02
        return {'hidden_states': jax.random.normal(ks[0], (B, S, H), jnp.float32), 'w_router': jax.random.normal(ks[1], (H, E), jnp.float32) * s, 'fc1_w': jax.random.normal(ks[2], (E, H, 2 * I), jnp.float32) * s, 'fc2_w': jax.random.normal(ks[3], (E, I, H), jnp.float32) * s, 'gate_w': jax.random.normal(ks[4], (H, ISH), jnp.float32) * s, 'up_w': jax.random.normal(ks[5], (H, ISH), jnp.float32) * s, 'down_w': jax.random.normal(ks[6], (ISH, H), jnp.float32) * s}
    _L0_ffn_all = _L0_ffn_setup()
    _L0_ffn_in = {k: v for k, v in _L0_ffn_all.items() if k in ('w_router', 'fc1_w', 'fc2_w', 'gate_w', 'up_w', 'down_w')}
    del _L0_ffn_all

    def _L1_attn_setup():
        import jax, jax.numpy as jnp
        import numpy as np
        B, T = (4, 512)
        D_MODEL = 256
        N_HEADS = 8
        HEAD_DIM = 64
        KV_LRANK = 64

        def _orthogonalize_per_head(w):
            chunks = w.reshape(N_HEADS, HEAD_DIM, D_MODEL)

            def ns(m):
                A = m @ m.T
                Bm = 1.5 * jnp.eye(HEAD_DIM, dtype=m.dtype) - 0.5 * A
                return Bm @ m
            return jax.vmap(ns)(chunks).reshape(w.shape)
        key = jax.random.key(seed)
        ks = jax.random.split(key, 6)

        def lin(k, out_dim, in_dim):
            bound = 1.0 / np.sqrt(in_dim)
            return jax.random.uniform(k, (out_dim, in_dim), jnp.float32, -bound, bound)
        Wq = _orthogonalize_per_head(lin(ks[0], N_HEADS * HEAD_DIM, D_MODEL))
        return {'x': jax.random.normal(ks[1], (B, T, D_MODEL), jnp.float32), 'Wq': Wq, 'Wkv_down': lin(ks[2], KV_LRANK, D_MODEL), 'Wk_up': lin(ks[3], N_HEADS * HEAD_DIM, KV_LRANK), 'Wv_up': lin(ks[4], N_HEADS * HEAD_DIM, KV_LRANK), 'Wo': lin(ks[5], D_MODEL, N_HEADS * HEAD_DIM)}
    _L1_attn_all = _L1_attn_setup()
    _L1_attn_in = {k: v for k, v in _L1_attn_all.items() if k in ('Wq', 'Wkv_down', 'Wk_up', 'Wv_up', 'Wo')}
    del _L1_attn_all

    def _L1_ffn_setup():
        import jax, jax.numpy as jnp
        import numpy as np
        EPS = 1e-06
        LN_EPS = 1e-05

        def _absmean_core(W):
            gamma = jnp.mean(jnp.abs(W)) + EPS
            Ws = W / gamma
            Wq = jnp.sign(Ws) * jnp.minimum(jnp.round(jnp.abs(Ws)), 1.0)
            return (Wq, gamma)

        @jax.custom_vjp
        def absmean(W):
            return _absmean_core(W)[0]

        def _absmean_fwd(W):
            Wq, gamma = _absmean_core(W)
            return (Wq, gamma)

        def _absmean_bwd(gamma, g):
            return (g / gamma,)
        absmean.defvjp(_absmean_fwd, _absmean_bwd)

        def layernorm(x, w, b, eps=LN_EPS):
            mu = jnp.mean(x, axis=-1, keepdims=True)
            var = jnp.mean((x - mu) ** 2, axis=-1, keepdims=True)
            return (x - mu) * jax.lax.rsqrt(var + eps) * w + b
        key = jax.random.key(seed)
        k1, k2, k3 = jax.random.split(key, 3)
        d, h = (256, 1024)
        B, T = (8, 512)
        return {'x': jax.random.normal(k1, (B, T, d), jnp.float32), 'W_fc': jax.random.normal(k2, (h, d), jnp.float32), 'ln_w': jnp.ones((h,), jnp.float32), 'ln_b': jnp.zeros((h,), jnp.float32), 'W_proj': jax.random.normal(k3, (d, h), jnp.float32)}
    _L1_ffn_all = _L1_ffn_setup()
    _L1_ffn_in = {k: v for k, v in _L1_ffn_all.items() if k in ('W_fc', 'ln_w', 'ln_b', 'W_proj')}
    del _L1_ffn_all
    return {'x': x, 'L0_tok_W': _L0_tok_in['W'], 'L0_tok_b': _L0_tok_in['b'], 'L0_attn_Wq': _L0_attn_in['Wq'], 'L0_attn_bq': _L0_attn_in['bq'], 'L0_attn_Wk': _L0_attn_in['Wk'], 'L0_attn_bk': _L0_attn_in['bk'], 'L0_attn_Wv': _L0_attn_in['Wv'], 'L0_attn_bv': _L0_attn_in['bv'], 'L0_attn_Wo': _L0_attn_in['Wo'], 'L0_attn_bo': _L0_attn_in['bo'], 'L0_ffn_w_router': _L0_ffn_in['w_router'], 'L0_ffn_fc1_w': _L0_ffn_in['fc1_w'], 'L0_ffn_fc2_w': _L0_ffn_in['fc2_w'], 'L0_ffn_gate_w': _L0_ffn_in['gate_w'], 'L0_ffn_up_w': _L0_ffn_in['up_w'], 'L0_ffn_down_w': _L0_ffn_in['down_w'], 'L1_attn_Wq': _L1_attn_in['Wq'], 'L1_attn_Wkv_down': _L1_attn_in['Wkv_down'], 'L1_attn_Wk_up': _L1_attn_in['Wk_up'], 'L1_attn_Wv_up': _L1_attn_in['Wv_up'], 'L1_attn_Wo': _L1_attn_in['Wo'], 'L1_ffn_W_fc': _L1_ffn_in['W_fc'], 'L1_ffn_ln_w': _L1_ffn_in['ln_w'], 'L1_ffn_ln_b': _L1_ffn_in['ln_b'], 'L1_ffn_W_proj': _L1_ffn_in['W_proj']}

def reference(x, L0_tok_W, L0_tok_b, L0_attn_Wq, L0_attn_bq, L0_attn_Wk, L0_attn_bk, L0_attn_Wv, L0_attn_bv, L0_attn_Wo, L0_attn_bo, L0_ffn_w_router, L0_ffn_fc1_w, L0_ffn_fc2_w, L0_ffn_gate_w, L0_ffn_up_w, L0_ffn_down_w, L1_attn_Wq, L1_attn_Wkv_down, L1_attn_Wk_up, L1_attn_Wv_up, L1_attn_Wo, L1_ffn_W_fc, L1_ffn_ln_w, L1_ffn_ln_b, L1_ffn_W_proj):
    import jax
    import jax.numpy as jnp

    def _L0_tok_ref(x, W, b):
        import jax, jax.numpy as jnp
        import numpy as np
        from jax import lax
        ALPHA = 0.1
        B, C_IN, T, D_MODEL = (32, 128, 512, 256)

        def _ewma_scan(xt):

            def step(carry, xi):
                carry = ALPHA * xi + (1.0 - ALPHA) * carry
                return (carry, carry)
            _, ys = lax.scan(step, xt[0], xt[1:])
            return jnp.concatenate([xt[:1], ys], axis=0)
        xp = jnp.transpose(x, (0, 2, 1))
        xt = jnp.moveaxis(xp, 1, 0)
        fwd = _ewma_scan(xt)
        bwd = _ewma_scan(xt[::-1])[::-1]
        ewma = jnp.moveaxis((fwd + bwd) * 0.5, 0, 1)
        return jnp.einsum('btc,dc->btd', ewma, W) + b

    def _L0_attn_ref(y_all, Wq, bq, Wk, bk, Wv, bv, Wo, bo):
        import jax, jax.numpy as jnp
        import numpy as np
        B, T, H, DK, DV = (4, 512, 256, 256, 256)
        dk = Wq.shape[1]
        q = (y_all @ Wq + bq) / jnp.sqrt(jnp.asarray(dk, y_all.dtype))
        k = y_all @ Wk + bk
        v = y_all @ Wv + bv
        scores = jnp.einsum('bqd,bkd->bqk', q, k)
        t = y_all.shape[1]
        causal = jnp.tril(jnp.ones((t, t), dtype=bool))
        scores = jnp.where(causal[None], scores, jnp.asarray(-jnp.inf, scores.dtype))
        w = jax.nn.softmax(scores, axis=-1)
        ctx = jnp.einsum('bqk,bkd->bqd', w, v)
        return ctx @ Wo + bo

    def _L0_ffn_ref(hidden_states, w_router, fc1_w, fc2_w, gate_w, up_w, down_w):
        import jax, jax.numpy as jnp
        import numpy as np
        E = 8
        TOPK = 2
        H = 256
        I = 256
        ISH = I * 2
        B, S = (2, 256)
        orig_shape = hidden_states.shape
        x = hidden_states.reshape(-1, orig_shape[-1])
        logits = x @ w_router
        top_logits, top_idx = jax.lax.top_k(logits, TOPK)
        scores = jax.nn.softmax(top_logits, axis=-1)
        flat_idx = top_idx.reshape(-1)
        sorted_idx = jnp.argsort(flat_idx)
        permuted = x[sorted_idx // TOPK]
        eid = flat_idx[sorted_idx]
        out_perm = jnp.zeros((permuted.shape[0], orig_shape[-1]), x.dtype)
        for e in range(E):
            m = (eid == e).astype(x.dtype)[:, None]
            h1 = permuted * m @ fc1_w[e]
            proj, gate = jnp.split(h1, 2, axis=-1)
            out_perm = out_perm + jax.nn.silu(proj) * gate @ fc2_w[e]
        unperm = jnp.zeros_like(out_perm).at[sorted_idx].set(out_perm)
        moe_out = (unperm.reshape(-1, TOPK, orig_shape[-1]) * scores[:, :, None]).sum(axis=1)
        moe_out = moe_out.reshape(orig_shape)
        shared = jax.nn.silu(hidden_states @ gate_w) * (hidden_states @ up_w) @ down_w
        return moe_out + shared

    def _L1_attn_ref(x, Wq, Wkv_down, Wk_up, Wv_up, Wo):
        import jax, jax.numpy as jnp
        import numpy as np
        B, T = (4, 512)
        D_MODEL = 256
        N_HEADS = 8
        HEAD_DIM = 64
        KV_LRANK = 64

        def _orthogonalize_per_head(w):
            chunks = w.reshape(N_HEADS, HEAD_DIM, D_MODEL)

            def ns(m):
                A = m @ m.T
                Bm = 1.5 * jnp.eye(HEAD_DIM, dtype=m.dtype) - 0.5 * A
                return Bm @ m
            return jax.vmap(ns)(chunks).reshape(w.shape)
        b, t, _ = x.shape
        q = (x @ Wq.T).reshape(b, t, N_HEADS, HEAD_DIM)
        kv_latent = x @ Wkv_down.T
        k = (kv_latent @ Wk_up.T).reshape(b, t, N_HEADS, HEAD_DIM)
        v = (kv_latent @ Wv_up.T).reshape(b, t, N_HEADS, HEAD_DIM)
        scale = HEAD_DIM ** (-0.5)
        scores = jnp.einsum('bqhd,bkhd->bhqk', q, k) * scale
        attn = jax.nn.softmax(scores, axis=-1)
        out = jnp.einsum('bhqk,bkhd->bqhd', attn, v)
        out = out.reshape(b, t, N_HEADS * HEAD_DIM)
        return out @ Wo.T

    def _L1_ffn_ref(x, W_fc, ln_w, ln_b, W_proj):
        import jax, jax.numpy as jnp
        import numpy as np
        EPS = 1e-06
        LN_EPS = 1e-05

        def _absmean_core(W):
            gamma = jnp.mean(jnp.abs(W)) + EPS
            Ws = W / gamma
            Wq = jnp.sign(Ws) * jnp.minimum(jnp.round(jnp.abs(Ws)), 1.0)
            return (Wq, gamma)

        @jax.custom_vjp
        def absmean(W):
            return _absmean_core(W)[0]

        def _absmean_fwd(W):
            Wq, gamma = _absmean_core(W)
            return (Wq, gamma)

        def _absmean_bwd(gamma, g):
            return (g / gamma,)
        absmean.defvjp(_absmean_fwd, _absmean_bwd)

        def layernorm(x, w, b, eps=LN_EPS):
            mu = jnp.mean(x, axis=-1, keepdims=True)
            var = jnp.mean((x - mu) ** 2, axis=-1, keepdims=True)
            return (x - mu) * jax.lax.rsqrt(var + eps) * w + b
        h = jnp.einsum('btd,hd->bth', x, absmean(W_fc))
        h = jax.nn.gelu(h, approximate=False)
        h = layernorm(h, ln_w, ln_b)
        return jnp.einsum('bth,dh->btd', h, absmean(W_proj))
    h = _L0_tok_ref(x, L0_tok_W, L0_tok_b)
    h = h + _L0_attn_ref(_layernorm(h, axis=-1), L0_attn_Wq, L0_attn_bq, L0_attn_Wk, L0_attn_bk, L0_attn_Wv, L0_attn_bv, L0_attn_Wo, L0_attn_bo)
    h = h + _L0_ffn_ref(_layernorm(h, axis=-1), L0_ffn_w_router, L0_ffn_fc1_w, L0_ffn_fc2_w, L0_ffn_gate_w, L0_ffn_up_w, L0_ffn_down_w)
    h = h + _L1_attn_ref(_layernorm(h, axis=-1), L1_attn_Wq, L1_attn_Wkv_down, L1_attn_Wk_up, L1_attn_Wv_up, L1_attn_Wo)
    h = h + _L1_ffn_ref(_layernorm(h, axis=-1), L1_ffn_W_fc, L1_ffn_ln_w, L1_ffn_ln_b, L1_ffn_W_proj)
    return h

_drawn_inputs = setup_inputs


def setup_inputs(seed=0):
    import zlib

    import numpy as np

    out = dict(_drawn_inputs(seed))
    spreads = {'L1_ffn_ln_w': (1.0, 0.2), 'L1_ffn_ln_b': (0.0, 0.1)}
    factors = {'L0_attn_bq': 8.0, 'L0_attn_bk': 8.0}
    for name, (base, spread) in spreads.items():
        noise = np.random.default_rng([zlib.crc32(name.encode()), seed]).standard_normal(out[name].shape)
        drawn = base * np.exp(spread * noise) if base else spread * noise
        out[name] = jnp.asarray(drawn.astype(out[name].dtype))
    for name, factor in factors.items():
        out[name] = (out[name] * factor).astype(out[name].dtype)
    return out
```

```python
from contextlib import ExitStack

import numpy as np
import concourse.bass as bass
from concourse import mybir

F32 = mybir.dt.float32
F32R = mybir.dt.float32r
I32 = mybir.dt.int32
U32 = mybir.dt.uint32
ALU = mybir.AluOpType
ACT = mybir.ActivationFunctionType
AX = mybir.AxisListType

B, C, T, D = 4, 128, 750, 256
TT = 125
NT = T // TT
NG = B * NT
KD = D // 128
E, I, ISH = 8, 256, 512
SLOT = 128
NSLOT = (2 * B * T - E) // SLOT + E
LH, HD, LAT = 8, 64, 64
PAIRS = LH // 2
FH = 1024
FB = FH // 128
BANK = 512
HALF = T // 2
RING = 4
GT = 3 * TT
NGR = NG // 3
GAMMA_EPS = 1e-6
STEPS = 2 * NT
ALPHA = 0.1
LN_EPS = 1e-5
MASKED = -1.0e30
RSQRT_SEED = 0x5F3759DF
NEWTON = 3
LN_CHAIN = 3 + 3 * NEWTON


def build(nc, a, out):
    with ExitStack() as ctx:
        def sb(name, shape, dt=F32):
            return ctx.enter_context(nc.sbuf_tensor(name, shape, dt))

        def sem(name):
            return ctx.enter_context(nc.semaphore(name))

        KB = 60 * 1024
        early_at = (nc.sbuf_base + 31) // 32 * 32
        sb("early", [128, KB // 4])
        late_at = (nc.sbuf_base + 31) // 32 * 32
        sb("late", [128, KB // 4])

        def lay(start, *tensors):
            handles = []
            for name, shape, dt in tensors:
                handles.append(nc.alloc_sbuf_tensor_at(name, [128, *shape], dt, offset=start))
                start += (4 * int(np.prod(shape)) + 31) // 32 * 32
            return handles + [start]

        h = sb("h", [128, NG, D])
        ident = sb("ident", [128, 128])
        xn = sb("xn", [128, NT, D])
        xT = sb("xT", [128, KD, T])
        probs = sb("probs", [128, 2, T])
        (w_tok, b_tok, bv0, bo0, wq0, wk0, wv0, wo0, x_in, x_scaled, fwd, bwd, ewma, qT, kT, v0, pT, end) = lay(
            early_at, ("w_tok", [D], F32), ("b_tok", [D], F32), ("bv0", [D], F32), ("bo0", [D], F32),
            ("wq0", [KD, D], F32), ("wk0", [KD, D], F32), ("wv0", [KD, D], F32), ("wo0", [KD, D], F32),
            ("x_in", [B, T], F32), ("x_scaled", [T], F32), ("fwd", [T], F32), ("bwd", [T], F32), ("ewma", [T], F32),
            ("qT", [KD, T], F32), ("kT", [KD, T], F32), ("v0", [NT, D], F32), ("pT", [2, NT, TT], F32))
        assert end <= early_at + KB
        ctxt = sb("ctxt", [128, D])
        ctxT = sb("ctxT", [128, KD, TT])
        decay = sb("decay", [128, 1])
        bq0 = sb("bq0", [128, KD])
        bq0s = sb("bq0s", [128, KD])
        bk0 = sb("bk0", [128, KD])
        mask = sb("mask", [128, TT])
        fc1, fc2, gate, up, down, end = lay(
            late_at, ("fc1", [E, KD, 2 * I], F32), ("fc2", [E, KD, D], F32), ("gate", [KD, ISH], F32),
            ("up", [KD, ISH], F32), ("down", [ISH // 128, D], F32))
        assert end <= late_at + KB
        act_s, x_all, after_rows = lay(early_at, ("act_s", [ISH // 128, 2 * HALF], F32), ("x_all", [NG, D], F32))
        xT_all, end = lay(after_rows, ("xT_all", [KD, B * T], F32))
        assert end <= early_at + KB
        xg, xgT, silu, u, uT, y_out, ring_at = lay(
            after_rows, ("xg", [2, D], F32), ("xgT", [2, KD, SLOT], F32), ("silu", [2, I], F32), ("u", [2, I], F32),
            ("uT", [2, KD, SLOT], F32), ("y_out", [2, D], F32))
        ring, end = lay(ring_at, ("ring", [RING, 2, D], F32))
        wq1, wk_up, wv_up, wo1, end = lay(
            early_at + 4 * 2 * HALF * ISH // 128, ("wq1", [LH, D], F32), ("wk_up", [LH, LAT], F32),
            ("wv_up", [LH, LAT], F32), ("wo1", [LH, D], F32))
        assert end <= after_rows
        heads_out, heads_end = lay(after_rows, ("heads_out", [NT, LH * LAT], F32))
        assert heads_end <= ring_at
        oT, end = lay(end, ("oT", [2, LH * LAT // 128, TT], F32))
        assert end <= after_rows
        q_st0, q_st1, k_hi, k_lo, v_st, pT_hi, pT_lo, w_qk, w_vo, w_kv, w_qp, end = lay(
            late_at, ("q_st0", [T], F32R), ("q_st1", [T], F32R), ("k_hi", [T], F32R), ("k_lo", [T], F32R),
            ("v_st", [NT, 2 * LAT], F32R), ("pT_hi", [2, NT, 128], F32R), ("pT_lo", [2, NT, 128], F32R),
            ("w_qk", [PAIRS, KD, 128], F32), ("w_vo", [PAIRS, D], F32), ("w_kv", [KD, 2 * LAT], F32),
            ("w_qp", [KD, 128], F32))
        assert end <= late_at + KB
        o_half = sb("o_half", [128, LAT])
        wf_at = (nc.sbuf_base + 31) // 32 * 32
        sb("ternary_room", [128, KD * FH + FB * D])
        wf_raw, wp_raw, end = lay(wf_at, ("wf_raw", [KD * FH], F32), ("wp_raw", [FB * D], F32))
        w_f, w_p, end = lay(wf_at, ("w_f", [KD, FH], F32R), ("w_p", [FB, D], F32R))
        x_hi, x_lo, n_hi, n_lo, end = lay(
            late_at, ("x_hi", [KD, GT], F32R), ("x_lo", [KD, GT], F32R), ("n_hi", [FB, GT], F32R),
            ("n_lo", [FB, GT], F32R))
        assert end <= late_at + KB
        hidden, end = lay(early_at, ("hidden", [2, 3, FH], F32))
        ln_w = sb("ln_w", [128, FB])
        ln_b = sb("ln_b", [128, FB])
        b_out = sb("b_out", [128, D])
        absum = sb("absum", [128, 2])
        above = sb("above", [128, 2])
        below = sb("below", [128, 2])
        bn_f = sb("bn_f", [128, 3, 2, 6])
        mv_f = sb("mv_f", [128, 3, 2])
        ve_f = sb("ve_f", [128, 3])
        yr_f = sb("yr_f", [128, 3])
        yt_f = sb("yt_f", [128, 3])
        nm_f = sb("nm_f", [128, 3])
        silu_s = sb("silu_s", [128, 2, HALF])
        router = sb("router", [128, KD, E])
        logits = sb("logits", [128, NT, E])
        top = sb("top", [128, NT, 8])
        top_i = sb("top_i", [128, NT, 8], U32)
        top_f = sb("top_f", [128, NT, 2])
        gap = sb("gap", [128, 2, NT])
        share = sb("share", [128, 2, NG])
        hot = sb("hot", [128, 2, NG, E])
        hots = sb("hots", [128, NG, E])
        iota_e = sb("iota_e", [128, E])
        iota_j = sb("iota_j", [128, NSLOT])
        iota_c = sb("iota_c", [128, NG])
        before = sb("before", [128, TT])
        ones = sb("ones", [128, 128])
        restart = sb("restart", [128, E, NG])
        tot = sb("tot", [128, E, NG])
        incl = sb("incl", [128, E, NG])
        base = sb("base", [128, E, NG])
        over = sb("over", [128, E, NG])
        n_slots = sb("n_slots", [128, E])
        slot_end = sb("slot_end", [128, E])
        slot_beg = sb("slot_beg", [128, E])
        place = sb("place", [128, NG, E])
        picked = sb("picked", [128, 2, NG, E])
        row_f = sb("row_f", [128, 2, NG])
        row = sb("row", [128, 2, NG], I32)
        ended = sb("ended", [1, NSLOT, E])
        slot_e_f = sb("slot_e_f", [1, NSLOT])
        slot_e = sb("slot_e", [1, NSLOT], I32)
        zeros = sb("zeros", [128, D])
        bn6 = sb("bn6", [128, NT, 6])
        mv = sb("mv", [128, NT, 2])
        ve = sb("ve", [128, NT])
        yr = sb("yr", [128, NT])
        yt = sb("yt", [128, NT])
        negmax = sb("negmax", [128, 2])
        rowsum = sb("rowsum", [128, 2])
        rinv = sb("rinv", [128, 2])
        rinv1 = sb("rinv1", [128, 4])

        xs_dram = nc.dram_tensor("xs_dram", [NSLOT * SLOT, D], F32, kind="Internal").ap()
        ys_dram = nc.dram_tensor("ys_dram", [NSLOT * SLOT, D], F32, kind="Internal").ap()

        PS = ctx.enter_context(nc.psum_tensor("PS", [128, 8 * BANK], F32))

        def bank(i, lo=0, hi=BANK, p0=0, p1=128):
            return PS[p0:p1, i * BANK + lo:i * BANK + hi]

        x_loaded, wA_loaded = sem("x_loaded"), sem("wA_loaded")
        const_made, ident_made = sem("const_made"), sem("ident_made")
        ew_step, tok_mm, h_tok = sem("ew_step"), sem("tok_mm"), sem("h_tok")
        ln_seq, xn_ready, xn_turned, xT_ready = sem("ln_seq"), sem("xn_ready"), sem("xn_turned"), sem("xT_ready")
        qk_mm, qk_ready, v_mm, v_ready = sem("qk_mm"), sem("qk_ready"), sem("v_mm"), sem("v_ready")
        s_mm, s_masked, max_ready, probs_ready = sem("s_mm"), sem("s_masked"), sem("max_ready"), sem("probs_ready")
        p_turned, pT_ready, pv_mm, rinv_ready = sem("p_turned"), sem("pT_ready"), sem("pv_mm"), sem("rinv_ready")
        ctx_ready, ctx_turned, ctxT_ready, wo_mm = sem("ctx_ready"), sem("ctx_turned"), sem("ctxT_ready"), sem("wo_mm")
        h_biased, h_attn = sem("h_biased"), sem("h_attn")
        stored = sem("stored")
        wM_loaded, zeroed = sem("wM_loaded"), sem("zeroed")
        x_kept, router_mm, logits_ready, routed, share_exp = (sem("x_kept"), sem("router_mm"), sem("logits_ready"),
                                                              sem("routed"), sem("share_exp"))
        gap_ready, hots_ready, rank_mm, rows_step, rows_ready = (sem("gap_ready"), sem("hots_ready"), sem("rank_mm"),
                                                                 sem("rows_step"), sem("rows_ready"))
        consts_m = sem("consts_m")
        scattered = sem("scattered")
        gu_mm, silu_s_ready, act_s_ready, down_mm, h_shared = (sem("gu_mm"), sem("silu_s_ready"), sem("act_s_ready"),
                                                               sem("down_mm"), sem("h_shared"))
        xg_loaded = [sem("xg_loaded0"), sem("xg_loaded1")]
        y_stored = [sem("y_stored0"), sem("y_stored1")]
        xg_turned, xgT_ready, fc1_mm, silu_ready, u_ready = (sem("xg_turned"), sem("xgT_ready"), sem("fc1_mm"),
                                                             sem("silu_ready"), sem("u_ready"))
        u_turned, uT_ready, fc2_mm, y_ready = sem("u_turned"), sem("uT_ready"), sem("fc2_mm"), sem("y_ready")
        gathered = [sem(f"gathered{r}") for r in range(RING)]
        h_moe = sem("h_moe")
        wF_loaded, absum_ready, gamma_mm, tern_step = sem("wF_loaded"), sem("absum_ready"), sem("gamma_mm"), sem("tern_step")
        bias_split, bias_mm, b_out_ready, h_biased2 = sem("bias_split"), sem("bias_mm"), sem("b_out_ready"), sem("h_biased2")
        lnx_seq, fx_ready, fx_turned, x_hi_ready, x_split = (sem("lnx_seq"), sem("fx_ready"), sem("fx_turned"),
                                                             sem("x_hi_ready"), sem("x_split"))
        fc_mm, gelu_ready, lnf_seq, norm_ready = sem("fc_mm"), sem("gelu_ready"), sem("lnf_seq"), sem("norm_ready")
        n_turned, n_hi_ready, n_split, proj_mm, h_out = (sem("n_turned"), sem("n_hi_ready"), sem("n_split"),
                                                         sem("proj_mm"), sem("h_out"))
        wC_loaded, w_mm, w_folded, w_picked = sem("wC_loaded"), sem("w_mm"), sem("w_folded"), sem("w_picked")
        kv_mm, kv_hi, kv_ready = sem("kv_mm"), sem("kv_hi"), sem("kv_ready")
        q_mm, q_hi, q_ready = sem("q_mm"), sem("q_hi"), sem("q_ready")
        s1_mm, max1_ready, probs1_ready = sem("s1_mm"), sem("max1_ready"), sem("probs1_ready")
        p1_turned, p1_hi, p1_ready, pv1_mm = sem("p1_turned"), sem("p1_hi"), sem("p1_ready"), sem("pv1_mm")
        rinv1_ready, o_half_ready, o_ready = sem("rinv1_ready"), sem("o_half_ready"), sem("o_ready")
        o_turned, oT_ready, out1_mm, h_lat = sem("o_turned"), sem("oT_ready"), sem("out1_mm"), sem("h_lat")

        passed = {"dve": sem("dve_passed"), "pool": sem("pool_passed")}
        passes = {"dve": 0, "pool": 0}

        def wait_apart(eng, name, s, value, times):
            eng.wait_ge(s, value)
            eng.sem_inc(passed[name], 1)
            passes[name] += times

        def rsqrt(dve, var, y, e, t, seq, at):
            dve.tensor_scalar(e, var, LN_EPS, None, ALU.add).then_inc(seq, 1)
            dve.wait_ge(seq, at + 1)
            dve.tensor_scalar(y.bitcast(I32), e.bitcast(I32), 1, None, ALU.logical_shift_right).then_inc(seq, 1)
            dve.wait_ge(seq, at + 2)
            dve.tensor_scalar(y.bitcast(I32), y.bitcast(I32), -1.0, float(RSQRT_SEED), ALU.mult, ALU.add).then_inc(seq, 1)
            for k in range(NEWTON):
                dve.wait_ge(seq, at + 3 + 3 * k)
                dve.scalar_tensor_tensor(t, y, 0.5, y, ALU.mult, ALU.mult).then_inc(seq, 1)
                dve.wait_ge(seq, at + 4 + 3 * k)
                dve.tensor_tensor(t, t, e, ALU.mult).then_inc(seq, 1)
                dve.wait_ge(seq, at + 5 + 3 * k)
                dve.scalar_tensor_tensor(y, t, 1.5, y, ALU.subtract, ALU.mult, reverse0=True).then_inc(seq, 1)

        LN_CALL = 2 * NT + LN_CHAIN
        R_CALL = 2 * NT + 7
        LNX_CALL = 6 + LN_CHAIN
        LNF_CALL = 9 + LN_CHAIN + 1

        def layernorm(dve, g0, at, times, n=NT, seq=ln_seq, ready=xn_ready):
            for t in range(n):
                dve.bn_stats(bn6[0:TT, t, :], h[0:TT, g0 + t, :]).then_inc(seq, 1)
            wait_apart(dve, "dve", seq, at + n, times)
            for t in range(n):
                dve.bn_aggr(mv[0:TT, t, :], bn6[0:TT, t, :]).then_inc(seq, 1)
            dve.wait_ge(seq, at + 2 * n)
            rsqrt(dve, mv[0:TT, 0:n, 1], yr[0:TT, 0:n], ve[0:TT, 0:n], yt[0:TT, 0:n], seq, at + 2 * n)
            dve.wait_ge(seq, at + 2 * n + LN_CHAIN)
            for t in range(n):
                dve.tensor_scalar(xn[0:TT, t, :], h[0:TT, g0 + t, :], mv[0:TT, t, 0:1], yr[0:TT, t:t + 1],
                                  ALU.subtract, ALU.mult).then_inc(ready, 1)

        block = ctx.enter_context(nc.Block())

        @block.sync
        def _(sp):
            sp.dma_start(x_in[:, :, :], a["x"].rearrange("b c t -> c b t")).then_inc(x_loaded, 16)
            sp.dma_start(w_tok[:, :], a["tok_wT"]).then_inc(wA_loaded, 16)
            sp.dma_start(b_tok[0:TT, :], a["tok_b"].partition_broadcast(TT)).then_inc(wA_loaded, 16)
            for w, n in ((wq0, "wq0"), (wk0, "wk0"), (wv0, "wv0"), (wo0, "wo0")):
                sp.dma_start(w[:, :, :], a[n]).then_inc(wA_loaded, 16)
            sp.dma_start(bq0[:, :], a["bq0"]).then_inc(wA_loaded, 16)
            sp.dma_start(bk0[:, :], a["bk0"]).then_inc(wA_loaded, 16)
            sp.dma_start(bv0[0:TT, :], a["bv0"].partition_broadcast(TT)).then_inc(wA_loaded, 16)
            sp.dma_start(bo0[0:TT, :], a["bo0"].partition_broadcast(TT)).then_inc(wA_loaded, 16)
            sp.dma_start(router[:, :, :], a["router"]).then_inc(wM_loaded, 16)
            for w, n in ((gate, "gate"), (up, "up"), (down, "down")):
                sp.dma_start(w[:, :, :], a[n]).then_inc(wM_loaded, 16)
            sp.dma_start(fc1[:, :, :, :], a["fc1"]).then_inc(wM_loaded, 16)
            sp.dma_start(fc2[:, :, :, :], a["fc2"]).then_inc(wM_loaded, 16)
            sp.dma_start(wf_raw[:, :], a["wfcT"].rearrange("p k n -> p (k n)")).then_inc(wF_loaded, 16)
            sp.dma_start(wp_raw[:, :], a["wprojT"].rearrange("p k n -> p (k n)")).then_inc(wF_loaded, 16)
            sp.dma_start(ln_w[:, :], a["ln_w"]).then_inc(wF_loaded, 16)
            sp.dma_start(ln_b[:, :], a["ln_b"]).then_inc(wF_loaded, 16)
            sp.wait_ge(consts_m, 8)
            for j in range(NSLOT):
                sp.dma_start(xs_dram[j * SLOT:(j + 1) * SLOT, :], zeros[:, :]).then_inc(zeroed, 16)

            def load(j, p):
                sp.dma_start(xg[:, p, :], xs_dram[bass.ds(j * SLOT, SLOT), :]).then_inc(xg_loaded[p], 16)

            def store(j, p):
                sp.wait_ge(y_ready, j + 1)
                sp.dma_start(ys_dram[bass.ds(j * SLOT, SLOT), :], y_out[:, p, :]).then_inc(y_stored[p], 16)

            sp.wait_ge(scattered, 16 * 2 * NG)
            sp.wait_ge(down_mm, NG)
            for w, n in ((wq1, "wq1"), (wk_up, "wk_up"), (wv_up, "wv_up"), (wo1, "wo1")):
                sp.dma_start(w[0:HD, :, :], a[n]).then_inc(wC_loaded, 16)
            for j in range(2):
                load(j, j)
            with sp.Fori(1, NSLOT // 2) as i:
                for p in range(2):
                    sp.wait_ge(xg_turned, 2 * i + p - 1)
                    load(2 * i + p, p)
                    store(2 * i + p - 2, p)
            for p in range(2):
                store(NSLOT - 2 + p, p)
            sp.wait_ge(fc2_mm, NSLOT)
            for o in range(2):
                sp.dma_start(w_kv[:, :, o * LAT:(o + 1) * LAT], a["wkvdT"]).then_inc(wC_loaded, 16)
            with sp.Fori(0, NGR) as g:
                sp.wait_ge(h_out, 3 * g + 3)
                sp.dma_start(out.rearrange("b (t p) d -> p (b t) d", p=TT)[:, bass.ds(3 * g, 3), :],
                             h[0:TT, bass.ds(3 * g, 3), :]).then_inc(stored, 16)
            sp.wait_ge(stored, 16 * NGR)

        WA = 10 * 16

        @block.gpsimd
        def _(pool):
            pool.memset(ident[:, :], 0.0).then_inc(ident_made, 1)
            pool.memset(mask[:, :], 0.0).then_inc(ident_made, 1)
            pool.wait_ge(ident_made, 2)
            pool.affine_select(out=ident[:, :], in_=ident[:, :], compare_op=ALU.not_equal, fill=1.0, base=0,
                               pattern=[[-1, 128]], channel_multiplier=1).then_inc(ident_made, 1)
            pool.affine_select(out=mask[:, :], in_=mask[:, :], compare_op=ALU.is_ge, fill=MASKED, base=0,
                               pattern=[[-1, TT]], channel_multiplier=1).then_inc(ident_made, 1)
            pool.memset(zeros[:, :], 0.0).then_inc(consts_m, 1)
            pool.memset(ones[:, :], 1.0).then_inc(consts_m, 1)
            pool.memset(restart[:, :, :], 1.0).then_inc(consts_m, 1)
            pool.iota(iota_e[:, :], pattern=[[1, E]], base=0, channel_multiplier=0,
                      allow_small_or_imprecise_dtypes=True).then_inc(consts_m, 1)
            pool.iota(iota_j[:, :], pattern=[[1, NSLOT]], base=0, channel_multiplier=0,
                      allow_small_or_imprecise_dtypes=True).then_inc(consts_m, 1)
            pool.iota(iota_c[:, :], pattern=[[SLOT, NG]], base=0, channel_multiplier=0,
                      allow_small_or_imprecise_dtypes=True).then_inc(consts_m, 1)
            pool.wait_ge(consts_m, 6)
            pool.memset(restart[:, :, 0:1], 0.0).then_inc(consts_m, 1)
            pool.affine_select(out=before[:, :], in_=ones[:, 0:TT], compare_op=ALU.is_gt, fill=0.0, base=0,
                               pattern=[[1, TT]], channel_multiplier=-1).then_inc(consts_m, 1)
            pool.wait_ge(wA_loaded, WA)
            with pool.Fori(0, B) as b:
                for t in range(NT):
                    pool.wait_ge(xn_ready, NT * b + t + 1)
                    pool.tensor_tensor(h[0:TT, b * NT + t, :], h[0:TT, b * NT + t, :], bo0[0:TT, :], ALU.add)\
                        .then_inc(h_biased, 1)

            with pool.Fori(0, B) as b:
                for t in range(NT):
                    wait_apart(pool, "pool", xn_ready, NT * b + NG + t + 1, B)
                    pool.tensor_copy(x_all[0:TT, b * NT + t, :], xn[0:TT, t, :]).then_inc(x_kept, 1)
            pool.wait_ge(rows_ready, 2)
            pool.wait_ge(x_kept, NG)
            pool.wait_ge(zeroed, 16 * NSLOT)
            for t in range(NG):
                for c in range(2):
                    pool.indirect_dma_start(
                        out=xs_dram[:, :], out_offset=bass.IndirectOffsetOnAxis(ap=row[0:TT, c, t:t + 1], axis=0),
                        in_=x_all[0:TT, t, :], in_offset=None).then_inc(scattered, 16)
            for p in range(2):
                pool.wait_ge(y_stored[p], 16 * (NSLOT // 2))
            for t in range(NG):
                if t >= RING:
                    pool.wait_ge(h_moe, 2 * (t - RING + 1))
                for c in range(2):
                    pool.indirect_dma_start(
                        out=ring[0:TT, t % RING, c, :], out_offset=None, in_=ys_dram[:, :],
                        in_offset=bass.IndirectOffsetOnAxis(ap=row[0:TT, c, t:t + 1], axis=0))\
                        .then_inc(gathered[t % RING], 16)
            pool.wait_ge(w_folded, 4)
            pool.tensor_copy(w_qp[:, :, :], w_qk[:, 0, :, :]).then_inc(w_picked, 1)
            with pool.Fori(0, B) as b:
                for n in range(PAIRS):
                    wait_apart(pool, "pool", q_mm, 2 * (PAIRS * b + n + 1), B)
                    pool.tensor_copy(w_qp[:, :, :], w_qk[:, (n + 1) % PAIRS, :, :]).then_inc(w_picked, 1)
            pool.wait_ge(b_out_ready, 1)
            with pool.Fori(0, NG) as t:
                pool.wait_ge(fx_ready, t + 1)
                pool.tensor_tensor(h[0:TT, t, :], h[0:TT, t, :], b_out[0:TT, :], ALU.add).then_inc(h_biased2, 1)
            pool.wait_ge(passed["pool"], passes["pool"])

        @block.vector
        def _(dve):
            dve.memset(decay[:, :], 1.0 - ALPHA).then_inc(const_made, 1)
            dve.wait_ge(wA_loaded, WA)
            dve.tensor_scalar(bq0s[:, :], bq0[:, :], 1.0 / 16, None, ALU.mult).then_inc(const_made, 1)
            dve.wait_ge(const_made, 2)
            dve.wait_ge(x_loaded, 16)
            dve.wait_ge(ident_made, 4)
            with dve.Fori(0, B) as b:
                ew = 6 * b
                dve.tensor_scalar(x_scaled[:, :], x_in[:, b, :], ALPHA / 2, None, ALU.mult).then_inc(ew_step, 1)
                dve.tensor_scalar(fwd[:, 0:1], x_in[:, b, 0:1], 0.5, None, ALU.mult).then_inc(ew_step, 1)
                dve.tensor_scalar(bwd[:, T - 1:T], x_in[:, b, T - 1:T], 0.5, None, ALU.mult).then_inc(ew_step, 1)
                dve.wait_ge(ew_step, ew + 3)
                dve.tensor_tensor_scan(fwd[:, 1:T], decay[:, 0:1].to_broadcast([128, T - 1]), x_scaled[:, 1:T],
                                       fwd[:, 0:1], ALU.mult, ALU.add).then_inc(ew_step, 1)
                dve.tensor_tensor_scan(bwd[:, T - 2::-1], decay[:, 0:1].to_broadcast([128, T - 1]),
                                       x_scaled[:, T - 2::-1], bwd[:, T - 1:T], ALU.mult, ALU.add).then_inc(ew_step, 1)
                dve.wait_ge(ew_step, ew + 5)
                dve.tensor_tensor(ewma[:, :], fwd[:, :], bwd[:, :], ALU.add).then_inc(ew_step, 1)
                for t in range(NT):
                    dve.wait_ge(tok_mm, NT * b + t + 1)
                    dve.tensor_tensor(h[0:TT, b * NT + t, :], bank(t, 0, D, 0, TT), b_tok[0:TT, :], ALU.add)\
                        .then_inc(h_tok, 1)
                wait_apart(dve, "dve", h_tok, NT * b + NT, B)
                layernorm(dve, b * NT, LN_CALL * b, B)
                for t in range(NT):
                    dve.wait_ge(v_mm, NT * b + t + 1)
                    dve.tensor_tensor(v0[0:TT, t, :], bank(t, 0, D, 0, TT), bv0[0:TT, :], ALU.add).then_inc(v_ready, 1)

                def dve_scores(i):
                    n, s = (i + 1) * TT, 2 * (i % 2)
                    diag = bank(s, i * TT, n, 0, TT)
                    dve.wait_ge(s_mm, NT * b + i + 1)
                    dve.tensor_tensor(diag, diag, mask[0:TT, :], ALU.add).then_inc(s_masked, 1)
                    dve.wait_ge(s_masked, NT * b + i + 1)
                    dve.tensor_reduce(negmax[0:TT, i % 2:i % 2 + 1], bank(s, 0, n, 0, TT), AX.X, ALU.max,
                                      negate=True).then_inc(max_ready, 1)

                def dve_pT(i):
                    dve.wait_ge(p_turned, NT * b + i + 1)
                    src = bank(4, 0, (i + 1) * 128, 0, TT).rearrange("p (k q) -> p k q", q=128)[:, :, 0:TT]
                    dve.tensor_copy(pT[0:TT, i % 2, 0:i + 1, :], src).then_inc(pT_ready, 1)
                    dve.reciprocal(rinv[0:TT, i % 2:i % 2 + 1], rowsum[0:TT, i % 2:i % 2 + 1]).then_inc(rinv_ready, 1)

                def dve_h(i):
                    dve.wait_ge(wo_mm, NT * b + i + 1)
                    dve.wait_ge(h_biased, NT * b + i + 1)
                    dve.tensor_tensor(h[0:TT, b * NT + i, :], bank(7, D, 2 * D, 0, TT), h[0:TT, b * NT + i, :],
                                      ALU.add).then_inc(h_attn, 1)

                dve_scores(0)
                for i in range(NT):
                    if i + 1 < NT:
                        dve_scores(i + 1)
                    dve_pT(i)
                    if i >= 1:
                        dve_h(i - 1)
                dve_h(NT - 1)

            dve.wait_ge(consts_m, 8)
            dve.wait_ge(h_attn, NG)
            with dve.Fori(0, B) as b:
                layernorm(dve, b * NT, LN_CALL * (b + B), B)
                dve.wait_ge(router_mm, b + 1)
                dve.tensor_copy(logits[0:TT, :, :], bank(6, 0, NT * E, 0, TT).rearrange("p (t e) -> p t e", e=E))\
                    .then_inc(logits_ready, 1)
                r = R_CALL * b
                wait_apart(dve, "dve", logits_ready, b + 1, B)
                for t in range(NT):
                    dve.max(top[0:TT, t, :], logits[0:TT, t, :]).then_inc(routed, 1)
                wait_apart(dve, "dve", routed, r + NT, B)
                for t in range(NT):
                    dve.max_index(top_i[0:TT, t, :], top[0:TT, t, :], logits[0:TT, t, :]).then_inc(routed, 1)
                dve.tensor_tensor(gap[0:TT, 0, :], top[0:TT, :, 1], top[0:TT, :, 0], ALU.subtract)\
                    .then_inc(gap_ready, 1)
                dve.wait_ge(routed, r + 2 * NT)
                dve.tensor_copy(top_f[0:TT, :, :], top_i[0:TT, :, 0:2]).then_inc(routed, 1)
                dve.wait_ge(routed, r + 2 * NT + 1)
                for c in range(2):
                    dve.tensor_tensor(hot[0:TT, c, bass.ds(b * NT, NT), :],
                                      top_f[0:TT, :, c:c + 1].to_broadcast([TT, NT, E]),
                                      iota_e[0:TT, :].unsqueeze(1).to_broadcast([TT, NT, E]), ALU.is_equal)\
                        .then_inc(routed, 1)
                dve.wait_ge(share_exp, b + 1)
                dve.tensor_scalar(gap[0:TT, 0, :], gap[0:TT, 1, :], 1.0, None, ALU.add).then_inc(routed, 1)
                dve.wait_ge(routed, r + 2 * NT + 4)
                dve.reciprocal(gap[0:TT, 0, :], gap[0:TT, 0, :]).then_inc(routed, 1)
                dve.wait_ge(routed, r + 2 * NT + 5)
                dve.tensor_copy(share[0:TT, 0, bass.ds(b * NT, NT)], gap[0:TT, 0, :]).then_inc(routed, 1)
                dve.tensor_tensor(share[0:TT, 1, bass.ds(b * NT, NT)], gap[0:TT, 0, :], gap[0:TT, 1, :], ALU.mult)\
                    .then_inc(routed, 1)
                dve.wait_ge(routed, r + R_CALL)
                dve.wait_ge(x_kept, NT * b + NT)

            steps = [0]

            def step(ins):
                steps[0] += 1
                ins.then_inc(rows_step, 1)
                dve.wait_ge(rows_step, steps[0])

            dve.tensor_tensor(hots[0:TT, :, :], hot[0:TT, 0, :, :], hot[0:TT, 1, :, :], ALU.add)\
                .then_inc(hots_ready, 1)
            dve.wait_ge(rank_mm, 1)
            step(dve.tensor_copy(tot[0:TT, :, :], bank(7, 0, NG * E, 0, TT).rearrange("p (t e) -> p e t", e=E)))
            flat = lambda v: v[0:TT, :, :].rearrange("p e t -> p (e t)")
            step(dve.tensor_tensor_scan(flat(incl), flat(restart), flat(tot), 0.0, ALU.mult, ALU.add))
            step(dve.tensor_tensor(over[0:TT, :, :], incl[0:TT, :, NG - 1:NG].to_broadcast([TT, E, NG]),
                                   iota_c[0:TT, :].unsqueeze(1).to_broadcast([TT, E, NG]), ALU.is_gt))
            step(dve.tensor_reduce(n_slots[0:TT, :], over[0:TT, :, :], AX.X, ALU.add))
            step(dve.tensor_tensor_scan(slot_end[0:TT, :], ones[0:TT, 0:E], n_slots[0:TT, :], 0.0, ALU.mult, ALU.add))
            step(dve.tensor_tensor(slot_beg[0:TT, :], slot_end[0:TT, :], n_slots[0:TT, :], ALU.subtract))
            step(dve.tensor_tensor(incl[0:TT, :, :], incl[0:TT, :, :], tot[0:TT, :, :], ALU.subtract))
            step(dve.scalar_tensor_tensor(base[0:TT, :, :], slot_beg[0:TT, :].unsqueeze(2).to_broadcast([TT, E, NG]),
                                          float(SLOT), incl[0:TT, :, :], ALU.mult, ALU.add))
            step(dve.tensor_tensor(place[0:TT, :, :], bank(6, 0, NG * E, 0, TT).rearrange("p (t e) -> p t e", e=E),
                                   base[0:TT, :, :].rearrange("p e t -> p t e"), ALU.add))
            for c in range(2):
                step(dve.tensor_tensor(picked[0:TT, c, :, :], hot[0:TT, c, :, :], place[0:TT, :, :], ALU.mult))
                step(dve.tensor_reduce(row_f[0:TT, c, :], picked[0:TT, c, :, :], AX.X, ALU.add))
            dve.tensor_copy(row[0:TT, :, :], row_f[0:TT, :, :]).then_inc(rows_ready, 1)
            step(dve.tensor_tensor(ended[:, :, :], slot_end[0:1, :].unsqueeze(1).to_broadcast([1, NSLOT, E]),
                                   iota_j[0:1, :].unsqueeze(2).to_broadcast([1, NSLOT, E]), ALU.is_le))
            step(dve.tensor_reduce(slot_e_f[:, :], ended[:, :, :], AX.X, ALU.add))
            dve.tensor_scalar(slot_e[:, :], slot_e_f[:, :], float(E - 1), None, ALU.min).then_inc(rows_ready, 1)

            dve.wait_ge(wF_loaded, 4 * 16)
            for c, w in enumerate((wf_raw, wp_raw)):
                dve.tensor_reduce(absum[:, c:c + 1], w[:, :], AX.X, ALU.add, apply_absolute_value=True)\
                    .then_inc(absum_ready, 1)
            dve.wait_ge(gamma_mm, 1)
            half = 0.5 / (FH * D)
            dve.tensor_scalar(above[:, :], bank(7, 0, 2), half, GAMMA_EPS / 2, ALU.mult, ALU.add).then_inc(tern_step, 1)
            dve.wait_ge(tern_step, 1)
            dve.tensor_scalar(below[:, :], above[:, :], -1.0, None, ALU.mult).then_inc(tern_step, 1)
            negs = probs[:, :, :].rearrange("p a t -> p (a t)")[:, 0:FH]
            flat_f = w_f[:, :, :].rearrange("p k n -> p (k n)")
            flat_p = w_p[:, :, :].rearrange("p k n -> p (k n)")
            for n in range(4):
                c, lo = n // 2, n % 2 * FH
                w, q = (wf_raw, flat_f) if c == 0 else (wp_raw, flat_p)
                dve.wait_ge(tern_step, 2 + 2 * n)
                dve.tensor_scalar(negs, w[:, lo:lo + FH], below[:, c:c + 1], -1.0, ALU.is_lt, ALU.mult)\
                    .then_inc(tern_step, 1)
                dve.wait_ge(tern_step, 3 + 2 * n)
                dve.scalar_tensor_tensor(q[:, lo:lo + FH], w[:, lo:lo + FH], above[:, c:c + 1], negs,
                                         ALU.is_gt, ALU.add).then_inc(tern_step, 1)

            MB = ISH // 128
            with dve.Fori(0, B) as b:
                for half in range(2):
                    c = 2 * b + half
                    for m in range(MB):
                        dve.wait_ge(silu_s_ready, MB * c + m + 1)
                        dve.tensor_tensor(act_s[:, m, half * HALF:(half + 1) * HALF], silu_s[:, m % 2, :],
                                          bank(2 * (m % 3) + 1, 0, HALF), ALU.mult).then_inc(act_s_ready, 1)
                    for t in range(3):
                        dve.wait_ge(down_mm, 3 * c + t + 1)
                        hh = h[0:TT, b * NT + half * 3 + t, :]
                        dve.tensor_tensor(hh, bank(6 + (half * 3 + t) % 2, 0, D, 0, TT), hh, ALU.add).then_inc(h_shared, 1)

            def dve_expert(j, p):
                dve.wait_ge(silu_ready, j + 1)
                dve.tensor_tensor(u[:, p, :], silu[:, p, :], bank(2 + p, I, 2 * I), ALU.mult).then_inc(u_ready, 1)

            def dve_uT(j, p):
                dve.wait_ge(u_turned, j + 1)
                dve.tensor_copy(uT[:, p, :, :], bank(4 + p, 0, KD * SLOT).rearrange("p (k q) -> p k q", k=KD))\
                    .then_inc(uT_ready, 1)

            dve_expert(0, 0)
            dve_uT(0, 0)
            dve_expert(1, 1)
            with dve.Fori(1, NSLOT // 2) as i:
                for p in range(2):
                    dve_uT(2 * i + p - 1, 1 - p)
                    dve_expert(2 * i + p, p)
            dve_uT(NSLOT - 1, 1)
            for t in range(NG):
                dve.wait_ge(gathered[t % RING], 32 * (t // RING + 1))
                for c in range(2):
                    dve.scalar_tensor_tensor(h[0:TT, t, :], ring[0:TT, t % RING, c, :], share[0:TT, c, t:t + 1],
                                             h[0:TT, t, :], ALU.mult, ALU.add).then_inc(h_moe, 1)
                    dve.wait_ge(h_moe, 2 * t + c + 1)

            with dve.Fori(0, B) as b:
                layernorm(dve, b * NT, LN_CALL * (b + 2 * B), B)
                dve.wait_ge(kv_hi, 2 * b + 1)
                dve.tensor_tensor(k_lo[:, :], bank(0, 0, T), k_hi[:, :].bitcast(F32), ALU.subtract)\
                    .then_inc(kv_ready, 1)
                dve.wait_ge(kv_hi, 2 * b + 2)
                dve.tensor_tensor(v_st[0:TT, :, LAT:2 * LAT],
                                  bank(2, 0, NT * LAT, 0, TT).rearrange("p (t l) -> p t l", l=LAT),
                                  v_st[0:TT, :, 0:LAT].bitcast(F32), ALU.subtract).then_inc(kv_ready, 1)

                def dve_q(n):
                    for c, (lo, hi) in enumerate(((0, BANK), (BANK, T))):
                        dve.wait_ge(q_hi, 4 * n + 2 * c + 2)
                        dve.tensor_tensor(q_st0[64:128, lo:hi], bank(7, 0, hi - lo, 0, 64),
                                          q_st0[0:64, lo:hi].bitcast(F32), ALU.subtract).then_inc(q_ready, 1)
                        dve.tensor_tensor(q_st1[0:64, lo:hi], bank(7, 0, hi - lo, 64, 128),
                                          q_st1[64:128, lo:hi].bitcast(F32), ALU.subtract).then_inc(q_ready, 1)

                def dve_max(g, s):
                    dve.wait_ge(s1_mm, g + s + 1)
                    dve.tensor_reduce(negmax[0:TT, s % 2:s % 2 + 1], bank(2 * (s % 2), 0, T, 0, TT), AX.X, ALU.max,
                                      negate=True).then_inc(max1_ready, 1)

                def dve_lo(g, s):
                    for c in range(2):
                        dve.wait_ge(p1_hi, 2 * (g + s) + c + 1)
                        src = bank(4 + c, 0, 3 * TT, 0, TT).rearrange("p (k q) -> p k q", q=TT)
                        dve.tensor_tensor(pT_lo[0:TT, s % 2, 3 * c:3 * c + 3, 0:TT], src,
                                          pT_hi[0:TT, s % 2, 3 * c:3 * c + 3, 0:TT].bitcast(F32), ALU.subtract)\
                            .then_inc(p1_ready, 1)
                    dve.reciprocal(rinv1[0:TT, s % 4:s % 4 + 1], rowsum[0:TT, s % 2:s % 2 + 1]).then_inc(rinv1_ready, 1)

                def dve_o(g, s, hp):
                    dve.wait_ge(o_half_ready, g + s + 1)
                    dve.scalar_tensor_tensor(heads_out[0:TT, s % NT, bass.ds((2 * hp + s // NT) * LAT, LAT)],
                                             bank(6, LAT, 2 * LAT, 0, TT), rinv1[0:TT, s % 4:s % 4 + 1],
                                             o_half[0:TT, :], ALU.mult, ALU.add).then_inc(o_ready, 1)

                def dve_pair(hp, last):
                    g = STEPS * PAIRS * b + STEPS * hp
                    for s in range(STEPS):
                        dve_lo(g, s)
                        if s + 2 < STEPS:
                            dve_max(g, s + 2)
                        elif not last:
                            if s == STEPS - 2:
                                dve_q(PAIRS * b + hp + 1)
                            else:
                                dve_max(g, s + 1)
                        if s >= 1:
                            dve_o(g, s - 1, hp)
                    if not last:
                        dve_max(g, STEPS + 1)
                    dve_o(g, STEPS - 1, hp)

                dve_q(PAIRS * b)
                dve_max(STEPS * PAIRS * b, 0)
                dve_max(STEPS * PAIRS * b, 1)
                with dve.Fori(0, PAIRS - 1) as hp:
                    dve_pair(hp, False)
                dve_pair(PAIRS - 1, True)
                for i in range(NT):
                    dve.wait_ge(out1_mm, NT * b + i + 1)
                    hh = h[0:TT, b * NT + i, :]
                    dve.tensor_tensor(hh, bank(6 + i % 2, 0, D, 0, TT), hh, ALU.add).then_inc(h_lat, 1)
                dve.wait_ge(h_lat, NT * b + NT)

            dve.wait_ge(bias_split, 1)
            dve.tensor_tensor(n_lo[:, :, 0:TT], ln_b[:, :].unsqueeze(2).to_broadcast([128, FB, TT]),
                              n_hi[:, :, 0:TT].bitcast(F32), ALU.subtract).then_inc(bias_split, 1)
            dve.wait_ge(bias_mm, 1)
            dve.tensor_copy(b_out[0:TT, :], bank(7, 0, D, 0, TT)).then_inc(b_out_ready, 1)

            def rounds(g):
                return 1 if isinstance(g, int) else NGR // 2 - 1

            def dve_x(g):
                layernorm(dve, 3 * g, LNX_CALL * g, rounds(g), 3, lnx_seq, fx_ready)

            def dve_x_lo(g):
                for k in range(KD):
                    dve.wait_ge(x_hi_ready, KD * g + k + 1)
                    dve.tensor_tensor(x_lo[:, k, :], bank(k, 0, GT), x_hi[:, k, :].bitcast(F32), ALU.subtract)\
                        .then_inc(x_split, 1)

            def dve_bn(g, p, t):
                wait_apart(dve, "dve", gelu_ready, 3 * g + t + 1, rounds(g))
                for c in range(2):
                    dve.bn_stats(bn_f[0:TT, t, c, :], hidden[0:TT, p, t, c * BANK:(c + 1) * BANK]).then_inc(lnf_seq, 1)

            def dve_norm(g):
                at = LNF_CALL * g
                wait_apart(dve, "dve", lnf_seq, at + 6, rounds(g))
                for t in range(3):
                    dve.bn_aggr(mv_f[0:TT, t, :], bn_f[0:TT, t, :, :].rearrange("p c s -> p (c s)")).then_inc(lnf_seq, 1)
                dve.wait_ge(lnf_seq, at + 9)
                rsqrt(dve, mv_f[0:TT, :, 1], yr_f[0:TT, :], ve_f[0:TT, :], yt_f[0:TT, :], lnf_seq, at + 9)
                dve.wait_ge(lnf_seq, at + 9 + LN_CHAIN)
                dve.scalar_tensor_tensor(nm_f[0:TT, :], mv_f[0:TT, :, 0], -1.0, yr_f[0:TT, :], ALU.mult, ALU.mult)\
                    .then_inc(lnf_seq, 1)

            def dve_n_lo(g, f):
                dve.wait_ge(n_hi_ready, FB * g + f + 1)
                dve.scalar_tensor_tensor(n_lo[:, f, :], bank(f % 2, 0, GT), ln_w[:, f:f + 1],
                                         n_hi[:, f, :].bitcast(F32), ALU.mult, ALU.subtract).then_inc(n_split, 1)

            def dve_out(g, t):
                dve.wait_ge(proj_mm, 3 * g + t + 1)
                dve.wait_ge(h_biased2, 3 * g + t + 1)
                hh = h[0:TT, 3 * g + t, :]
                dve.tensor_tensor(hh, bank(6 + t % 2, 0, D, 0, TT), hh, ALU.add).then_inc(h_out, 1)

            def dve_step(g, p, more=True, more2=True):
                if more:
                    dve_x_lo(g + 1)
                for f in range(FB):
                    dve_n_lo(g, f)
                    if more and f in (3, 5, 7):
                        dve_bn(g + 1, 1 - p, (f - 3) // 2)
                if more:
                    dve_norm(g + 1)
                for t in range(3):
                    dve_out(g, t)
                if more2:
                    dve_x(g + 2)

            dve_x(0)
            dve_x_lo(0)
            dve_x(1)
            for t in range(3):
                dve_bn(0, 0, t)
            dve_norm(0)
            with dve.Fori(0, NGR // 2 - 1) as i:
                for p in range(2):
                    dve_step(2 * i + p, p)
            dve_step(NGR - 2, 0, True, False)
            dve_step(NGR - 1, 1, False, False)
            dve.wait_ge(passed["dve"], passes["dve"])

        @block.scalar
        def _(act):
            act.wait_ge(const_made, 2)
            act.wait_ge(wA_loaded, WA)
            with act.Fori(0, B) as b:
                for t in range(NT):
                    act.wait_ge(xn_turned, NT * b + t + 1)
                    act.copy(xT[:, :, t * TT:(t + 1) * TT],
                             bank(t, 0, KD * TT).rearrange("p (k q) -> p k q", k=KD)).then_inc(xT_ready, 1)
                for j in range(8):
                    m, half, isk = j // 2 % 2, j % 2, j // 4
                    dst = (kT if isk else qT)[:, m, half * 375:(half + 1) * 375]
                    act.wait_ge(qk_mm, 8 * b + j + 1)
                    act.activation(dst, bank(j, 0, 375), ACT.Identity,
                                   bias=(bk0 if isk else bq0s)[:, m:m + 1], scale=1.0 if isk else 1.0 / 16)\
                        .then_inc(qk_ready, 1)

                def act_exp(i):
                    n, s = (i + 1) * TT, i % 2
                    act.wait_ge(max_ready, NT * b + i + 1)
                    act.activation(probs[0:TT, s, 0:n], bank(2 * s, 0, n, 0, TT), ACT.Exp,
                                   bias=negmax[0:TT, s:s + 1], scale=1.0, accum_out=rowsum[0:TT, s:s + 1])\
                        .then_inc(probs_ready, 1)

                def act_ctx(i):
                    act.wait_ge(pv_mm, NT * b + i + 1)
                    act.wait_ge(rinv_ready, NT * b + i + 1)
                    act.mul(ctxt[0:TT, :], bank(6, 0, D, 0, TT), rinv[0:TT, i % 2:i % 2 + 1]).then_inc(ctx_ready, 1)

                def act_ctxT(i):
                    act.wait_ge(ctx_turned, NT * b + i + 1)
                    act.copy(ctxT[:, :, :], bank(7, 0, KD * TT).rearrange("p (k q) -> p k q", k=KD))\
                        .then_inc(ctxT_ready, 1)

                act_exp(0)
                for i in range(NT):
                    if i + 1 < NT:
                        act_exp(i + 1)
                    act_ctx(i)
                    act_ctxT(i)

            with act.Fori(0, B) as b:
                for t in range(NT):
                    act.wait_ge(xn_turned, NT * b + NG + t + 1)
                    act.copy(xT_all[:, :, bass.ds(b * T + t * TT, TT)],
                             bank(t, 0, KD * TT).rearrange("p (k q) -> p k q", k=KD)).then_inc(xT_ready, 1)
                    act.copy(xT[:, :, t * TT:(t + 1) * TT],
                             bank(t, 0, KD * TT).rearrange("p (k q) -> p k q", k=KD)).then_inc(xT_ready, 1)
                act.wait_ge(gap_ready, b + 1)
                act.activation(gap[0:TT, 1, :], gap[0:TT, 0, :], ACT.Exp).then_inc(share_exp, 1)
            MB = ISH // 128
            with act.Fori(0, B) as b:
                for half in range(2):
                    for m in range(MB):
                        n = MB * (2 * b + half) + m
                        act.wait_ge(gu_mm, n + 1)
                        if half or m >= 2:
                            act.wait_ge(act_s_ready, n - 1)
                        act.activation(silu_s[:, m % 2, :], bank(2 * (m % 3), 0, HALF), ACT.Silu)\
                            .then_inc(silu_s_ready, 1)

            def act_xgT(j, p):
                act.wait_ge(xg_turned, j + 1)
                act.copy(xgT[:, p, :, :], bank(p, 0, KD * SLOT).rearrange("p (k q) -> p k q", k=KD))\
                    .then_inc(xgT_ready, 1)

            def act_silu(j, p):
                act.wait_ge(fc1_mm, j + 1)
                act.activation(silu[:, p, :], bank(2 + p, 0, I), ACT.Silu).then_inc(silu_ready, 1)

            def act_y(j, p, wait):
                act.wait_ge(fc2_mm, j + 1)
                if wait:
                    act.wait_ge(y_stored[p], 8 * (j - p))
                act.copy(y_out[:, p, :], bank(6 + p, 0, D)).then_inc(y_ready, 1)

            act_xgT(0, 0)
            act_silu(0, 0)
            act_xgT(1, 1)
            act_silu(1, 1)
            act_xgT(2, 0)
            act_y(0, 0, False)
            act_silu(2, 0)
            act_xgT(3, 1)
            act_y(1, 1, False)
            act_silu(3, 1)
            with act.Fori(2, NSLOT // 2) as i:
                for p in range(2):
                    act_xgT(2 * i + p, p)
                    act_y(2 * i + p - 2, p, True)
                    act_silu(2 * i + p, p)
            for p in range(2):
                act_y(NSLOT - 2 + p, p, True)

            act.wait_ge(w_mm, 1)
            for c in range(2):
                act.mul(w_qk[:, 2 * c:2 * c + 2, :, :],
                        bank(c).rearrange("p (n k m) -> p n k m", n=2, k=KD), HD ** -0.5).then_inc(w_folded, 1)
            for c in range(2):
                act.copy(w_vo[:, 2 * c:2 * c + 2, :], bank(2 + c).rearrange("p (n m) -> p n m", n=2))\
                    .then_inc(w_folded, 1)
            with act.Fori(0, B) as b:
                for t in range(NT):
                    act.wait_ge(xn_turned, NT * b + 2 * NG + t + 1)
                    act.copy(xT[:, :, t * TT:(t + 1) * TT],
                             bank(t, 0, KD * TT).rearrange("p (k q) -> p k q", k=KD)).then_inc(xT_ready, 1)
                act.wait_ge(kv_mm, 2 * b + 1)
                act.copy(k_hi[:, :], bank(0, 0, T)).then_inc(kv_hi, 1)
                act.wait_ge(kv_mm, 2 * b + 2)
                act.copy(v_st[0:TT, :, 0:LAT], bank(2, 0, NT * LAT, 0, TT).rearrange("p (t l) -> p t l", l=LAT))\
                    .then_inc(kv_hi, 1)

                def act_q(n):
                    for c, (lo, hi) in enumerate(((0, BANK), (BANK, T))):
                        act.wait_ge(q_mm, 2 * n + c + 1)
                        act.copy(q_st0[0:64, lo:hi], bank(7, 0, hi - lo, 0, 64)).then_inc(q_hi, 1)
                        act.copy(q_st1[64:128, lo:hi], bank(7, 0, hi - lo, 64, 128)).then_inc(q_hi, 1)

                def act_exp1(g, s):
                    act.wait_ge(max1_ready, g + s + 1)
                    act.activation(probs[0:TT, s % 2, :], bank(2 * (s % 2), 0, T, 0, TT), ACT.Exp,
                                   bias=negmax[0:TT, s % 2:s % 2 + 1], scale=1.0,
                                   accum_out=rowsum[0:TT, s % 2:s % 2 + 1]).then_inc(probs1_ready, 1)

                def act_hi(g, s):
                    for c in range(2):
                        act.wait_ge(p1_turned, 2 * (g + s) + c + 1)
                        src = bank(4 + c, 0, 3 * TT, 0, TT).rearrange("p (k q) -> p k q", q=TT)
                        act.copy(pT_hi[0:TT, s % 2, 3 * c:3 * c + 3, 0:TT], src).then_inc(p1_hi, 1)

                def act_o(g, s):
                    act.wait_ge(pv1_mm, g + s + 1)
                    act.wait_ge(rinv1_ready, g + s + 1)
                    act.mul(o_half[0:TT, :], bank(6, 0, LAT, 0, TT), rinv1[0:TT, s % 4:s % 4 + 1])\
                        .then_inc(o_half_ready, 1)

                def act_pair(hp, last):
                    g = STEPS * PAIRS * b + STEPS * hp
                    for s in range(STEPS):
                        if s + 1 < STEPS:
                            act_exp1(g, s + 1)
                        act_hi(g, s)
                        if s == STEPS - 2 and not last:
                            act_q(PAIRS * b + hp + 1)
                        if s >= 1:
                            act_o(g, s - 1)
                    if not last:
                        act_exp1(g, STEPS)
                    act_o(g, STEPS - 1)

                act_q(PAIRS * b)
                act_exp1(STEPS * PAIRS * b, 0)
                with act.Fori(0, PAIRS - 1) as hp:
                    act_pair(hp, False)
                act_pair(PAIRS - 1, True)
                for i in range(NT):
                    act.wait_ge(o_turned, NT * b + i + 1)
                    act.copy(oT[:, i % 2, :, :], bank(4 + i % 2, 0, 4 * TT).rearrange("p (c q) -> p c q", c=4))\
                        .then_inc(oT_ready, 1)

            act.wait_ge(h_lat, NG)
            act.wait_ge(w_picked, PAIRS * B + 1)
            act.copy(n_hi[:, :, 0:TT], ln_b[:, :].unsqueeze(2).to_broadcast([128, FB, TT])).then_inc(bias_split, 1)

            def act_x_hi(g):
                for k in range(KD):
                    act.wait_ge(fx_turned, KD * g + k + 1)
                    act.copy(x_hi[:, k, :], bank(k, 0, GT)).then_inc(x_hi_ready, 1)

            def act_gelu(g, p, t):
                s = 2 + 2 * ((3 * p + t) % 2)
                act.wait_ge(fc_mm, 3 * g + t + 1)
                act.activation(hidden[0:TT, p, t, :], bank(s, 0, FH, 0, TT), ACT.Gelu).then_inc(gelu_ready, 1)

            def act_norm(g, p):
                act.wait_ge(lnf_seq, LNF_CALL * (g + 1))
                for t in range(3):
                    act.activation(hidden[0:TT, p, t, :], hidden[0:TT, p, t, :], ACT.Identity,
                                   bias=nm_f[0:TT, t:t + 1], scale=yr_f[0:TT, t:t + 1]).then_inc(norm_ready, 1)

            def act_n_hi(g, f):
                act.wait_ge(n_turned, FB * g + f + 1)
                act.mul(n_hi[:, f, :], bank(f % 2, 0, GT), ln_w[:, f:f + 1]).then_inc(n_hi_ready, 1)

            def act_step(g, p, more=True):
                if more:
                    act_x_hi(g + 1)
                for f in range(FB):
                    act_n_hi(g, f)
                    if more and f in (3, 5, 7):
                        act_gelu(g + 1, 1 - p, (f - 3) // 2)
                if more:
                    act_norm(g + 1, 1 - p)

            act_x_hi(0)
            for t in range(3):
                act_gelu(0, 0, t)
            act_norm(0, 0)
            with act.Fori(0, NGR // 2 - 1) as i:
                for p in range(2):
                    act_step(2 * i + p, p)
            act_step(NGR - 2, 0)
            act_step(NGR - 1, 1, False)

        @block.tensor
        def _(pe):
            pe.wait_ge(wA_loaded, WA)
            pe.wait_ge(ident_made, 4)
            with pe.Fori(0, B) as b:
                pe.wait_ge(ew_step, 6 * b + 6)
                for t in range(NT):
                    pe.matmul(bank(t, 0, D, 0, TT), ewma[:, t * TT:(t + 1) * TT], w_tok[:, :],
                              start=True, stop=True).then_inc(tok_mm, 1)
                for t in range(NT):
                    pe.wait_ge(xn_ready, NT * b + t + 1)
                    for k in range(KD):
                        mm = pe.transpose(bank(t, k * TT, (k + 1) * TT), xn[0:TT, t, k * 128:(k + 1) * 128], ident[0:TT, 0:TT])
                    mm.then_inc(xn_turned, 1)
                pe.wait_ge(xT_ready, NT * b + NT)
                for j in range(8):
                    m, half, w = j // 2 % 2, j % 2, (wk0 if j // 4 else wq0)
                    for k in range(KD):
                        mm = pe.matmul(bank(j, 0, 375), w[:, k, m * 128:(m + 1) * 128],
                                       xT[:, k, half * 375:(half + 1) * 375], start=k == 0, stop=k == KD - 1)
                    mm.then_inc(qk_mm, 1)
                for t in range(NT):
                    pe.wait_ge(qk_ready, 8 * b + t + 1)
                    for k in range(KD):
                        mm = pe.matmul(bank(t, 0, D, 0, TT), xT[:, k, t * TT:(t + 1) * TT], wv0[:, k, :],
                                       start=k == 0, stop=k == KD - 1)
                    mm.then_inc(v_mm, 1)
                pe.wait_ge(qk_ready, 8 * b + 8)
                pe.wait_ge(v_ready, NT * b + NT)

                def scores(i):
                    n, s = (i + 1) * TT, 2 * (i % 2)
                    if i >= 2:
                        pe.wait_ge(probs_ready, NT * b + i - 1)
                    for lo in range(0, n, BANK):
                        hi = min(n, lo + BANK)
                        for k in range(KD):
                            mm = pe.matmul(bank(s, lo, hi, 0, TT), qT[:, k, i * TT:(i + 1) * TT], kT[:, k, lo:hi],
                                           start=k == 0, stop=k == KD - 1)
                    mm.then_inc(s_mm, 1)

                def turn_probs(i):
                    pe.wait_ge(probs_ready, NT * b + i + 1)
                    if i >= 1:
                        pe.wait_ge(pT_ready, NT * b + i)
                    for k in range(i + 1):
                        mm = pe.transpose(bank(4, k * 128, k * 128 + TT, 0, TT),
                                          probs[0:TT, i % 2, k * TT:(k + 1) * TT], ident[0:TT, 0:TT])
                    mm.then_inc(p_turned, 1)

                def weigh_values(i):
                    pe.wait_ge(pT_ready, NT * b + i + 1)
                    for k in range(i + 1):
                        mm = pe.matmul(bank(6, 0, D, 0, TT), pT[0:TT, i % 2, k, :], v0[0:TT, k, :],
                                       start=k == 0, stop=k == i)
                    mm.then_inc(pv_mm, 1)

                def turn_ctx(i):
                    pe.wait_ge(ctx_ready, NT * b + i + 1)
                    if i >= 1:
                        pe.wait_ge(h_attn, NT * b + i)
                    for k in range(KD):
                        mm = pe.transpose(bank(7, k * TT, (k + 1) * TT), ctxt[0:TT, k * 128:(k + 1) * 128],
                                          ident[0:TT, 0:TT])
                    mm.then_inc(ctx_turned, 1)

                def project(i):
                    pe.wait_ge(ctxT_ready, NT * b + i + 1)
                    for k in range(KD):
                        mm = pe.matmul(bank(7, D, 2 * D, 0, TT), ctxT[:, k, :], wo0[:, k, :],
                                       start=k == 0, stop=k == KD - 1)
                    mm.then_inc(wo_mm, 1)

                scores(0)
                for i in range(NT):
                    if i + 1 < NT:
                        scores(i + 1)
                    turn_probs(i)
                    if i >= 1:
                        turn_ctx(i - 1)
                    weigh_values(i)
                    if i >= 1:
                        project(i - 1)
                turn_ctx(NT - 1)
                project(NT - 1)

            pe.wait_ge(wM_loaded, 6 * 16)
            pe.wait_ge(h_attn, NG)
            with pe.Fori(0, B) as b:
                for t in range(NT):
                    pe.wait_ge(xn_ready, NT * b + NG + t + 1)
                    for k in range(KD):
                        mm = pe.transpose(bank(t, k * TT, (k + 1) * TT), xn[0:TT, t, k * 128:(k + 1) * 128],
                                          ident[0:TT, 0:TT])
                    mm.then_inc(xn_turned, 1)
                pe.wait_ge(xT_ready, 2 * NT * b + NG + 2 * NT)
                for t in range(NT):
                    for k in range(KD):
                        mm = pe.matmul(bank(6, t * E, (t + 1) * E, 0, TT), xT[:, k, t * TT:(t + 1) * TT],
                                       router[:, k, :], start=k == 0, stop=k == KD - 1)
                mm.then_inc(router_mm, 1)

            pe.wait_ge(hots_ready, 1)
            pe.wait_ge(consts_m, 8)
            flat = hots[0:TT, :, :].rearrange("p t e -> p (t e)")
            pe.matmul(bank(6, 0, NG * E, 0, TT), before[0:TT, :], flat, start=True, stop=True)
            pe.matmul(bank(7, 0, NG * E, 0, TT), ones[0:TT, 0:TT], flat, start=True, stop=True).then_inc(rank_mm, 1)

            pe.wait_ge(absum_ready, 2)
            pe.wait_ge(rows_ready, 1)
            pe.matmul(bank(7, 0, 2), ones[:, :], absum[:, :], start=True, stop=True).then_inc(gamma_mm, 1)

            MB = ISH // 128
            pe.wait_ge(tern_step, 1)
            with pe.Fori(0, B) as b:
                for half in range(2):
                    c = 2 * b + half
                    for m in range(MB):
                        n = MB * c + m
                        if half or m >= 3:
                            pe.wait_ge(act_s_ready, n - 2)
                        for w, o in ((gate, 0), (up, 1)):
                            for k in range(KD):
                                mm = pe.matmul(bank(2 * (m % 3) + o, 0, HALF), w[:, k, m * 128:(m + 1) * 128],
                                               xT_all[:, k, bass.ds(b * T + half * HALF, HALF)],
                                               start=k == 0, stop=k == KD - 1)
                        mm.then_inc(gu_mm, 1)
                    pe.wait_ge(act_s_ready, MB * c + MB)
                    for t in range(3):
                        if half or t == 2:
                            pe.wait_ge(h_shared, 3 * c + t - 1)
                        for m in range(MB):
                            mm = pe.matmul(bank(6 + (half * 3 + t) % 2, 0, D, 0, TT),
                                           act_s[:, m, half * HALF + t * TT:half * HALF + (t + 1) * TT], down[:, m, :],
                                           start=m == 0, stop=m == MB - 1)
                        mm.then_inc(down_mm, 1)
                pe.wait_ge(h_shared, 6 * b + 6)

            def turn_x(j, p):
                pe.wait_ge(xg_loaded[p], 8 * (j - p) + 16)
                for k in range(KD):
                    mm = pe.transpose(bank(p, k * SLOT, (k + 1) * SLOT), xg[:, p, k * 128:(k + 1) * 128], ident[:, :])
                mm.then_inc(xg_turned, 1)

            def turn_u(j, p):
                pe.wait_ge(u_ready, j + 1)
                for k in range(KD):
                    mm = pe.transpose(bank(4 + p, k * SLOT, (k + 1) * SLOT), u[:, p, k * 128:(k + 1) * 128], ident[:, :])
                mm.then_inc(u_turned, 1)

            def first(j, p, e):
                pe.wait_ge(xgT_ready, j + 1)
                for k in range(KD):
                    mm = pe.matmul(bank(2 + p, 0, 2 * I), xgT[:, p, k, :], fc1[:, e, k, :],
                                   start=k == 0, stop=k == KD - 1)
                mm.then_inc(fc1_mm, 1)

            def second(j, p, e, wait=True):
                pe.wait_ge(uT_ready, j + 1)
                if wait:
                    pe.wait_ge(y_ready, j - 1)
                for k in range(KD):
                    mm = pe.matmul(bank(6 + p, 0, D), uT[:, p, k, :], fc2[:, e, k, :],
                                   start=k == 0, stop=k == KD - 1)
                mm.then_inc(fc2_mm, 1)

            def expert_of(j):
                return pe.value_load(slot_e[0:1, bass.ds(j, 1)], min_val=0, max_val=E - 1)

            pe.wait_ge(rows_ready, 2)
            turn_x(0, 0)
            first(0, 0, expert_of(0))
            turn_x(1, 1)
            turn_u(0, 0)
            first(1, 1, expert_of(1))
            turn_x(2, 0)
            second(0, 0, expert_of(0), False)
            turn_u(1, 1)
            first(2, 0, expert_of(2))
            turn_x(3, 1)
            second(1, 1, expert_of(1), False)
            turn_u(2, 0)
            first(3, 1, expert_of(3))
            with pe.Fori(2, NSLOT // 2) as i:
                for p in range(2):
                    j = 2 * i + p
                    turn_x(j, p)
                    second(j - 2, p, expert_of(j - 2))
                    turn_u(j - 1, 1 - p)
                    first(j, p, expert_of(j))
            second(NSLOT - 2, 0, expert_of(NSLOT - 2))
            turn_u(NSLOT - 1, 1)
            second(NSLOT - 1, 1, expert_of(NSLOT - 1))

            pe.wait_ge(wC_loaded, 6 * 16)
            pe.wait_ge(y_ready, NSLOT)
            for n in range(LH):
                for k in range(KD):
                    col = (n // 2 * KD + k) * 128 + n % 2 * LAT
                    pe.matmul(bank(0, col, col + LAT), wq1[0:HD, n, k * 128:(k + 1) * 128], wk_up[0:HD, n, :],
                              start=True, stop=True)
                p0, col = n % 2 * LAT, n // 2 * D
                mm = pe.matmul(bank(2, col, col + D, p0, p0 + LAT), wv_up[0:HD, n, :], wo1[0:HD, n, :],
                               start=True, stop=True)
            mm.then_inc(w_mm, 1)
            pe.wait_ge(w_folded, 4)
            with pe.Fori(0, B) as b:
                for t in range(NT):
                    pe.wait_ge(xn_ready, NT * b + 2 * NG + t + 1)
                    for k in range(KD):
                        mm = pe.transpose(bank(t, k * TT, (k + 1) * TT), xn[0:TT, t, k * 128:(k + 1) * 128],
                                          ident[0:TT, 0:TT])
                    mm.then_inc(xn_turned, 1)
                pe.wait_ge(xT_ready, NT * b + 3 * NG + NT)
                for lo, hi in ((0, BANK), (BANK, T)):
                    for k in range(KD):
                        mm = pe.matmul(bank(0, lo, hi), w_kv[:, k, :], xT[:, k, lo:hi], start=k == 0, stop=k == KD - 1)
                mm.then_inc(kv_mm, 1)
                for t in range(NT):
                    for k in range(KD):
                        mm = pe.matmul(bank(2, t * LAT, (t + 1) * LAT, 0, TT), xT[:, k, t * TT:(t + 1) * TT],
                                       w_kv[:, k, 0:LAT], start=k == 0, stop=k == KD - 1)
                mm.then_inc(kv_mm, 1)

                def queries(n, first=False):
                    pe.wait_ge(w_picked, n + 1)
                    for c, (lo, hi) in enumerate(((0, BANK), (BANK, T))):
                        if c:
                            pe.wait_ge(q_ready, 4 * n + 2)
                        for k in range(KD):
                            mm = pe.matmul(bank(7, 0, hi - lo), w_qp[:, k, :], xT[:, k, lo:hi],
                                           start=k == 0, stop=k == KD - 1)
                        mm.then_inc(q_mm, 1)

                def scores1(g, s, j):
                    q = q_st0 if j < NT else q_st1
                    t = j % NT
                    if s >= 2:
                        pe.wait_ge(probs1_ready, g + s - 1)
                    for lo, hi in ((0, BANK), (BANK, T)):
                        pe.matmul(bank(2 * (s % 2), lo, hi, 0, TT), q[:, t * TT:(t + 1) * TT], k_hi[:, lo:hi],
                                  start=True, stop=False)
                        mm = pe.matmul(bank(2 * (s % 2), lo, hi, 0, TT), q[:, t * TT:(t + 1) * TT], k_lo[:, lo:hi],
                                       start=False, stop=True)
                    mm.then_inc(s1_mm, 1)

                def turn_probs1(g, s):
                    pe.wait_ge(probs1_ready, g + s + 1)
                    for c in range(2):
                        if s >= 1:
                            pe.wait_ge(p1_ready, 2 * (g + s) - 1 + c)
                        for k in range(3):
                            mm = pe.transpose(bank(4 + c, k * TT, (k + 1) * TT, 0, TT),
                                              probs[0:TT, s % 2, (3 * c + k) * TT:(3 * c + k + 1) * TT],
                                              ident[0:TT, 0:TT])
                        mm.then_inc(p1_turned, 1)

                def weigh1(g, s):
                    pe.wait_ge(p1_ready, 2 * (g + s) + 2)
                    if s >= 1:
                        pe.wait_ge(o_ready, g + s)
                    for k in range(NT):
                        for half, pt in enumerate((pT_hi, pT_lo)):
                            mm = pe.matmul(bank(6, 0, 2 * LAT, 0, TT), pt[0:TT, s % 2, k, 0:TT], v_st[0:TT, k, :],
                                           start=k == 0 and half == 0, stop=k == NT - 1 and half == 1)
                    mm.then_inc(pv1_mm, 1)

                def pair(hp, last):
                    g = STEPS * PAIRS * b + STEPS * hp
                    for s in range(STEPS):
                        turn_probs1(g, s)
                        if s + 2 < STEPS:
                            scores1(g, s + 2, s + 2)
                        elif not last:
                            if s == STEPS - 2:
                                queries(PAIRS * b + hp + 1)
                            else:
                                pe.wait_ge(q_ready, 4 * (PAIRS * b + hp + 2))
                                scores1(g, STEPS, 0)
                        if s >= 1:
                            weigh1(g, s - 1)
                    if not last:
                        scores1(g, STEPS + 1, 1)
                    weigh1(g, STEPS - 1)

                queries(PAIRS * b)
                pe.wait_ge(kv_ready, 2 * b + 2)
                pe.wait_ge(q_ready, 4 * (PAIRS * b + 1))
                scores1(STEPS * PAIRS * b, 0, 0)
                scores1(STEPS * PAIRS * b, 1, 1)
                with pe.Fori(0, PAIRS - 1) as hp:
                    pair(hp, False)
                pair(PAIRS - 1, True)

                pe.wait_ge(o_ready, STEPS * PAIRS * (b + 1))
                for i in range(NT):
                    if i >= 2:
                        pe.wait_ge(oT_ready, NT * b + i - 1)
                    for c in range(LH * LAT // 128):
                        mm = pe.transpose(bank(4 + i % 2, c * TT, (c + 1) * TT),
                                          heads_out[0:TT, i, c * 128:(c + 1) * 128], ident[0:TT, 0:TT])
                    mm.then_inc(o_turned, 1)
                    pe.wait_ge(oT_ready, NT * b + i + 1)
                    if i >= 2:
                        pe.wait_ge(h_lat, NT * b + i - 1)
                    for c in range(LH * LAT // 128):
                        mm = pe.matmul(bank(6 + i % 2, 0, D, 0, TT), oT[:, i % 2, c, :], w_vo[:, c, :],
                                       start=c == 0, stop=c == LH * LAT // 128 - 1)
                    mm.then_inc(out1_mm, 1)
                pe.wait_ge(h_lat, NT * b + NT)

            pe.wait_ge(bias_split, 2)
            for f in range(FB):
                for half, nt in enumerate((n_hi, n_lo)):
                    mm = pe.matmul(bank(7, 0, D, 0, TT), nt[:, f, 0:TT], w_p[:, f, :],
                                   start=f == 0 and half == 0, stop=f == FB - 1 and half == 1)
            mm.then_inc(bias_mm, 1)

            def turn_x3(g):
                pe.wait_ge(fx_ready, 3 * g + 3)
                for k in range(KD):
                    for t in range(3):
                        mm = pe.transpose(bank(k, t * TT, (t + 1) * TT), xn[0:TT, t, k * 128:(k + 1) * 128],
                                          ident[0:TT, 0:TT])
                    mm.then_inc(fx_turned, 1)

            def fc(g, p, t, half, wait=True):
                s = 2 + 2 * ((3 * p + t) % 2) + half
                if half == 0:
                    pe.wait_ge(x_split, KD * g + KD)
                    if wait:
                        pe.wait_ge(gelu_ready, 3 * g + t - 1)
                for k in range(KD):
                    for part, xt in enumerate((x_hi, x_lo)):
                        mm = pe.matmul(bank(s, 0, BANK, 0, TT), xt[:, k, t * TT:(t + 1) * TT],
                                       w_f[:, k, half * BANK:(half + 1) * BANK],
                                       start=k == 0 and part == 0, stop=k == KD - 1 and part == 1)
                if half:
                    mm.then_inc(fc_mm, 1)

            def turn_n(g, p, f):
                if f == 0:
                    pe.wait_ge(norm_ready, 3 * g + 3)
                if f >= 2:
                    pe.wait_ge(n_split, FB * g + f - 1)
                for t in range(3):
                    mm = pe.transpose(bank(f % 2, t * TT, (t + 1) * TT), hidden[0:TT, p, t, f * 128:(f + 1) * 128],
                                      ident[0:TT, 0:TT])
                mm.then_inc(n_turned, 1)

            def proj(g, t, first=False):
                pe.wait_ge(n_split, FB * g + FB)
                if not first or t == 2:
                    pe.wait_ge(h_out, 3 * g + t - 1)
                for f in range(FB):
                    for half, nt in enumerate((n_hi, n_lo)):
                        mm = pe.matmul(bank(6 + t % 2, 0, D, 0, TT), nt[:, f, t * TT:(t + 1) * TT], w_p[:, f, :],
                                       start=f == 0 and half == 0, stop=f == FB - 1 and half == 1)
                mm.then_inc(proj_mm, 1)

            def step3(g, p, more=True, first=False):
                if more:
                    turn_x3(g + 1)
                    pe.wait_ge(x_split, KD * g + 2 * KD)
                for f in range(FB):
                    turn_n(g, p, f)
                    if more and f in (2, 4, 6):
                        fc(g + 1, 1 - p, (f - 2) // 2, 0)
                    if more and f in (3, 5, 7):
                        fc(g + 1, 1 - p, (f - 3) // 2, 1)
                for t in range(3):
                    proj(g, t, first)

            turn_x3(0)
            pe.wait_ge(b_out_ready, 1)
            for t in range(3):
                for half in range(2):
                    fc(0, 0, t, half, t == 2)
            step3(0, 0, True, True)
            step3(1, 1)
            with pe.Fori(1, NGR // 2 - 1) as i:
                for p in range(2):
                    step3(2 * i + p, p)
            step3(NGR - 2, 0)
            step3(NGR - 1, 1, False)


def layout(x, L0_tok_W, L0_tok_b, L0_attn_Wq, L0_attn_bq, L0_attn_Wk, L0_attn_bk, L0_attn_Wv, L0_attn_bv, L0_attn_Wo,
           L0_attn_bo, L0_ffn_w_router, L0_ffn_fc1_w, L0_ffn_fc2_w, L0_ffn_gate_w, L0_ffn_up_w, L0_ffn_down_w,
           L1_attn_Wq, L1_attn_Wkv_down, L1_attn_Wk_up, L1_attn_Wv_up, L1_attn_Wo, L1_ffn_W_fc, L1_ffn_ln_w,
           L1_ffn_ln_b, L1_ffn_W_proj):
    kp = lambda w: np.moveaxis(np.asarray(w).reshape(*w.shape[:-2], -1, 128, w.shape[-1]), -2, 0)
    cols = lambda v: np.asarray(v).reshape(-1, 128).T
    heads = lambda w: np.asarray(w).reshape(LH, HD, -1).transpose(1, 0, 2)
    arrays = dict(
        x=x, tok_wT=np.asarray(L0_tok_W).T, tok_b=L0_tok_b, wq0=kp(L0_attn_Wq), wk0=kp(L0_attn_Wk), wv0=kp(L0_attn_Wv),
        wo0=kp(L0_attn_Wo), bq0=cols(L0_attn_bq), bk0=cols(L0_attn_bk), bv0=L0_attn_bv, bo0=L0_attn_bo,
        router=kp(L0_ffn_w_router), fc1=kp(L0_ffn_fc1_w), fc2=kp(L0_ffn_fc2_w), gate=kp(L0_ffn_gate_w), up=kp(L0_ffn_up_w),
        down=kp(L0_ffn_down_w), wq1=heads(L1_attn_Wq), wkvdT=kp(np.asarray(L1_attn_Wkv_down).T), wk_up=heads(L1_attn_Wk_up),
        wv_up=heads(L1_attn_Wv_up), wo1=heads(np.asarray(L1_attn_Wo).T), wfcT=kp(np.asarray(L1_ffn_W_fc).T),
        ln_w=cols(L1_ffn_ln_w), ln_b=cols(L1_ffn_ln_b), wprojT=kp(np.asarray(L1_ffn_W_proj).T))
    return {n: np.ascontiguousarray(v) for n, v in arrays.items()}


def kernel(**inputs):
    import concourse.bacc as bacc
    from concourse.bass_utils import run_bass_kernel_spmd

    nc = bacc.Bacc("TRN2", target_bir_lowering=False, num_devices=1)
    arrays = layout(**inputs)
    a = {n: nc.dram_tensor(f"in_{n}", v.shape, mybir.dt.from_np(v.dtype), kind="ExternalInput").ap()
         for n, v in arrays.items()}
    out = nc.dram_tensor("out", (B, T, D), F32, kind="ExternalOutput").ap()
    build(nc, a, out)
    r = run_bass_kernel_spmd(nc, [{f"in_{n}": v for n, v in arrays.items()}], core_ids=[0])
    return r.results[0]["out"]
```

```python
from contextlib import ExitStack

import numpy as np
import concourse.bass as bass
from concourse import mybir

F32 = mybir.dt.float32
F32R = mybir.dt.float32r
I32 = mybir.dt.int32
U32 = mybir.dt.uint32
ALU = mybir.AluOpType
ACT = mybir.ActivationFunctionType
AX = mybir.AxisListType

B, C, T, D = 4, 128, 750, 256
TT = 125
NT = T // TT
NG = B * NT
KD = D // 128
E, I, ISH = 8, 256, 512
SLOT = 128
NSLOT = (2 * B * T - E) // SLOT + E
LH, HD, LAT = 8, 64, 64
PAIRS = LH // 2
FH = 1024
FB = FH // 128
BANK = 512
HALF = T // 2
GT = 3 * TT
NGR = NG // 3
GAMMA_EPS = 1e-6
HEAD_STEPS = 2 * NT
STEPS = PAIRS * HEAD_STEPS
ALPHA = 0.1
LN_EPS = 1e-5
MASKED = -1.0e30
RSQRT_SEED = 0x5F3759DF
NEWTON = 3
LN_CHAIN = 3 + 3 * NEWTON


def build(nc, a, out):
    with ExitStack() as ctx:
        def sb(name, shape, dt=F32):
            return ctx.enter_context(nc.sbuf_tensor(name, shape, dt))

        def sem(name):
            return ctx.enter_context(nc.semaphore(name))

        KB = 60 * 1024
        early_at = (nc.sbuf_base + 31) // 32 * 32
        sb("early", [128, KB // 4])
        late_at = (nc.sbuf_base + 31) // 32 * 32
        sb("late", [128, KB // 4])

        def lay(start, *tensors):
            handles = []
            for name, shape, dt in tensors:
                handles.append(nc.alloc_sbuf_tensor_at(name, [128, *shape], dt, offset=start))
                start += (4 * int(np.prod(shape)) + 31) // 32 * 32
            return handles + [start]

        h = sb("h", [128, NG, D])
        ident = sb("ident", [128, 128])
        xn = sb("xn", [128, NT, D])
        xT = sb("xT", [128, KD, T])
        probs = sb("probs", [128, 2, T])
        (w_tok, b_tok, bv0, bo0, wq0, wk0, wv0, wo0, x_in, x_scaled, fwd, bwd, ewma, qT, kT, v0, pT, end) = lay(
            early_at, ("w_tok", [D], F32), ("b_tok", [D], F32), ("bv0", [D], F32), ("bo0", [D], F32),
            ("wq0", [KD, D], F32), ("wk0", [KD, D], F32), ("wv0", [KD, D], F32), ("wo0", [KD, D], F32),
            ("x_in", [B, T], F32), ("x_scaled", [T], F32), ("fwd", [T], F32), ("bwd", [T], F32), ("ewma", [T], F32),
            ("qT", [KD, T], F32), ("kT", [KD, T], F32), ("v0", [NT, D], F32), ("pT", [2, NT, TT], F32))
        assert end <= early_at + KB
        ctxt = sb("ctxt", [128, D])
        ctxT = sb("ctxT", [128, KD, TT])
        decay = sb("decay", [128, 1])
        bq0 = sb("bq0", [128, KD])
        bq0s = sb("bq0s", [128, KD])
        bk0 = sb("bk0", [128, KD])
        mask = sb("mask", [128, TT])
        fc1, fc2, gate, up, down, end = lay(
            late_at, ("fc1", [E, KD, 2 * I], F32), ("fc2", [E, KD, D], F32), ("gate", [KD, ISH], F32),
            ("up", [KD, ISH], F32), ("down", [ISH // 128, D], F32))
        assert end <= late_at + KB
        act_s, x_all, after_rows = lay(early_at, ("act_s", [ISH // 128, 2 * HALF], F32), ("x_all", [NG, D], F32))
        xT_late, end = lay(after_rows, ("xT_late", [KD, B * HALF], F32))
        assert end <= early_at + KB
        xg, xgT, silu, u, uT, y_out, ring_at = lay(
            after_rows, ("xg", [2, D], F32), ("xgT", [2, KD, SLOT], F32), ("silu", [2, I], F32), ("u", [2, I], F32),
            ("uT", [2, KD, SLOT], F32), ("y_out", [2, D], F32))
        ring, end = lay(ring_at, ("ring", [NT, 2, D], F32))
        wq1, wk_up, wv_up, wo1, end = lay(
            early_at + 4 * 2 * HALF * ISH // 128, ("wq1", [LH, D], F32), ("wk_up", [LH, LAT], F32),
            ("wv_up", [LH, 2 * LAT], F32), ("wo1", [LH, D], F32))
        assert end <= after_rows
        o_T, probs1, end = lay(early_at, ("o_T", [2, T], F32), ("probs1", [3, T], F32))
        assert end <= after_rows
        q_st, k_hi, k_lo, v_st, pT1, w_qk, w_vo, w_kv, w_qp, end = lay(
            late_at, ("q_st", [4, T], F32R), ("k_hi", [2, T], F32R), ("k_lo", [2, T], F32R),
            ("v_st", [NT, 2 * LAT], F32R), ("pT1", [2, NT, 2, TT], F32R),
            ("w_qk", [PAIRS, KD, 128], F32), ("w_vo", [LH, D], F32), ("w_kv", [KD, 2 * LAT], F32),
            ("w_qp", [KD, 128], F32))
        assert end <= late_at + KB
        wf_at = (nc.sbuf_base + 31) // 32 * 32
        sb("ternary_room", [128, KD * FH + FB * D])
        wf_raw, wp_raw, end = lay(wf_at, ("wf_raw", [KD * FH], F32), ("wp_raw", [FB * D], F32))
        w_f, w_p, end = lay(wf_at, ("w_f", [KD, FH], F32R), ("w_p", [FB, D], F32R))
        x_hi, x_lo, n_hi, n_lo, end = lay(
            late_at, ("x_hi", [KD, GT], F32R), ("x_lo", [KD, GT], F32R), ("n_hi", [FB, GT], F32R),
            ("n_lo", [FB, GT], F32R))
        assert end <= late_at + KB
        hidden, end = lay(early_at, ("hidden", [2, 3, FH], F32))
        ln_w = sb("ln_w", [128, FB])
        ln_b = sb("ln_b", [128, FB])
        b_out = sb("b_out", [128, D])
        absum = sb("absum", [128, 2])
        above = sb("above", [128, 2])
        below = sb("below", [128, 2])
        bn_f = sb("bn_f", [128, 3, 2, 6])
        mv_f = sb("mv_f", [128, 3, 2])
        ve_f = sb("ve_f", [128, 3])
        yr_f = sb("yr_f", [128, 3])
        yt_f = sb("yt_f", [128, 3])
        nm_f = sb("nm_f", [128, 3])
        silu_s = sb("silu_s", [128, 2, HALF])
        router = sb("router", [128, KD, E])
        logits = sb("logits", [128, NT, E])
        top = sb("top", [128, NT, 8])
        top_i = sb("top_i", [128, NT, 8], U32)
        top_f = sb("top_f", [128, NT, 2])
        gap = sb("gap", [128, 2, NG])
        share = sb("share", [128, 2, NG])
        hot = sb("hot", [128, 2, NG, E])
        hots = sb("hots", [128, NG, E])
        iota_e = sb("iota_e", [128, E])
        iota_j = sb("iota_j", [128, NSLOT])
        iota_c = sb("iota_c", [128, NG])
        before = sb("before", [128, TT])
        ones = sb("ones", [128, 128])
        restart = sb("restart", [128, E, NG])
        tot = sb("tot", [128, E, NG])
        incl = sb("incl", [128, E, NG])
        base = sb("base", [128, E, NG])
        over = sb("over", [128, E, NG])
        n_slots = sb("n_slots", [128, E])
        slot_end = sb("slot_end", [128, E])
        slot_beg = sb("slot_beg", [128, E])
        place = sb("place", [128, NG, E])
        picked = sb("picked", [128, 2, NG, E])
        row_f = sb("row_f", [128, 2, NG])
        row = sb("row", [128, 2, NG], I32)
        ended = sb("ended", [1, NSLOT, E])
        slot_e_f = sb("slot_e_f", [1, NSLOT])
        slot_e = sb("slot_e", [1, NSLOT], I32)
        zeros = sb("zeros", [128, D])
        bn6 = sb("bn6", [128, NT, 6])
        mv = sb("mv", [128, NT, 2])
        ve = sb("ve", [128, NT])
        yr = sb("yr", [128, NT])
        yt = sb("yt", [128, NT])
        negmax = sb("negmax", [128, 2])
        rowsum = sb("rowsum", [128, 2])
        rinv = sb("rinv", [128, 2])
        rinv1 = sb("rinv1", [128, 2])

        xs_dram = nc.dram_tensor("xs_dram", [NSLOT * SLOT, D], F32, kind="Internal").ap()
        ys_dram = nc.dram_tensor("ys_dram", [NSLOT * SLOT, D], F32, kind="Internal").ap()

        PS = ctx.enter_context(nc.psum_tensor("PS", [128, 8 * BANK], F32))

        def bank(i, lo=0, hi=BANK, p0=0, p1=128):
            return PS[p0:p1, i * BANK + lo:i * BANK + hi]

        x_loaded, wA_loaded = sem("x_loaded"), sem("wA_loaded")
        const_made, ident_made = sem("const_made"), sem("ident_made")
        ew_step, tok_mm, h_tok = sem("ew_step"), sem("tok_mm"), sem("h_tok")
        ln_seq, xn_ready, xn_turned, xT_ready = sem("ln_seq"), sem("xn_ready"), sem("xn_turned"), sem("xT_ready")
        qk_mm, qk_ready, v_mm, v_ready = sem("qk_mm"), sem("qk_ready"), sem("v_mm"), sem("v_ready")
        s_mm, s_masked, max_ready, probs_ready = sem("s_mm"), sem("s_masked"), sem("max_ready"), sem("probs_ready")
        p_turned, pT_ready, pv_mm, rinv_ready = sem("p_turned"), sem("pT_ready"), sem("pv_mm"), sem("rinv_ready")
        ctx_ready, ctx_turned, ctxT_ready, wo_mm = sem("ctx_ready"), sem("ctx_turned"), sem("ctxT_ready"), sem("wo_mm")
        h_biased, h_attn = sem("h_biased"), sem("h_attn")
        stored = sem("stored")
        wM_loaded, zeroed = sem("wM_loaded"), sem("zeroed")
        x_kept, router_mm, logits_ready, routed, share_exp = (sem("x_kept"), sem("router_mm"), sem("logits_ready"),
                                                              sem("routed"), sem("share_exp"))
        x_late = sem("x_late")
        gap_ready, hots_ready, rank_mm, rows_step, rows_ready = (sem("gap_ready"), sem("hots_ready"), sem("rank_mm"),
                                                                 sem("rows_step"), sem("rows_ready"))
        consts_m = sem("consts_m")
        scattered = sem("scattered")
        gu_mm, silu_s_ready, act_s_ready, down_mm, h_shared = (sem("gu_mm"), sem("silu_s_ready"), sem("act_s_ready"),
                                                               sem("down_mm"), sem("h_shared"))
        xg_loaded = [sem("xg_loaded0"), sem("xg_loaded1")]
        y_stored = [sem("y_stored0"), sem("y_stored1")]
        xg_turned, xgT_ready, fc1_mm, silu_ready, u_ready = (sem("xg_turned"), sem("xgT_ready"), sem("fc1_mm"),
                                                             sem("silu_ready"), sem("u_ready"))
        u_turned, uT_ready, fc2_mm, y_ready = sem("u_turned"), sem("uT_ready"), sem("fc2_mm"), sem("y_ready")
        gathered = [sem(f"gathered{i}") for i in range(NT)]
        h_moe, rows_scaled = sem("h_moe"), sem("rows_scaled")
        wF_loaded, absum_ready, gamma_mm, tern_step = sem("wF_loaded"), sem("absum_ready"), sem("gamma_mm"), sem("tern_step")
        bias_split, bias_mm, b_out_ready, h_biased2 = sem("bias_split"), sem("bias_mm"), sem("b_out_ready"), sem("h_biased2")
        lnx_seq, fx_ready, fx_turned, x_hi_ready, x_split = (sem("lnx_seq"), sem("fx_ready"), sem("fx_turned"),
                                                             sem("x_hi_ready"), sem("x_split"))
        fc_mm, gelu_ready, lnf_seq, norm_ready = sem("fc_mm"), sem("gelu_ready"), sem("lnf_seq"), sem("norm_ready")
        n_turned, n_hi_ready, n_split, proj_mm, h_out = (sem("n_turned"), sem("n_hi_ready"), sem("n_split"),
                                                         sem("proj_mm"), sem("h_out"))
        wC_loaded, w_mm, w_folded, w_picked = sem("wC_loaded"), sem("w_mm"), sem("w_folded"), sem("w_picked")
        kv_mm, kv_hi, kv_ready = sem("kv_mm"), sem("kv_hi"), sem("kv_ready")
        q_mm, q_hi, q_ready = sem("q_mm"), sem("q_hi"), sem("q_ready")
        s1_mm, max1_ready, probs1_ready = sem("s1_mm"), sem("max1_ready"), sem("probs1_ready")
        p1_turned, p1_hi, p1_ready, pv1_mm = sem("p1_turned"), sem("p1_hi"), sem("p1_ready"), sem("pv1_mm")
        rinv1_ready, scaled_ready, o_ready = sem("rinv1_ready"), sem("scaled_ready"), sem("o_ready")
        out1_mm, h_lat, o_zeroed = sem("out1_mm"), sem("h_lat"), sem("o_zeroed")

        PROJECT_AT = {HEAD_STEPS * p + i + 1: (p, i) for p in range(PAIRS) for i in range(NT)}
        QUERY_AT = {7: (1, 0), 8: (1, 1), 11: (2, 0), 12: (2, 1), 21: (3, 0), 23: (3, 1), 36: (4, 0), 43: (4, 1)}
        TURN_AT = {31: 0, 32: 2, 33: 4}
        KEYS_AT = {34: 0, 35: 1}
        VALUES_AT = 44
        STATS_AT, CHAIN_AT, NORM_AT = (10, 11, 19), range(21, 21 + LN_CHAIN // 2), (27, 28, 29)
        CUTS = ((0, HALF), (HALF, T))
        BANKS = ((0, BANK), (BANK, T))

        passed = {"dve": sem("dve_passed"), "pool": sem("pool_passed")}
        passes = {"dve": 0, "pool": 0}

        def wait_apart(eng, name, s, value, times):
            eng.wait_ge(s, value)
            eng.sem_inc(passed[name], 1)
            passes[name] += times

        def rsqrt(dve, var, y, e, t, seq, at, steps=None):
            for k in range(LN_CHAIN) if steps is None else steps:
                if k and steps is None:
                    dve.wait_ge(seq, at + k)
                if k == 0:
                    op = dve.tensor_scalar(e, var, LN_EPS, None, ALU.add)
                elif k == 1:
                    op = dve.tensor_scalar(y.bitcast(I32), e.bitcast(I32), 1, None, ALU.logical_shift_right)
                elif k == 2:
                    op = dve.tensor_scalar(y.bitcast(I32), y.bitcast(I32), -1.0, float(RSQRT_SEED), ALU.mult, ALU.add)
                elif k % 3 == 0:
                    op = dve.scalar_tensor_tensor(t, y, 0.5, y, ALU.mult, ALU.mult)
                elif k % 3 == 1:
                    op = dve.tensor_tensor(t, t, e, ALU.mult)
                else:
                    op = dve.scalar_tensor_tensor(y, t, 1.5, y, ALU.subtract, ALU.mult, reverse0=True)
                op.then_inc(seq, 1)

        LN_CALL = 2 * NT + LN_CHAIN
        R_CALL = 2 * NT + 3
        LNX_CALL = 6 + LN_CHAIN
        LNF_CALL = 9 + LN_CHAIN + 1

        def layernorm(dve, g0, at, times, n=NT, seq=ln_seq, ready=xn_ready):
            for t in range(n):
                dve.bn_stats(bn6[0:TT, t, :], h[0:TT, g0 + t, :]).then_inc(seq, 1)
            wait_apart(dve, "dve", seq, at + n, times)
            for t in range(n):
                dve.bn_aggr(mv[0:TT, t, :], bn6[0:TT, t, :]).then_inc(seq, 1)
            dve.wait_ge(seq, at + 2 * n)
            rsqrt(dve, mv[0:TT, 0:n, 1], yr[0:TT, 0:n], ve[0:TT, 0:n], yt[0:TT, 0:n], seq, at + 2 * n)
            dve.wait_ge(seq, at + 2 * n + LN_CHAIN)
            for t in range(n):
                dve.tensor_scalar(xn[0:TT, t, :], h[0:TT, g0 + t, :], mv[0:TT, t, 0:1], yr[0:TT, t:t + 1],
                                  ALU.subtract, ALU.mult).then_inc(ready, 1)

        block = ctx.enter_context(nc.Block())

        @block.sync
        def _(sp):
            sp.dma_start(x_in[:, :, :], a["x"].rearrange("b c t -> c b t")).then_inc(x_loaded, 16)
            sp.dma_start(w_tok[:, :], a["tok_wT"]).then_inc(wA_loaded, 16)
            sp.dma_start(b_tok[0:TT, :], a["tok_b"].partition_broadcast(TT)).then_inc(wA_loaded, 16)
            for w, n in ((wq0, "wq0"), (wk0, "wk0"), (wv0, "wv0"), (wo0, "wo0")):
                sp.dma_start(w[:, :, :], a[n]).then_inc(wA_loaded, 16)
            sp.dma_start(bq0[:, :], a["bq0"]).then_inc(wA_loaded, 16)
            sp.dma_start(bk0[:, :], a["bk0"]).then_inc(wA_loaded, 16)
            sp.dma_start(bv0[0:TT, :], a["bv0"].partition_broadcast(TT)).then_inc(wA_loaded, 16)
            sp.dma_start(bo0[0:TT, :], a["bo0"].partition_broadcast(TT)).then_inc(wA_loaded, 16)
            sp.dma_start(router[:, :, :], a["router"]).then_inc(wM_loaded, 16)
            for w, n in ((gate, "gate"), (up, "up"), (down, "down")):
                sp.dma_start(w[:, :, :], a[n]).then_inc(wM_loaded, 16)
            sp.dma_start(fc1[:, :, :, :], a["fc1"]).then_inc(wM_loaded, 16)
            sp.dma_start(fc2[:, :, :, :], a["fc2"]).then_inc(wM_loaded, 16)
            sp.dma_start(wf_raw[:, :], a["wfcT"].rearrange("p k n -> p (k n)")).then_inc(wF_loaded, 16)
            sp.dma_start(wp_raw[:, :], a["wprojT"].rearrange("p k n -> p (k n)")).then_inc(wF_loaded, 16)
            sp.dma_start(ln_w[:, :], a["ln_w"]).then_inc(wF_loaded, 16)
            sp.dma_start(ln_b[:, :], a["ln_b"]).then_inc(wF_loaded, 16)
            sp.wait_ge(consts_m, 8)
            for j in range(NSLOT):
                sp.dma_start(xs_dram[j * SLOT:(j + 1) * SLOT, :], zeros[:, :]).then_inc(zeroed, 16)

            def load(j, p):
                sp.dma_start(xg[:, p, :], xs_dram[bass.ds(j * SLOT, SLOT), :]).then_inc(xg_loaded[p], 16)

            sp.wait_ge(scattered, 16 * 2 * NG)
            sp.wait_ge(down_mm, NG)
            for w, n in ((wq1, "wq1"), (wk_up, "wk_up"), (wo1, "wo1")):
                sp.dma_start(w[0:HD, :, :], a[n]).then_inc(wC_loaded, 16)
            for o in range(2):
                sp.dma_start(wv_up[0:HD, :, o * LAT:(o + 1) * LAT], a["wv_up"]).then_inc(wC_loaded, 16)
            for j in range(2):
                load(j, j)
            with sp.Fori(1, NSLOT // 2) as i:
                for p in range(2):
                    sp.wait_ge(xg_turned, 2 * i + p - 1)
                    load(2 * i + p, p)
            sp.wait_ge(fc2_mm, NSLOT)
            for o in range(2):
                sp.dma_start(w_kv[:, :, o * LAT:(o + 1) * LAT], a["wkvdT"]).then_inc(wC_loaded, 16)
            with sp.Fori(0, NGR) as g:
                sp.wait_ge(h_out, 3 * g + 3)
                sp.dma_start(out.rearrange("b (t p) d -> p (b t) d", p=TT)[:, bass.ds(3 * g, 3), :],
                             h[0:TT, bass.ds(3 * g, 3), :]).then_inc(stored, 16)
            sp.wait_ge(stored, 16 * NGR)

        WA = 10 * 16

        @block.gpsimd
        def _(pool):
            pool.memset(ident[:, :], 0.0).then_inc(ident_made, 1)
            pool.memset(mask[:, :], 0.0).then_inc(ident_made, 1)
            pool.wait_ge(ident_made, 2)
            pool.affine_select(out=ident[:, :], in_=ident[:, :], compare_op=ALU.not_equal, fill=1.0, base=0,
                               pattern=[[-1, 128]], channel_multiplier=1).then_inc(ident_made, 1)
            pool.affine_select(out=mask[:, :], in_=mask[:, :], compare_op=ALU.is_ge, fill=MASKED, base=0,
                               pattern=[[-1, TT]], channel_multiplier=1).then_inc(ident_made, 1)
            pool.memset(zeros[:, :], 0.0).then_inc(consts_m, 1)
            pool.memset(ones[:, :], 1.0).then_inc(consts_m, 1)
            pool.memset(restart[:, :, :], 1.0).then_inc(consts_m, 1)
            pool.iota(iota_e[:, :], pattern=[[1, E]], base=0, channel_multiplier=0,
                      allow_small_or_imprecise_dtypes=True).then_inc(consts_m, 1)
            pool.iota(iota_j[:, :], pattern=[[1, NSLOT]], base=0, channel_multiplier=0,
                      allow_small_or_imprecise_dtypes=True).then_inc(consts_m, 1)
            pool.iota(iota_c[:, :], pattern=[[SLOT, NG]], base=0, channel_multiplier=0,
                      allow_small_or_imprecise_dtypes=True).then_inc(consts_m, 1)
            pool.wait_ge(consts_m, 6)
            pool.memset(restart[:, :, 0:1], 0.0).then_inc(consts_m, 1)
            pool.affine_select(out=before[:, :], in_=ones[:, 0:TT], compare_op=ALU.is_gt, fill=0.0, base=0,
                               pattern=[[1, TT]], channel_multiplier=-1).then_inc(consts_m, 1)
            pool.wait_ge(wA_loaded, WA)
            with pool.Fori(0, B) as b:
                for t in range(NT):
                    pool.wait_ge(xn_ready, NT * b + t + 1)
                    pool.tensor_tensor(h[0:TT, b * NT + t, :], h[0:TT, b * NT + t, :], bo0[0:TT, :], ALU.add)\
                        .then_inc(h_biased, 1)

            with pool.Fori(0, B) as b:
                for t in range(NT):
                    wait_apart(pool, "pool", xn_ready, NT * b + NG + t + 1, B)
                    pool.tensor_copy(x_all[0:TT, b * NT + t, :], xn[0:TT, t, :]).then_inc(x_kept, 1)
            pool.wait_ge(rows_ready, 2)
            pool.wait_ge(x_kept, NG)
            pool.wait_ge(zeroed, 16 * NSLOT)
            for t in range(NG):
                for c in range(2):
                    pool.indirect_dma_start(
                        out=xs_dram[:, :], out_offset=bass.IndirectOffsetOnAxis(ap=row[0:TT, c, t:t + 1], axis=0),
                        in_=x_all[0:TT, t, :], in_offset=None).then_inc(scattered, 16)
            for p in range(2):
                pool.wait_ge(y_stored[p], 16 * (NSLOT // 2))

            def gather(b):
                for i in range(NT):
                    t = b * NT + i
                    if b:
                        pool.wait_ge(h_moe, 2 * (t - NT + 1))
                    for c in range(2):
                        pool.indirect_dma_start(
                            out=ring[0:TT, i, c, :], out_offset=None, in_=ys_dram[:, :],
                            in_offset=bass.IndirectOffsetOnAxis(ap=row[0:TT, c, t:t + 1], axis=0))\
                            .then_inc(gathered[i], 16)

            gather(0)
            pool.wait_ge(w_folded, 6)
            pool.tensor_copy(w_qp[:, :, :], w_qk[:, 0, :, :]).then_inc(w_picked, 1)
            gather(1)

            def pick(b, n):
                pool.wait_ge(q_mm, 2 * (PAIRS * b + n + 1))
                pool.tensor_copy(w_qp[:, :, :], w_qk[:, (n + 1) % PAIRS, :, :]).then_inc(w_picked, 1)

            def combine(b, i):
                t = b * NT + i
                pool.wait_ge(gathered[i], 32 * (b + 1))
                pool.tensor_tensor(ring[0:TT, i, :, :], ring[0:TT, i, :, :],
                                   share[0:TT, :, t:t + 1].to_broadcast([TT, 2, D]), ALU.mult).then_inc(rows_scaled, 1)
                pool.wait_ge(rows_scaled, t - NT + 1)
                for c in range(2):
                    if c:
                        pool.wait_ge(h_moe, 2 * t + 1)
                    pool.tensor_tensor(h[0:TT, t, :], ring[0:TT, i, c, :], h[0:TT, t, :], ALU.add).then_inc(h_moe, 1)

            for b in range(B):
                pick(b, 0)
                if b + 1 < B:
                    for i in range(NT):
                        combine(b + 1, i)
                pick(b, 1)
                pick(b, 2)
                if b + 2 < B:
                    gather(b + 2)
                pick(b, PAIRS - 1)
            pool.wait_ge(b_out_ready, 1)
            with pool.Fori(0, NG) as t:
                pool.wait_ge(fx_ready, t + 1)
                pool.tensor_tensor(h[0:TT, t, :], h[0:TT, t, :], b_out[0:TT, :], ALU.add).then_inc(h_biased2, 1)
            pool.wait_ge(passed["pool"], passes["pool"])

        @block.vector
        def _(dve):
            dve.memset(decay[:, :], 1.0 - ALPHA).then_inc(const_made, 1)
            dve.wait_ge(wA_loaded, WA)
            dve.tensor_scalar(bq0s[:, :], bq0[:, :], 1.0 / 16, None, ALU.mult).then_inc(const_made, 1)
            dve.wait_ge(const_made, 2)
            dve.wait_ge(x_loaded, 16)
            dve.wait_ge(ident_made, 4)
            with dve.Fori(0, B) as b:
                ew = 6 * b
                dve.tensor_scalar(x_scaled[:, :], x_in[:, b, :], ALPHA / 2, None, ALU.mult).then_inc(ew_step, 1)
                dve.tensor_scalar(fwd[:, 0:1], x_in[:, b, 0:1], 0.5, None, ALU.mult).then_inc(ew_step, 1)
                dve.tensor_scalar(bwd[:, T - 1:T], x_in[:, b, T - 1:T], 0.5, None, ALU.mult).then_inc(ew_step, 1)
                dve.wait_ge(ew_step, ew + 3)
                dve.tensor_tensor_scan(fwd[:, 1:T], decay[:, 0:1].to_broadcast([128, T - 1]), x_scaled[:, 1:T],
                                       fwd[:, 0:1], ALU.mult, ALU.add).then_inc(ew_step, 1)
                dve.tensor_tensor_scan(bwd[:, T - 2::-1], decay[:, 0:1].to_broadcast([128, T - 1]),
                                       x_scaled[:, T - 2::-1], bwd[:, T - 1:T], ALU.mult, ALU.add).then_inc(ew_step, 1)
                dve.wait_ge(ew_step, ew + 5)
                dve.tensor_tensor(ewma[:, :], fwd[:, :], bwd[:, :], ALU.add).then_inc(ew_step, 1)
                for t in range(NT):
                    dve.wait_ge(tok_mm, NT * b + t + 1)
                    dve.tensor_tensor(h[0:TT, b * NT + t, :], bank(t, 0, D, 0, TT), b_tok[0:TT, :], ALU.add)\
                        .then_inc(h_tok, 1)
                wait_apart(dve, "dve", h_tok, NT * b + NT, B)
                layernorm(dve, b * NT, LN_CALL * b, B)
                for t in range(NT):
                    dve.wait_ge(v_mm, NT * b + t + 1)
                    dve.tensor_tensor(v0[0:TT, t, :], bank(t, 0, D, 0, TT), bv0[0:TT, :], ALU.add).then_inc(v_ready, 1)

                def dve_scores(i):
                    n, s = (i + 1) * TT, 2 * (i % 2)
                    diag = bank(s, i * TT, n, 0, TT)
                    dve.wait_ge(s_mm, NT * b + i + 1)
                    dve.tensor_tensor(diag, diag, mask[0:TT, :], ALU.add).then_inc(s_masked, 1)
                    dve.wait_ge(s_masked, NT * b + i + 1)
                    dve.tensor_reduce(negmax[0:TT, i % 2:i % 2 + 1], bank(s, 0, n, 0, TT), AX.X, ALU.max,
                                      negate=True).then_inc(max_ready, 1)

                def dve_pT(i):
                    dve.wait_ge(p_turned, NT * b + i + 1)
                    src = bank(4, 0, (i + 1) * 128, 0, TT).rearrange("p (k q) -> p k q", q=128)[:, :, 0:TT]
                    dve.tensor_copy(pT[0:TT, i % 2, 0:i + 1, :], src).then_inc(pT_ready, 1)
                    dve.reciprocal(rinv[0:TT, i % 2:i % 2 + 1], rowsum[0:TT, i % 2:i % 2 + 1]).then_inc(rinv_ready, 1)

                def dve_h(i):
                    dve.wait_ge(wo_mm, NT * b + i + 1)
                    dve.wait_ge(h_biased, NT * b + i + 1)
                    dve.tensor_tensor(h[0:TT, b * NT + i, :], bank(7, D, 2 * D, 0, TT), h[0:TT, b * NT + i, :],
                                      ALU.add).then_inc(h_attn, 1)

                dve_scores(0)
                for i in range(NT):
                    if i + 1 < NT:
                        dve_scores(i + 1)
                    dve_pT(i)
                    if i >= 1:
                        dve_h(i - 1)
                dve_h(NT - 1)

            MB = ISH // 128

            def dve_act_s(c, half, m):
                dve.wait_ge(silu_s_ready, MB * c + m + 1)
                dve.tensor_tensor(act_s[:, m, half * HALF:(half + 1) * HALF], silu_s[:, m % 2, :],
                                  bank(2 * (m % 3) + 1, 0, HALF), ALU.mult).then_inc(act_s_ready, 1)

            def dve_h_shared(c, b, half):
                for t in range(3):
                    dve.wait_ge(down_mm, 3 * c + t + 1)
                    hh = h[0:TT, b * NT + half * 3 + t, :]
                    dve.tensor_tensor(hh, bank(6 + t % 2, 0, D, 0, TT), hh, ALU.add).then_inc(h_shared, 1)

            dve.wait_ge(consts_m, 8)
            dve.wait_ge(h_attn, NG)
            layernorm(dve, 0, LN_CALL * B, 1)
            with dve.Fori(0, B) as b:
                dve.wait_ge(router_mm, b + 1)
                dve.tensor_copy(logits[0:TT, :, :], bank(6, 0, NT * E, 0, TT).rearrange("p (t e) -> p t e", e=E))\
                    .then_inc(logits_ready, 1)
                r = R_CALL * b
                wait_apart(dve, "dve", logits_ready, b + 1, B)
                for t in range(NT):
                    dve.max(top[0:TT, t, :], logits[0:TT, t, :]).then_inc(routed, 1)
                wait_apart(dve, "dve", routed, r + NT, B)
                for t in range(NT):
                    dve.max_index(top_i[0:TT, t, :], top[0:TT, t, :], logits[0:TT, t, :]).then_inc(routed, 1)
                dve.tensor_tensor(gap[0:TT, 0, bass.ds(b * NT, NT)], top[0:TT, :, 1], top[0:TT, :, 0], ALU.subtract)\
                    .then_inc(gap_ready, 1)
                dve.wait_ge(routed, r + 2 * NT)
                dve.tensor_copy(top_f[0:TT, :, :], top_i[0:TT, :, 0:2]).then_inc(routed, 1)
                dve.wait_ge(routed, r + 2 * NT + 1)
                for c in range(2):
                    dve.tensor_tensor(hot[0:TT, c, bass.ds(b * NT, NT), :],
                                      top_f[0:TT, :, c:c + 1].to_broadcast([TT, NT, E]),
                                      iota_e[0:TT, :].unsqueeze(1).to_broadcast([TT, NT, E]), ALU.is_equal)\
                        .then_inc(routed, 1)
                dve.wait_ge(routed, r + R_CALL)
                dve_act_s(b, 0, 0)
                at, nxt = LN_CALL * (B + 1 + b), (b + 1) % B * NT
                for t in range(NT):
                    dve.bn_stats(bn6[0:TT, t, :], h[0:TT, nxt + t, :]).then_inc(ln_seq, 1)
                dve_act_s(b, 0, 1)
                wait_apart(dve, "dve", ln_seq, at + NT, B)
                for t in range(NT):
                    dve.bn_aggr(mv[0:TT, t, :], bn6[0:TT, t, :]).then_inc(ln_seq, 1)
                dve.wait_ge(ln_seq, at + 2 * NT)
                rsqrt(dve, mv[0:TT, 0:NT, 1], yr[0:TT, 0:NT], ve[0:TT, 0:NT], yt[0:TT, 0:NT], ln_seq, at + 2 * NT)
                dve_act_s(b, 0, 2)
                dve.wait_ge(ln_seq, at + LN_CALL)
                dve.wait_ge(x_kept, NT * b + NT)
                for t in range(NT):
                    dve.tensor_scalar(xn[0:TT, t, :], h[0:TT, nxt + t, :], mv[0:TT, t, 0:1], yr[0:TT, t:t + 1],
                                      ALU.subtract, ALU.mult).then_inc(xn_ready, 1)
                    if t == 1:
                        dve_act_s(b, 0, 3)
                dve_h_shared(b, b, 0)

            steps = [0]

            def step(ins):
                steps[0] += 1
                ins.then_inc(rows_step, 1)
                dve.wait_ge(rows_step, steps[0])

            dve.tensor_tensor(hots[0:TT, :, :], hot[0:TT, 0, :, :], hot[0:TT, 1, :, :], ALU.add)\
                .then_inc(hots_ready, 1)
            dve.wait_ge(share_exp, 1)
            step(dve.tensor_scalar(gap[0:TT, 0, :], gap[0:TT, 1, :], 1.0, None, ALU.add))
            step(dve.reciprocal(share[0:TT, 0, 0:NG], gap[0:TT, 0, :]))
            step(dve.tensor_tensor(share[0:TT, 1, 0:NG], share[0:TT, 0, 0:NG], gap[0:TT, 1, :], ALU.mult))
            dve.wait_ge(rank_mm, 1)
            step(dve.tensor_copy(tot[0:TT, :, :], bank(7, 0, NG * E, 0, TT).rearrange("p (t e) -> p e t", e=E)))
            flat = lambda v: v[0:TT, :, :].rearrange("p e t -> p (e t)")
            step(dve.tensor_tensor_scan(flat(incl), flat(restart), flat(tot), 0.0, ALU.mult, ALU.add))
            step(dve.tensor_tensor(over[0:TT, :, :], incl[0:TT, :, NG - 1:NG].to_broadcast([TT, E, NG]),
                                   iota_c[0:TT, :].unsqueeze(1).to_broadcast([TT, E, NG]), ALU.is_gt))
            step(dve.tensor_reduce(n_slots[0:TT, :], over[0:TT, :, :], AX.X, ALU.add))
            step(dve.tensor_tensor_scan(slot_end[0:TT, :], ones[0:TT, 0:E], n_slots[0:TT, :], 0.0, ALU.mult, ALU.add))
            step(dve.tensor_tensor(slot_beg[0:TT, :], slot_end[0:TT, :], n_slots[0:TT, :], ALU.subtract))
            step(dve.tensor_tensor(incl[0:TT, :, :], incl[0:TT, :, :], tot[0:TT, :, :], ALU.subtract))
            step(dve.scalar_tensor_tensor(base[0:TT, :, :], slot_beg[0:TT, :].unsqueeze(2).to_broadcast([TT, E, NG]),
                                          float(SLOT), incl[0:TT, :, :], ALU.mult, ALU.add))
            step(dve.tensor_tensor(place[0:TT, :, :], bank(6, 0, NG * E, 0, TT).rearrange("p (t e) -> p t e", e=E),
                                   base[0:TT, :, :].rearrange("p e t -> p t e"), ALU.add))
            for c in range(2):
                step(dve.tensor_tensor(picked[0:TT, c, :, :], hot[0:TT, c, :, :], place[0:TT, :, :], ALU.mult))
                step(dve.tensor_reduce(row_f[0:TT, c, :], picked[0:TT, c, :, :], AX.X, ALU.add))
            dve.tensor_copy(row[0:TT, :, :], row_f[0:TT, :, :]).then_inc(rows_ready, 1)
            step(dve.tensor_tensor(ended[:, :, :], slot_end[0:1, :].unsqueeze(1).to_broadcast([1, NSLOT, E]),
                                   iota_j[0:1, :].unsqueeze(2).to_broadcast([1, NSLOT, E]), ALU.is_le))
            step(dve.tensor_reduce(slot_e_f[:, :], ended[:, :, :], AX.X, ALU.add))
            dve.tensor_scalar(slot_e[:, :], slot_e_f[:, :], float(E - 1), None, ALU.min).then_inc(rows_ready, 1)

            with dve.Fori(0, B) as b:
                for m in range(MB):
                    dve_act_s(b + B, 1, m)
                dve_h_shared(b + B, b, 1)

            def dve_expert(j, p):
                dve.wait_ge(silu_ready, j + 1)
                dve.tensor_tensor(u[:, p, :], silu[:, p, :], bank(2 + p, I, 2 * I), ALU.mult).then_inc(u_ready, 1)

            def dve_uT(j, p):
                dve.wait_ge(u_turned, j + 1)
                dve.tensor_copy(uT[:, p, :, :], bank(4 + p, 0, KD * SLOT).rearrange("p (k q) -> p k q", k=KD))\
                    .then_inc(uT_ready, 1)

            dve_expert(0, 0)
            dve_uT(0, 0)
            dve_expert(1, 1)
            with dve.Fori(1, NSLOT // 2) as i:
                for p in range(2):
                    dve_uT(2 * i + p - 1, 1 - p)
                    dve_expert(2 * i + p, p)
            dve_uT(NSLOT - 1, 1)

            dve.wait_ge(wF_loaded, 4 * 16)
            for c, w in enumerate((wf_raw, wp_raw)):
                dve.tensor_reduce(absum[:, c:c + 1], w[:, :], AX.X, ALU.add, apply_absolute_value=True)\
                    .then_inc(absum_ready, 1)
            dve.wait_ge(gamma_mm, 1)
            half = 0.5 / (FH * D)
            dve.tensor_scalar(above[:, :], bank(7, 0, 2), half, GAMMA_EPS / 2, ALU.mult, ALU.add).then_inc(tern_step, 1)
            dve.wait_ge(tern_step, 1)
            dve.tensor_scalar(below[:, :], above[:, :], -1.0, None, ALU.mult).then_inc(tern_step, 1)
            negs = probs[:, :, :].rearrange("p a t -> p (a t)")[:, 0:FH]
            flat_f = w_f[:, :, :].rearrange("p k n -> p (k n)")
            flat_p = w_p[:, :, :].rearrange("p k n -> p (k n)")
            for n in range(4):
                c, lo = n // 2, n % 2 * FH
                w, q = (wf_raw, flat_f) if c == 0 else (wp_raw, flat_p)
                dve.wait_ge(tern_step, 2 + 2 * n)
                dve.tensor_scalar(negs, w[:, lo:lo + FH], below[:, c:c + 1], -1.0, ALU.is_lt, ALU.mult)\
                    .then_inc(tern_step, 1)
                dve.wait_ge(tern_step, 3 + 2 * n)
                dve.scalar_tensor_tensor(q[:, lo:lo + FH], w[:, lo:lo + FH], above[:, c:c + 1], negs,
                                         ALU.is_gt, ALU.add).then_inc(tern_step, 1)

            for t in range(NT):
                dve.wait_ge(gathered[t], 32)
                for c in range(2):
                    if c:
                        dve.wait_ge(h_moe, 2 * t + 1)
                    dve.scalar_tensor_tensor(h[0:TT, t, :], ring[0:TT, t, c, :], share[0:TT, c, t:t + 1],
                                             h[0:TT, t, :], ALU.mult, ALU.add).then_inc(h_moe, 1)
            dve.wait_ge(h_moe, 2 * NT)

            dve.sem_inc(o_ready, 1)
            dve.memset(o_T[:, :, :], 0.0).then_inc(o_zeroed, 1)

            def dve_k(b, c):
                lo, hi = CUTS[c]
                dve.wait_ge(kv_hi, 3 * b + c + 1)
                dve.tensor_tensor(k_lo[:, b % 2, lo:hi], bank(7, 0, hi - lo), k_hi[:, b % 2, lo:hi].bitcast(F32),
                                  ALU.subtract).then_inc(kv_ready, 1)

            def dve_v(b):
                dve.wait_ge(kv_hi, 3 * b + 3)
                dve.tensor_tensor(v_st[0:TT, :, LAT:2 * LAT],
                                  bank(7, 0, NT * LAT, 0, TT).rearrange("p (t l) -> p t l", l=LAT),
                                  v_st[0:TT, :, 0:LAT].bitcast(F32), ALU.subtract).then_inc(kv_ready, 1)

            def dve_q(b, p, c):
                lo, hi = CUTS[c]
                dve.wait_ge(q_hi, 4 * (PAIRS * b + p) + 2 * c + 2)
                for n in range(2):
                    own, other = ((0, 64), (64, 128))[::1 - 2 * n]
                    q = q_st[:, 2 * (p % 2) + n, lo:hi]
                    dve.tensor_tensor(q[other[0]:other[1], :], bank(7, 0, hi - lo, own[0], own[1]),
                                      q[own[0]:own[1], :].bitcast(F32), ALU.subtract).then_inc(q_ready, 1)

            def dve_max(g):
                dve.wait_ge(s1_mm, first + g + 1)
                dve.tensor_reduce(negmax[0:TT, g % 2:g % 2 + 1], bank(2 * (g % 2), 0, T, 0, TT), AX.X, ALU.max,
                                  negate=True).then_inc(max1_ready, 1)

            def dve_rinv(g):
                dve.wait_ge(probs1_ready, first + g + 1)
                dve.reciprocal(rinv1[0:TT, g % 2:g % 2 + 1], rowsum[0:TT, g % 2:g % 2 + 1]).then_inc(rinv1_ready, 1)

            def dve_lo(g):
                for c in range(2):
                    dve.wait_ge(p1_hi, 2 * (first + g) + c + 1)
                    src = bank(4 + c, 0, 3 * TT, 0, TT).rearrange("p (k q) -> p k q", q=TT)
                    dve.tensor_tensor(pT1[0:TT, g % 2, 3 * c:3 * c + 3, 1, :], src,
                                      pT1[0:TT, g % 2, 3 * c:3 * c + 3, 0, :].bitcast(F32), ALU.subtract)\
                        .then_inc(p1_ready, 1)

            def dve_o(g):
                t, n = g % NT, g // NT % 2
                dve.wait_ge(pv1_mm, first + g + 1)
                dve.tensor_reduce(o_T[:, n, t * TT:(t + 1) * TT],
                                  bank(6, 0, 2 * TT).rearrange("p (a q) -> p q a", a=2), AX.X, ALU.add)\
                    .then_inc(o_ready, 1)

            def dve_out(slot, b, i, at=7):
                dve.wait_ge(out1_mm, NT * slot + i + 1)
                hh = h[0:TT, b * NT + i, :]
                dve.tensor_tensor(hh, bank(at, 0, D, 0, TT), hh, ALU.add).then_inc(h_lat, 1)

            def dve_ln(b, s):
                at = LN_CALL * (2 * B + 2 + b)
                nxt = (b + 1) % B * NT
                if s in STATS_AT:
                    if s == STATS_AT[0]:
                        wait_apart(dve, "dve", h_moe, 2 * NT * ((b + 1) % B + 1), B)
                    t = 2 * STATS_AT.index(s)
                    for t in (t, t + 1):
                        dve.bn_stats(bn6[0:TT, t, :], h[0:TT, nxt + t, :]).then_inc(ln_seq, 1)
                if s == STATS_AT[-1] + 1:
                    wait_apart(dve, "dve", ln_seq, at + NT, B)
                    for t in range(NT):
                        dve.bn_aggr(mv[0:TT, t, :], bn6[0:TT, t, :]).then_inc(ln_seq, 1)
                if s in CHAIN_AT:
                    for k in (2 * CHAIN_AT.index(s), 2 * CHAIN_AT.index(s) + 1):
                        dve.wait_ge(ln_seq, at + 2 * NT + k)
                        rsqrt(dve, mv[0:TT, 0:NT, 1], yr[0:TT, 0:NT], ve[0:TT, 0:NT], yt[0:TT, 0:NT], ln_seq,
                              at + 2 * NT, [k])
                if s in NORM_AT:
                    if s == NORM_AT[0]:
                        dve.wait_ge(ln_seq, at + LN_CALL)
                    t = 2 * NORM_AT.index(s)
                    for t in (t, t + 1):
                        dve.tensor_scalar(xn[0:TT, t, :], h[0:TT, nxt + t, :], mv[0:TT, t, 0:1], yr[0:TT, t:t + 1],
                                          ALU.subtract, ALU.mult).then_inc(xn_ready, 1)

            layernorm(dve, 0, LN_CALL * (2 * B + 1), 1)
            first = 0
            for c in range(2):
                dve_k(0, c)
            for c in range(2):
                dve_q(0, 0, c)
            dve_v(0)
            dve_max(0)
            dve_max(1)
            dve_rinv(0)
            dve_max(2)
            dve_rinv(1)
            dve_max(3)
            dve_rinv(2)
            dve_lo(0)
            with dve.Fori(0, B) as b:
                first = STEPS * b
                for s in range(1, STEPS + 1):
                    dve_max(s + 3)
                    dve_rinv(s + 2)
                    dve_lo(s)
                    dve_o(s - 1)
                    if s in PROJECT_AT:
                        p, i = PROJECT_AT[s]
                        dve_out(PAIRS * b + p, b if p else (b + B - 1) % B, i)
                    dve_ln(b, s)
                    if s in QUERY_AT:
                        p, c = QUERY_AT[s]
                        dve_q(b, p, c)
                    if s in KEYS_AT:
                        dve_k(b + 1, KEYS_AT[s])
                dve_v(b + 1)
            for i in range(NT):
                dve_out(PAIRS * B, B - 1, i, (7, 6)[i % 2])
            dve.wait_ge(h_lat, NT * (PAIRS * B + 1))

            dve.wait_ge(bias_split, 1)
            dve.tensor_tensor(n_lo[:, :, 0:TT], ln_b[:, :].unsqueeze(2).to_broadcast([128, FB, TT]),
                              n_hi[:, :, 0:TT].bitcast(F32), ALU.subtract).then_inc(bias_split, 1)
            dve.wait_ge(bias_mm, 1)
            dve.tensor_copy(b_out[0:TT, :], bank(7, 0, D, 0, TT)).then_inc(b_out_ready, 1)

            def rounds(g):
                return 1 if isinstance(g, int) else NGR // 2 - 1

            def dve_x(g):
                layernorm(dve, 3 * g, LNX_CALL * g, rounds(g), 3, lnx_seq, fx_ready)

            def dve_x_stats(g, f):
                at = LNX_CALL * g
                if f == 0:
                    for t in range(3):
                        dve.bn_stats(bn6[0:TT, t, :], h[0:TT, 3 * g + t, :]).then_inc(lnx_seq, 1)
                else:
                    wait_apart(dve, "dve", lnx_seq, at + 3, rounds(g))
                    for t in range(3):
                        dve.bn_aggr(mv[0:TT, t, :], bn6[0:TT, t, :]).then_inc(lnx_seq, 1)

            def dve_x_norm(g):
                dve.wait_ge(lnx_seq, LNX_CALL * (g + 1))
                for t in range(3):
                    dve.tensor_scalar(xn[0:TT, t, :], h[0:TT, 3 * g + t, :], mv[0:TT, t, 0:1], yr[0:TT, t:t + 1],
                                      ALU.subtract, ALU.mult).then_inc(fx_ready, 1)

            def dve_x_lo(g):
                for k in range(KD):
                    dve.wait_ge(x_hi_ready, KD * g + k + 1)
                    dve.tensor_tensor(x_lo[:, k, :], bank(k, 0, GT), x_hi[:, k, :].bitcast(F32), ALU.subtract)\
                        .then_inc(x_split, 1)

            def dve_bn(g, p, t):
                wait_apart(dve, "dve", gelu_ready, 3 * g + t + 1, rounds(g))
                for c in range(2):
                    dve.bn_stats(bn_f[0:TT, t, c, :], hidden[0:TT, p, t, c * BANK:(c + 1) * BANK]).then_inc(lnf_seq, 1)

            def dve_norm(g, x_too=False):
                at, x_at = LNF_CALL * g, LNX_CALL * (g + 1) + 6
                wait_apart(dve, "dve", lnf_seq, at + 6, rounds(g))
                for t in range(3):
                    dve.bn_aggr(mv_f[0:TT, t, :], bn_f[0:TT, t, :, :].rearrange("p c s -> p (c s)")).then_inc(lnf_seq, 1)
                for k in range(LN_CHAIN):
                    dve.wait_ge(lnf_seq, at + 9 + k)
                    rsqrt(dve, mv_f[0:TT, :, 1], yr_f[0:TT, :], ve_f[0:TT, :], yt_f[0:TT, :], lnf_seq, at + 9, [k])
                    if x_too:
                        dve.wait_ge(lnx_seq, x_at + k)
                        rsqrt(dve, mv[0:TT, 0:3, 1], yr[0:TT, 0:3], ve[0:TT, 0:3], yt[0:TT, 0:3], lnx_seq, x_at, [k])
                dve.wait_ge(lnf_seq, at + 9 + LN_CHAIN)
                dve.scalar_tensor_tensor(nm_f[0:TT, :], mv_f[0:TT, :, 0], -1.0, yr_f[0:TT, :], ALU.mult, ALU.mult)\
                    .then_inc(lnf_seq, 1)

            def dve_n_lo(g, f):
                dve.wait_ge(n_hi_ready, FB * g + f + 1)
                dve.scalar_tensor_tensor(n_lo[:, f, :], bank(f % 2, 0, GT), ln_w[:, f:f + 1],
                                         n_hi[:, f, :].bitcast(F32), ALU.mult, ALU.subtract).then_inc(n_split, 1)

            def dve_out(g, t):
                dve.wait_ge(proj_mm, 3 * g + t + 1)
                dve.wait_ge(h_biased2, 3 * g + t + 1)
                hh = h[0:TT, 3 * g + t, :]
                dve.tensor_tensor(hh, bank(6 + t % 2, 0, D, 0, TT), hh, ALU.add).then_inc(h_out, 1)

            def dve_step(g, p, more=True, more2=True):
                if more:
                    dve_x_lo(g + 1)
                for f in range(FB):
                    dve_n_lo(g, f)
                    if more2 and f < 2:
                        dve_x_stats(g + 2, f)
                    if more and f in (2, 4, 6):
                        dve_bn(g + 1, 1 - p, (f - 2) // 2)
                if more:
                    dve_norm(g + 1, more2)
                if more2:
                    dve_x_norm(g + 2)
                for t in range(3):
                    dve_out(g, t)

            dve_x(0)
            dve_x_lo(0)
            dve_x(1)
            for t in range(3):
                dve_bn(0, 0, t)
            dve_norm(0)
            with dve.Fori(0, NGR // 2 - 1) as i:
                for p in range(2):
                    dve_step(2 * i + p, p)
            dve_step(NGR - 2, 0, True, False)
            dve_step(NGR - 1, 1, False, False)
            dve.wait_ge(passed["dve"], passes["dve"])

        @block.scalar
        def _(act):
            act.wait_ge(const_made, 2)
            act.wait_ge(wA_loaded, WA)
            with act.Fori(0, B) as b:
                for t in range(NT):
                    act.wait_ge(xn_turned, NT * b + t + 1)
                    act.copy(xT[:, :, t * TT:(t + 1) * TT],
                             bank(t, 0, KD * TT).rearrange("p (k q) -> p k q", k=KD)).then_inc(xT_ready, 1)
                for j in range(8):
                    m, half, isk = j // 2 % 2, j % 2, j // 4
                    dst = (kT if isk else qT)[:, m, half * 375:(half + 1) * 375]
                    act.wait_ge(qk_mm, 8 * b + j + 1)
                    act.activation(dst, bank(j, 0, 375), ACT.Identity,
                                   bias=(bk0 if isk else bq0s)[:, m:m + 1], scale=1.0 if isk else 1.0 / 16)\
                        .then_inc(qk_ready, 1)

                def act_exp(i):
                    n, s = (i + 1) * TT, i % 2
                    act.wait_ge(max_ready, NT * b + i + 1)
                    act.activation(probs[0:TT, s, 0:n], bank(2 * s, 0, n, 0, TT), ACT.Exp,
                                   bias=negmax[0:TT, s:s + 1], scale=1.0, accum_out=rowsum[0:TT, s:s + 1])\
                        .then_inc(probs_ready, 1)

                def act_ctx(i):
                    act.wait_ge(pv_mm, NT * b + i + 1)
                    act.wait_ge(rinv_ready, NT * b + i + 1)
                    act.mul(ctxt[0:TT, :], bank(6, 0, D, 0, TT), rinv[0:TT, i % 2:i % 2 + 1]).then_inc(ctx_ready, 1)

                def act_ctxT(i):
                    act.wait_ge(ctx_turned, NT * b + i + 1)
                    act.copy(ctxT[:, :, :], bank(7, 0, KD * TT).rearrange("p (k q) -> p k q", k=KD))\
                        .then_inc(ctxT_ready, 1)

                act_exp(0)
                for i in range(NT):
                    if i + 1 < NT:
                        act_exp(i + 1)
                    act_ctx(i)
                    act_ctxT(i)

            MB = ISH // 128

            def act_silu_s(c, m):
                act.wait_ge(gu_mm, MB * c + m + 1)
                if m >= 2:
                    act.wait_ge(act_s_ready, MB * c + m - 1)
                act.activation(silu_s[:, m % 2, :], bank(2 * (m % 3), 0, HALF), ACT.Silu).then_inc(silu_s_ready, 1)

            with act.Fori(0, B) as b:
                for t in range(NT):
                    act.wait_ge(xn_turned, NT * b + NG + t + 1)
                    act.copy(xT[:, :, t * TT:(t + 1) * TT],
                             bank(t, 0, KD * TT).rearrange("p (k q) -> p k q", k=KD)).then_inc(xT_ready, 1)
                act_silu_s(b, 0)
                act.wait_ge(xT_ready, NT * b + NG + NT)
                act.copy(xT_late[:, :, bass.ds(b * HALF, HALF)], xT[:, :, HALF:T]).then_inc(x_late, 1)
                for m in range(1, MB):
                    act_silu_s(b, m)
                act.wait_ge(x_late, b + 1)
            act.wait_ge(gap_ready, B)
            act.activation(gap[0:TT, 1, :], gap[0:TT, 0, :], ACT.Exp).then_inc(share_exp, 1)
            with act.Fori(B, 2 * B) as c:
                for m in range(MB):
                    act_silu_s(c, m)

            def act_xgT(j, p):
                act.wait_ge(xg_turned, j + 1)
                act.copy(xgT[:, p, :, :], bank(p, 0, KD * SLOT).rearrange("p (k q) -> p k q", k=KD))\
                    .then_inc(xgT_ready, 1)

            def act_silu(j, p):
                act.wait_ge(fc1_mm, j + 1)
                act.activation(silu[:, p, :], bank(2 + p, 0, I), ACT.Silu).then_inc(silu_ready, 1)

            def act_y(j, p, wait):
                act.wait_ge(fc2_mm, j + 1)
                if wait:
                    act.wait_ge(y_stored[p], 8 * (j - p))
                act.copy(y_out[:, p, :], bank(6 + p, 0, D)).then_inc(y_ready, 1)

            def store_y(j, p):
                act.wait_ge(y_ready, j + 1)
                act.dma_start(ys_dram[bass.ds(j * SLOT, SLOT), :], y_out[:, p, :]).then_inc(y_stored[p], 16)

            act_xgT(0, 0)
            act_silu(0, 0)
            act_xgT(1, 1)
            act_silu(1, 1)
            act_xgT(2, 0)
            act_y(0, 0, False)
            act_silu(2, 0)
            store_y(0, 0)
            act_xgT(3, 1)
            act_y(1, 1, False)
            act_silu(3, 1)
            store_y(1, 1)
            with act.Fori(2, NSLOT // 2) as i:
                for p in range(2):
                    act_xgT(2 * i + p, p)
                    act_y(2 * i + p - 2, p, True)
                    act_silu(2 * i + p, p)
                    store_y(2 * i + p - 2, p)
            for p in range(2):
                act_y(NSLOT - 2 + p, p, True)
                store_y(NSLOT - 2 + p, p)

            act.wait_ge(w_mm, 1)
            for c in range(2):
                act.mul(w_qk[:, 2 * c:2 * c + 2, :, :],
                        bank(c).rearrange("p (n k m) -> p n k m", n=2, k=KD), HD ** -0.5).then_inc(w_folded, 1)
            for c in range(4):
                act.copy(w_vo[:, 2 * c:2 * c + 2, :], bank(2 + c).rearrange("p (n m) -> p n m", n=2))\
                    .then_inc(w_folded, 1)

            def act_xT1(b, t):
                act.wait_ge(xn_turned, NT * b + 2 * NG + t + 2)
                act.copy(xT[:, :, t * TT:(t + 2) * TT],
                         bank(7, 0, KD * 2 * TT).rearrange("p (k q) -> p k q", k=KD)).then_inc(xT_ready, 2)

            def act_k(b, c):
                lo, hi = CUTS[c]
                act.wait_ge(kv_mm, 3 * b + c + 1)
                act.copy(k_hi[:, b % 2, lo:hi], bank(7, 0, hi - lo)).then_inc(kv_hi, 1)

            def act_v(b):
                act.wait_ge(kv_mm, 3 * b + 3)
                act.copy(v_st[0:TT, :, 0:LAT], bank(7, 0, NT * LAT, 0, TT).rearrange("p (t l) -> p t l", l=LAT))\
                    .then_inc(kv_hi, 1)

            def act_q(b, p, c):
                lo, hi = CUTS[c]
                act.wait_ge(q_mm, 2 * (PAIRS * b + p) + c + 1)
                for n, (p0, p1) in enumerate(((0, 64), (64, 128))):
                    act.copy(q_st[p0:p1, 2 * (p % 2) + n, lo:hi], bank(7, 0, hi - lo, p0, p1)).then_inc(q_hi, 1)

            def act_exp1(g):
                act.wait_ge(max1_ready, first + g + 1)
                act.activation(probs1[0:TT, g % 3, :], bank(2 * (g % 2), 0, T, 0, TT), ACT.Exp,
                               bias=negmax[0:TT, g % 2:g % 2 + 1], scale=1.0,
                               accum_out=rowsum[0:TT, g % 2:g % 2 + 1]).then_inc(probs1_ready, 1)

            def act_scale(g):
                act.wait_ge(rinv1_ready, first + g + 1)
                act.mul(probs1[0:TT, g % 3, :], probs1[0:TT, g % 3, :], rinv1[0:TT, g % 2:g % 2 + 1])\
                    .then_inc(scaled_ready, 1)

            def act_hi(g):
                for c in range(2):
                    act.wait_ge(p1_turned, 2 * (first + g) + c + 1)
                    src = bank(4 + c, 0, 3 * TT, 0, TT).rearrange("p (k q) -> p k q", q=TT)
                    act.copy(pT1[0:TT, g % 2, 3 * c:3 * c + 3, 0, :], src).then_inc(p1_hi, 1)

            for t in range(0, NT, 2):
                act_xT1(0, t)
            first = 0
            for c in range(2):
                act_k(0, c)
            for c in range(2):
                act_q(0, 0, c)
            act_v(0)
            act_exp1(0)
            act_exp1(1)
            act_scale(0)
            act_exp1(2)
            act_scale(1)
            act_hi(0)
            with act.Fori(0, B) as b:
                first = STEPS * b
                for s in range(1, STEPS + 1):
                    act_exp1(s + 2)
                    act_scale(s + 1)
                    act_hi(s)
                    if s in QUERY_AT:
                        p, c = QUERY_AT[s]
                        act_q(b, p, c)
                    if s in TURN_AT:
                        act_xT1(b + 1, TURN_AT[s])
                    if s in KEYS_AT:
                        act_k(b + 1, KEYS_AT[s])
                act.wait_ge(pv1_mm, STEPS * (b + 1))
                act_v(b + 1)

            act.wait_ge(h_lat, NT * (PAIRS * B + 1))
            act.wait_ge(w_picked, PAIRS * B + 1)
            act.copy(n_hi[:, :, 0:TT], ln_b[:, :].unsqueeze(2).to_broadcast([128, FB, TT])).then_inc(bias_split, 1)

            def act_x_hi(g):
                for k in range(KD):
                    act.wait_ge(fx_turned, KD * g + k + 1)
                    act.copy(x_hi[:, k, :], bank(k, 0, GT)).then_inc(x_hi_ready, 1)

            def act_gelu(g, p, t):
                s = 2 + 2 * ((3 * p + t) % 2)
                act.wait_ge(fc_mm, 3 * g + t + 1)
                act.activation(hidden[0:TT, p, t, :], bank(s, 0, FH, 0, TT), ACT.Gelu).then_inc(gelu_ready, 1)

            def act_norm(g, p):
                act.wait_ge(lnf_seq, LNF_CALL * (g + 1))
                for t in range(3):
                    act.activation(hidden[0:TT, p, t, :], hidden[0:TT, p, t, :], ACT.Identity,
                                   bias=nm_f[0:TT, t:t + 1], scale=yr_f[0:TT, t:t + 1]).then_inc(norm_ready, 1)

            def act_n_hi(g, f):
                act.wait_ge(n_turned, FB * g + f + 1)
                act.mul(n_hi[:, f, :], bank(f % 2, 0, GT), ln_w[:, f:f + 1]).then_inc(n_hi_ready, 1)

            def act_step(g, p, more=True):
                if more:
                    act_x_hi(g + 1)
                for f in range(FB):
                    act_n_hi(g, f)
                    if more and f in (2, 4, 6):
                        act_gelu(g + 1, 1 - p, (f - 2) // 2)
                if more:
                    act_norm(g + 1, 1 - p)

            act_x_hi(0)
            for t in range(3):
                act_gelu(0, 0, t)
            act_norm(0, 0)
            with act.Fori(0, NGR // 2 - 1) as i:
                for p in range(2):
                    act_step(2 * i + p, p)
            act_step(NGR - 2, 0)
            act_step(NGR - 1, 1, False)

        @block.tensor
        def _(pe):
            pe.wait_ge(wA_loaded, WA)
            pe.wait_ge(ident_made, 4)
            with pe.Fori(0, B) as b:
                pe.wait_ge(ew_step, 6 * b + 6)
                for t in range(NT):
                    pe.matmul(bank(t, 0, D, 0, TT), ewma[:, t * TT:(t + 1) * TT], w_tok[:, :],
                              start=True, stop=True).then_inc(tok_mm, 1)
                for t in range(NT):
                    pe.wait_ge(xn_ready, NT * b + t + 1)
                    for k in range(KD):
                        mm = pe.transpose(bank(t, k * TT, (k + 1) * TT), xn[0:TT, t, k * 128:(k + 1) * 128], ident[0:TT, 0:TT])
                    mm.then_inc(xn_turned, 1)
                pe.wait_ge(xT_ready, NT * b + NT)
                for j in range(8):
                    m, half, w = j // 2 % 2, j % 2, (wk0 if j // 4 else wq0)
                    for k in range(KD):
                        mm = pe.matmul(bank(j, 0, 375), w[:, k, m * 128:(m + 1) * 128],
                                       xT[:, k, half * 375:(half + 1) * 375], start=k == 0, stop=k == KD - 1)
                    mm.then_inc(qk_mm, 1)
                for t in range(NT):
                    pe.wait_ge(qk_ready, 8 * b + t + 1)
                    for k in range(KD):
                        mm = pe.matmul(bank(t, 0, D, 0, TT), xT[:, k, t * TT:(t + 1) * TT], wv0[:, k, :],
                                       start=k == 0, stop=k == KD - 1)
                    mm.then_inc(v_mm, 1)
                pe.wait_ge(qk_ready, 8 * b + 8)
                pe.wait_ge(v_ready, NT * b + NT)

                def scores(i):
                    n, s = (i + 1) * TT, 2 * (i % 2)
                    if i >= 2:
                        pe.wait_ge(probs_ready, NT * b + i - 1)
                    for lo in range(0, n, BANK):
                        hi = min(n, lo + BANK)
                        for k in range(KD):
                            mm = pe.matmul(bank(s, lo, hi, 0, TT), qT[:, k, i * TT:(i + 1) * TT], kT[:, k, lo:hi],
                                           start=k == 0, stop=k == KD - 1)
                    mm.then_inc(s_mm, 1)

                def turn_probs(i):
                    pe.wait_ge(probs_ready, NT * b + i + 1)
                    if i >= 1:
                        pe.wait_ge(pT_ready, NT * b + i)
                    for k in range(i + 1):
                        mm = pe.transpose(bank(4, k * 128, k * 128 + TT, 0, TT),
                                          probs[0:TT, i % 2, k * TT:(k + 1) * TT], ident[0:TT, 0:TT])
                    mm.then_inc(p_turned, 1)

                def weigh_values(i):
                    pe.wait_ge(pT_ready, NT * b + i + 1)
                    for k in range(i + 1):
                        mm = pe.matmul(bank(6, 0, D, 0, TT), pT[0:TT, i % 2, k, :], v0[0:TT, k, :],
                                       start=k == 0, stop=k == i)
                    mm.then_inc(pv_mm, 1)

                def turn_ctx(i):
                    pe.wait_ge(ctx_ready, NT * b + i + 1)
                    if i >= 1:
                        pe.wait_ge(h_attn, NT * b + i)
                    for k in range(KD):
                        mm = pe.transpose(bank(7, k * TT, (k + 1) * TT), ctxt[0:TT, k * 128:(k + 1) * 128],
                                          ident[0:TT, 0:TT])
                    mm.then_inc(ctx_turned, 1)

                def project(i):
                    pe.wait_ge(ctxT_ready, NT * b + i + 1)
                    for k in range(KD):
                        mm = pe.matmul(bank(7, D, 2 * D, 0, TT), ctxT[:, k, :], wo0[:, k, :],
                                       start=k == 0, stop=k == KD - 1)
                    mm.then_inc(wo_mm, 1)

                scores(0)
                for i in range(NT):
                    if i + 1 < NT:
                        scores(i + 1)
                    turn_probs(i)
                    if i >= 1:
                        turn_ctx(i - 1)
                    weigh_values(i)
                    if i >= 1:
                        project(i - 1)
                turn_ctx(NT - 1)
                project(NT - 1)

            MB = ISH // 128

            def gate_up(c, rows):
                for m in range(MB):
                    if m >= 3:
                        pe.wait_ge(act_s_ready, MB * c + m - 2)
                    for w, o in ((gate, 0), (up, 1)):
                        for k in range(KD):
                            mm = pe.matmul(bank(2 * (m % 3) + o, 0, HALF), w[:, k, m * 128:(m + 1) * 128],
                                           rows(k), start=k == 0, stop=k == KD - 1)
                    mm.then_inc(gu_mm, 1)

            def down_s(c, half):
                pe.wait_ge(act_s_ready, MB * c + MB)
                for t in range(3):
                    if t == 2:
                        pe.wait_ge(h_shared, 3 * c + 1)
                    for m in range(MB):
                        mm = pe.matmul(bank(6 + t % 2, 0, D, 0, TT),
                                       act_s[:, m, half * HALF + t * TT:half * HALF + (t + 1) * TT], down[:, m, :],
                                       start=m == 0, stop=m == MB - 1)
                    mm.then_inc(down_mm, 1)
                pe.wait_ge(h_shared, 3 * c + 3)

            pe.wait_ge(wM_loaded, 6 * 16)
            pe.wait_ge(h_attn, NG)
            with pe.Fori(0, B) as b:
                for t in range(NT):
                    pe.wait_ge(xn_ready, NT * b + NG + t + 1)
                    for k in range(KD):
                        mm = pe.transpose(bank(t, k * TT, (k + 1) * TT), xn[0:TT, t, k * 128:(k + 1) * 128],
                                          ident[0:TT, 0:TT])
                    mm.then_inc(xn_turned, 1)
                pe.wait_ge(xT_ready, NT * b + NG + NT)
                for t in range(NT):
                    for k in range(KD):
                        mm = pe.matmul(bank(6, t * E, (t + 1) * E, 0, TT), xT[:, k, t * TT:(t + 1) * TT],
                                       router[:, k, :], start=k == 0, stop=k == KD - 1)
                mm.then_inc(router_mm, 1)
                gate_up(b, lambda k: xT[:, k, 0:HALF])
                pe.wait_ge(logits_ready, b + 1)
                down_s(b, 0)

            pe.wait_ge(hots_ready, 1)
            pe.wait_ge(consts_m, 8)
            flat = hots[0:TT, :, :].rearrange("p t e -> p (t e)")
            pe.matmul(bank(6, 0, NG * E, 0, TT), before[0:TT, :], flat, start=True, stop=True)
            pe.matmul(bank(7, 0, NG * E, 0, TT), ones[0:TT, 0:TT], flat, start=True, stop=True).then_inc(rank_mm, 1)

            pe.wait_ge(rows_ready, 1)
            pe.wait_ge(x_late, B)
            with pe.Fori(0, B) as b:
                gate_up(b + B, lambda k: xT_late[:, k, bass.ds(b * HALF, HALF)])
                down_s(b + B, 1)

            def turn_x(j, p):
                pe.wait_ge(xg_loaded[p], 8 * (j - p) + 16)
                for k in range(KD):
                    mm = pe.transpose(bank(p, k * SLOT, (k + 1) * SLOT), xg[:, p, k * 128:(k + 1) * 128], ident[:, :])
                mm.then_inc(xg_turned, 1)

            def turn_u(j, p):
                pe.wait_ge(u_ready, j + 1)
                for k in range(KD):
                    mm = pe.transpose(bank(4 + p, k * SLOT, (k + 1) * SLOT), u[:, p, k * 128:(k + 1) * 128], ident[:, :])
                mm.then_inc(u_turned, 1)

            def first(j, p, e):
                pe.wait_ge(xgT_ready, j + 1)
                for k in range(KD):
                    mm = pe.matmul(bank(2 + p, 0, 2 * I), xgT[:, p, k, :], fc1[:, e, k, :],
                                   start=k == 0, stop=k == KD - 1)
                mm.then_inc(fc1_mm, 1)

            def second(j, p, e, wait=True):
                pe.wait_ge(uT_ready, j + 1)
                if wait:
                    pe.wait_ge(y_ready, j - 1)
                for k in range(KD):
                    mm = pe.matmul(bank(6 + p, 0, D), uT[:, p, k, :], fc2[:, e, k, :],
                                   start=k == 0, stop=k == KD - 1)
                mm.then_inc(fc2_mm, 1)

            def expert_of(j):
                return pe.value_load(slot_e[0:1, bass.ds(j, 1)], min_val=0, max_val=E - 1)

            pe.wait_ge(rows_ready, 2)
            turn_x(0, 0)
            first(0, 0, expert_of(0))
            turn_x(1, 1)
            turn_u(0, 0)
            first(1, 1, expert_of(1))
            turn_x(2, 0)
            second(0, 0, expert_of(0), False)
            turn_u(1, 1)
            first(2, 0, expert_of(2))
            turn_x(3, 1)
            second(1, 1, expert_of(1), False)
            turn_u(2, 0)
            first(3, 1, expert_of(3))
            with pe.Fori(2, NSLOT // 2) as i:
                for p in range(2):
                    j = 2 * i + p
                    e_second, e_first = expert_of(j - 2), expert_of(j)
                    turn_x(j, p)
                    second(j - 2, p, e_second)
                    turn_u(j - 1, 1 - p)
                    first(j, p, e_first)
            second(NSLOT - 2, 0, expert_of(NSLOT - 2))
            turn_u(NSLOT - 1, 1)
            second(NSLOT - 1, 1, expert_of(NSLOT - 1))
            pe.wait_ge(absum_ready, 2)
            pe.wait_ge(y_ready, NSLOT)
            pe.matmul(bank(7, 0, 2), ones[:, :], absum[:, :], start=True, stop=True).then_inc(gamma_mm, 1)
            pe.wait_ge(tern_step, 1)

            pe.wait_ge(wC_loaded, 7 * 16)
            pe.wait_ge(y_ready, NSLOT)
            for n in range(LH):
                for k in range(KD):
                    col = (n // 2 * KD + k) * 128 + n % 2 * LAT
                    pe.matmul(bank(0, col, col + LAT), wq1[0:HD, n, k * 128:(k + 1) * 128], wk_up[0:HD, n, :],
                              start=True, stop=True)
                mm = pe.matmul(bank(2 + n // 2, n % 2 * D, (n % 2 + 1) * D), wv_up[0:HD, n, :], wo1[0:HD, n, :],
                               start=True, stop=True)
            mm.then_inc(w_mm, 1)
            pe.wait_ge(w_folded, 6)

            def turn_x1(b, t):
                pe.wait_ge(xn_ready, NT * b + 2 * NG + NT + t + 2)
                for k in range(KD):
                    for i in range(2):
                        mm = pe.transpose(bank(7, (2 * k + i) * TT, (2 * k + i + 1) * TT),
                                          xn[0:TT, t + i, k * 128:(k + 1) * 128], ident[0:TT, 0:TT])
                mm.then_inc(xn_turned, 2)

            def keys(b, c):
                lo, hi = CUTS[c]
                for k in range(KD):
                    mm = pe.matmul(bank(7, 0, hi - lo), w_kv[:, k, :], xT[:, k, lo:hi], start=k == 0, stop=k == KD - 1)
                mm.then_inc(kv_mm, 1)

            def values():
                for t in range(NT):
                    for k in range(KD):
                        mm = pe.matmul(bank(7, t * LAT, (t + 1) * LAT, 0, TT), xT[:, k, t * TT:(t + 1) * TT],
                                       w_kv[:, k, 0:LAT], start=k == 0, stop=k == KD - 1)
                mm.then_inc(kv_mm, 1)

            def queries(b, p, c):
                lo, hi = CUTS[c]
                if c == 0:
                    pe.wait_ge(w_picked, PAIRS * b + p + 1)
                for k in range(KD):
                    mm = pe.matmul(bank(7, 0, hi - lo), w_qp[:, k, :], xT[:, k, lo:hi], start=k == 0, stop=k == KD - 1)
                mm.then_inc(q_mm, 1)

            def scores1(g, kv):
                p, n, t = g // HEAD_STEPS, g // NT % 2, g % NT
                q = q_st[:, 2 * (p % 2) + n, t * TT:(t + 1) * TT]
                if g >= 2:
                    pe.wait_ge(probs1_ready, first + g - 1)
                for kh in (k_hi, k_lo):
                    for lo, hi in BANKS:
                        mm = pe.matmul(bank(2 * (g % 2), lo, hi, 0, TT), q, kh[:, kv % 2, lo:hi],
                                       start=kh is k_hi, stop=kh is k_lo)
                mm.then_inc(s1_mm, 1)

            def turn_probs1(g):
                pe.wait_ge(scaled_ready, first + g + 1)
                for c in range(2):
                    if g:
                        pe.wait_ge(p1_ready, 2 * (first + g) - 1 + c)
                    for k in range(3):
                        mm = pe.transpose(bank(4 + c, k * TT, (k + 1) * TT, 0, TT),
                                          probs1[0:TT, g % 3, (3 * c + k) * TT:(3 * c + k + 1) * TT],
                                          ident[0:TT, 0:TT])
                    mm.then_inc(p1_turned, 1)

            def weigh1(g):
                pe.wait_ge(p1_ready, 2 * (first + g) + 2)
                pe.wait_ge(o_ready, first + g + 1)
                for k in range(NT):
                    mm = pe.matmul(bank(6, 0, 2 * TT), v_st[0:TT, k, :],
                                   pT1[0:TT, g % 2, k, :, :].rearrange("p a q -> p (a q)"),
                                   start=k == 0, stop=k == NT - 1)
                mm.then_inc(pv1_mm, 1)

            def project1(p, i, at=7):
                for n in range(2):
                    mm = pe.matmul(bank(at, 0, D, 0, TT), o_T[:, n, i * TT:(i + 1) * TT],
                                   w_vo[:, 2 * p + n, :], start=n == 0, stop=n == 1)
                mm.then_inc(out1_mm, 1)

            def bank7_free(b, s):
                made = max(x for x in (*PROJECT_AT, *QUERY_AT, *TURN_AT, *KEYS_AT, VALUES_AT, 0) if x < s)
                if made in PROJECT_AT:
                    p, i = PROJECT_AT[made]
                    pe.wait_ge(h_lat, NT * (PAIRS * b + p) + i + 1)
                elif made in QUERY_AT:
                    p, c = QUERY_AT[made]
                    pe.wait_ge(q_ready, 4 * (PAIRS * b + p) + 2 * c + 2)
                elif made in TURN_AT:
                    pe.wait_ge(xT_ready, NT * (b + 1) + 2 * NG + TURN_AT[made] + 2)
                elif made in KEYS_AT:
                    pe.wait_ge(kv_ready, 3 * (b + 1) + KEYS_AT[made] + 1)
                else:
                    pe.wait_ge(kv_ready, 3 * b + 3)

            pe.wait_ge(o_zeroed, 1)
            for t in range(0, NT, 2):
                if t:
                    pe.wait_ge(xT_ready, 2 * NG + t)
                turn_x1(0, t)
            pe.wait_ge(xT_ready, 2 * NG + NT)
            for c in range(2):
                if c:
                    pe.wait_ge(kv_ready, 1)
                keys(0, c)
            pe.wait_ge(kv_ready, 2)
            for c in range(2):
                if c:
                    pe.wait_ge(q_ready, 2)
                queries(0, 0, c)
            pe.wait_ge(q_ready, 4)
            values()
            first = 0
            for g in range(3):
                scores1(g, 0)
            turn_probs1(0)
            scores1(3, 0)
            with pe.Fori(0, B) as b:
                first = STEPS * b
                for s in range(1, STEPS + 1):
                    if s + 3 in range(HEAD_STEPS, STEPS + 1, HEAD_STEPS):
                        pe.wait_ge(q_ready, 4 * (PAIRS * b + (s + 3) // HEAD_STEPS + 1))
                    if s + 3 == STEPS:
                        pe.wait_ge(kv_ready, 3 * (b + 1) + 2)
                    scores1(s + 3, b if s + 3 < STEPS else b + 1)
                    turn_probs1(s)
                    if s in PROJECT_AT:
                        p, i = PROJECT_AT[s]
                        bank7_free(b, s)
                        project1((p - 1) % PAIRS, i)
                    if s in QUERY_AT:
                        bank7_free(b, s)
                        queries(b, *QUERY_AT[s])
                    if s in TURN_AT:
                        bank7_free(b, s)
                        turn_x1(b + 1, TURN_AT[s])
                    if s in KEYS_AT:
                        bank7_free(b, s)
                        pe.wait_ge(xT_ready, NT * (b + 1) + 2 * NG + NT)
                        keys(b + 1, KEYS_AT[s])
                    if s == VALUES_AT:
                        bank7_free(b, s)
                        values()
                    if s == 1:
                        pe.wait_ge(kv_ready, 3 * b + 3)
                    weigh1(s - 1)
            pe.wait_ge(kv_ready, 3 * B + 3)
            pe.wait_ge(o_ready, STEPS * B + 1)
            for i in range(NT):
                if i >= 2:
                    pe.wait_ge(h_lat, NT * PAIRS * B + i - 1)
                project1(PAIRS - 1, i, (7, 6)[i % 2])
            pe.wait_ge(h_lat, NT * (PAIRS * B + 1))
            pe.wait_ge(max1_ready, STEPS * B + 4)
            pe.wait_ge(p1_ready, 2 * (STEPS * B + 1))
            pe.wait_ge(scaled_ready, STEPS * B + 2)
            pe.wait_ge(rinv1_ready, STEPS * B + 3)
            pe.wait_ge(q_ready, 4 * (PAIRS * B + 1))

            pe.wait_ge(bias_split, 2)
            for f in range(FB):
                for half, nt in enumerate((n_hi, n_lo)):
                    mm = pe.matmul(bank(7, 0, D, 0, TT), nt[:, f, 0:TT], w_p[:, f, :],
                                   start=f == 0 and half == 0, stop=f == FB - 1 and half == 1)
            mm.then_inc(bias_mm, 1)

            def turn_x3(g):
                pe.wait_ge(fx_ready, 3 * g + 3)
                for k in range(KD):
                    for t in range(3):
                        mm = pe.transpose(bank(k, t * TT, (t + 1) * TT), xn[0:TT, t, k * 128:(k + 1) * 128],
                                          ident[0:TT, 0:TT])
                    mm.then_inc(fx_turned, 1)

            def fc(g, p, t, half, wait=True):
                s = 2 + 2 * ((3 * p + t) % 2) + half
                if half == 0:
                    pe.wait_ge(x_split, KD * g + KD)
                    if wait:
                        pe.wait_ge(gelu_ready, 3 * g + t - 1)
                for k in range(KD):
                    for part, xt in enumerate((x_hi, x_lo)):
                        mm = pe.matmul(bank(s, 0, BANK, 0, TT), xt[:, k, t * TT:(t + 1) * TT],
                                       w_f[:, k, half * BANK:(half + 1) * BANK],
                                       start=k == 0 and part == 0, stop=k == KD - 1 and part == 1)
                if half:
                    mm.then_inc(fc_mm, 1)

            def turn_n(g, p, f):
                if f == 0:
                    pe.wait_ge(norm_ready, 3 * g + 3)
                if f >= 2:
                    pe.wait_ge(n_split, FB * g + f - 1)
                for t in range(3):
                    mm = pe.transpose(bank(f % 2, t * TT, (t + 1) * TT), hidden[0:TT, p, t, f * 128:(f + 1) * 128],
                                      ident[0:TT, 0:TT])
                mm.then_inc(n_turned, 1)

            def proj(g, t, first=False):
                pe.wait_ge(n_split, FB * g + FB)
                if not first or t == 2:
                    pe.wait_ge(h_out, 3 * g + t - 1)
                for f in range(FB):
                    for half, nt in enumerate((n_hi, n_lo)):
                        mm = pe.matmul(bank(6 + t % 2, 0, D, 0, TT), nt[:, f, t * TT:(t + 1) * TT], w_p[:, f, :],
                                       start=f == 0 and half == 0, stop=f == FB - 1 and half == 1)
                mm.then_inc(proj_mm, 1)

            def step3(g, p, more=True, first=False):
                if more:
                    turn_x3(g + 1)
                    pe.wait_ge(x_split, KD * g + 2 * KD)
                for f in range(FB):
                    turn_n(g, p, f)
                    if more and f in (1, 3, 5):
                        fc(g + 1, 1 - p, f // 2, 0)
                    if more and f in (2, 4, 6):
                        fc(g + 1, 1 - p, f // 2 - 1, 1)
                for t in range(3):
                    proj(g, t, first)

            turn_x3(0)
            pe.wait_ge(b_out_ready, 1)
            for t in range(3):
                for half in range(2):
                    fc(0, 0, t, half, t == 2)
            step3(0, 0, True, True)
            step3(1, 1)
            with pe.Fori(1, NGR // 2 - 1) as i:
                for p in range(2):
                    step3(2 * i + p, p)
            step3(NGR - 2, 0)
            step3(NGR - 1, 1, False)


def layout(x, L0_tok_W, L0_tok_b, L0_attn_Wq, L0_attn_bq, L0_attn_Wk, L0_attn_bk, L0_attn_Wv, L0_attn_bv, L0_attn_Wo,
           L0_attn_bo, L0_ffn_w_router, L0_ffn_fc1_w, L0_ffn_fc2_w, L0_ffn_gate_w, L0_ffn_up_w, L0_ffn_down_w,
           L1_attn_Wq, L1_attn_Wkv_down, L1_attn_Wk_up, L1_attn_Wv_up, L1_attn_Wo, L1_ffn_W_fc, L1_ffn_ln_w,
           L1_ffn_ln_b, L1_ffn_W_proj):
    kp = lambda w: np.moveaxis(np.asarray(w).reshape(*w.shape[:-2], -1, 128, w.shape[-1]), -2, 0)
    cols = lambda v: np.asarray(v).reshape(-1, 128).T
    heads = lambda w: np.asarray(w).reshape(LH, HD, -1).transpose(1, 0, 2)
    arrays = dict(
        x=x, tok_wT=np.asarray(L0_tok_W).T, tok_b=L0_tok_b, wq0=kp(L0_attn_Wq), wk0=kp(L0_attn_Wk), wv0=kp(L0_attn_Wv),
        wo0=kp(L0_attn_Wo), bq0=cols(L0_attn_bq), bk0=cols(L0_attn_bk), bv0=L0_attn_bv, bo0=L0_attn_bo,
        router=kp(L0_ffn_w_router), fc1=kp(L0_ffn_fc1_w), fc2=kp(L0_ffn_fc2_w), gate=kp(L0_ffn_gate_w), up=kp(L0_ffn_up_w),
        down=kp(L0_ffn_down_w), wq1=heads(L1_attn_Wq), wkvdT=kp(np.asarray(L1_attn_Wkv_down).T), wk_up=heads(L1_attn_Wk_up),
        wv_up=heads(L1_attn_Wv_up), wo1=heads(np.asarray(L1_attn_Wo).T), wfcT=kp(np.asarray(L1_ffn_W_fc).T),
        ln_w=cols(L1_ffn_ln_w), ln_b=cols(L1_ffn_ln_b), wprojT=kp(np.asarray(L1_ffn_W_proj).T))
    return {n: np.ascontiguousarray(v) for n, v in arrays.items()}


def kernel(**inputs):
    import concourse.bacc as bacc
    from concourse.bass_utils import run_bass_kernel_spmd

    nc = bacc.Bacc("TRN2", target_bir_lowering=False, num_devices=1)
    arrays = layout(**inputs)
    a = {n: nc.dram_tensor(f"in_{n}", v.shape, mybir.dt.from_np(v.dtype), kind="ExternalInput").ap()
         for n, v in arrays.items()}
    out = nc.dram_tensor("out", (B, T, D), F32, kind="ExternalOutput").ap()
    build(nc, a, out)
    r = run_bass_kernel_spmd(nc, [{f"in_{n}": v for n, v in arrays.items()}], core_ids=[0])
    return r.results[0]["out"]
```

```python
from contextlib import ExitStack

import numpy as np
import concourse.bass as bass
from concourse import mybir

F32 = mybir.dt.float32
F32R = mybir.dt.float32r
I32 = mybir.dt.int32
U32 = mybir.dt.uint32
ALU = mybir.AluOpType
ACT = mybir.ActivationFunctionType
AX = mybir.AxisListType

B, C, T, D = 4, 128, 750, 256
TT = 125
NT = T // TT
NG = B * NT
KD = D // 128
E, I, ISH = 8, 256, 512
SLOT = 128
NSLOT = (2 * B * T - E) // SLOT + E
LH, HD, LAT = 8, 64, 64
PAIRS = LH // 2
FH = 1024
FB = FH // 128
BANK = 512
HALF = T // 2
GT = 3 * TT
NGR = NG // 3
GAMMA_EPS = 1e-6
HEAD_STEPS = 2 * NT
STEPS = PAIRS * HEAD_STEPS
ALPHA = 0.1
LN_EPS = 1e-5
MASKED = -1.0e30
RSQRT_SEED = 0x5F3759DF
NEWTON = 3
LN_CHAIN = 3 + 3 * NEWTON


def build(nc, a, out):
    with ExitStack() as ctx:
        def sb(name, shape, dt=F32):
            return ctx.enter_context(nc.sbuf_tensor(name, shape, dt))

        def sem(name):
            return ctx.enter_context(nc.semaphore(name))

        ARENA = 60 * 1024
        early_at = (nc.sbuf_base + 31) // 32 * 32
        sb("early", [128, ARENA // 4])
        late_at = (nc.sbuf_base + 31) // 32 * 32
        sb("late", [128, ARENA // 4])

        def lay(start, *tensors):
            handles = []
            for name, shape, dt in tensors:
                handles.append(nc.alloc_sbuf_tensor_at(name, [128, *shape], dt, offset=start))
                start += (4 * int(np.prod(shape)) + 31) // 32 * 32
            return handles + [start]

        h = sb("h", [128, NG + NT, D])
        ident = sb("ident", [128, 128])
        xn = sb("xn", [128, NT, D])
        xT = sb("xT", [128, KD, T])
        probs = sb("probs", [128, 2, T])
        (w_tok, b_tok, bv0, bo0, wq0, wk0, wv0, wo0, x_in, x_scaled, fwd, bwd, ewma, qT, kT, v0, pT, end) = lay(
            early_at, ("w_tok", [D], F32), ("b_tok", [D], F32), ("bv0", [D], F32), ("bo0", [D], F32),
            ("wq0", [KD, D], F32), ("wk0", [KD, D], F32), ("wv0", [KD, D], F32), ("wo0", [KD, D], F32),
            ("x_in", [B, T], F32), ("x_scaled", [T], F32), ("fwd", [T], F32), ("bwd", [T], F32), ("ewma", [T], F32),
            ("qT", [KD, T], F32), ("kT", [KD, T], F32), ("v0", [NT, D], F32), ("pT", [2, NT, TT], F32))
        assert end <= early_at + ARENA
        ctxt = sb("ctxt", [128, D])
        ctxT = sb("ctxT", [128, KD, TT])
        decay = sb("decay", [128, 1])
        bq0 = sb("bq0", [128, KD])
        bq0s = sb("bq0s", [128, KD])
        bk0 = sb("bk0", [128, KD])
        mask = sb("mask", [128, TT])
        fc1, fc2, gate, up, down, end = lay(
            late_at, ("fc1", [E, KD, 2 * I], F32), ("fc2", [E, KD, D], F32), ("gate", [KD, ISH], F32),
            ("up", [KD, ISH], F32), ("down", [ISH // 128, D], F32))
        assert end <= late_at + ARENA
        act_s, x_all, after_rows = lay(early_at, ("act_s", [ISH // 128, 2 * HALF], F32), ("x_all", [NG, D], F32))
        xT_late, end = lay(after_rows, ("xT_late", [KD, B * HALF], F32))
        assert end <= early_at + ARENA
        xg, xgT, silu, u, uT, y_out, ring_at = lay(
            after_rows, ("xg", [2, D], F32), ("xgT", [2, KD, SLOT], F32), ("silu", [2, I], F32), ("u", [2, I], F32),
            ("uT", [2, KD, SLOT], F32), ("y_out", [2, D], F32))
        ring, end = lay(ring_at, ("ring", [NT, 2, D], F32))
        wq1, wk_up, wv_up, wo1, end = lay(
            early_at + 4 * 2 * HALF * ISH // 128, ("wq1", [LH, D], F32), ("wk_up", [LH, LAT], F32),
            ("wv_up", [LH, 2 * LAT], F32), ("wo1", [LH, D], F32))
        assert end <= after_rows
        o_T, probs1, end = lay(early_at, ("o_T", [2, T], F32), ("probs1", [3, T], F32))
        assert end <= after_rows
        q_st, k_hi, k_lo, v_st, pT1, w_qk, w_vo, w_kv, w_qp, end = lay(
            late_at, ("q_st", [4, T], F32R), ("k_hi", [2, T], F32R), ("k_lo", [2, T], F32R),
            ("v_st", [NT, 2 * LAT], F32R), ("pT1", [2, NT, 2, TT], F32R),
            ("w_qk", [PAIRS, KD, 128], F32), ("w_vo", [LH, D], F32), ("w_kv", [KD, 2 * LAT], F32),
            ("w_qp", [KD, 128], F32))
        assert end <= late_at + ARENA
        wf_at = (nc.sbuf_base + 31) // 32 * 32
        sb("ternary_room", [128, KD * FH + FB * D])
        wf_raw, wp_raw, end = lay(wf_at, ("wf_raw", [KD * FH], F32), ("wp_raw", [FB * D], F32))
        w_f, w_p, end = lay(wf_at, ("w_f", [KD, FH], F32R), ("w_p", [FB, D], F32R))
        x_hi, x_lo, n_hi, n_lo, end = lay(
            late_at, ("x_hi", [KD, GT], F32R), ("x_lo", [KD, GT], F32R), ("n_hi", [FB, GT], F32R),
            ("n_lo", [FB, GT], F32R))
        assert end <= late_at + ARENA
        hidden, end = lay(early_at, ("hidden", [2, 3, FH], F32))
        ln_w = sb("ln_w", [128, FB])
        ln_b = sb("ln_b", [128, FB])
        b_out = sb("b_out", [128, D])
        absum = sb("absum", [128, 2])
        above = sb("above", [128, 2])
        below = sb("below", [128, 2])
        bn_f = sb("bn_f", [128, 3, 2, 6])
        mv_f = sb("mv_f", [128, 3, 2])
        ve_f = sb("ve_f", [128, 3])
        yr_f = sb("yr_f", [128, 3])
        yt_f = sb("yt_f", [128, 3])
        nm_f = sb("nm_f", [128, 3])
        silu_s = sb("silu_s", [128, 2, HALF])
        router = sb("router", [128, KD, E])
        logits = sb("logits", [128, NT, E])
        top = sb("top", [128, NT, 8])
        top_i = sb("top_i", [128, NT, 8], U32)
        top_f = sb("top_f", [128, NT, 2])
        gap = sb("gap", [128, 2, NG])
        share = sb("share", [128, 2, NG])
        hot = sb("hot", [128, 2, NG, E])
        hots = sb("hots", [128, NG, E])
        iota_e = sb("iota_e", [128, E])
        iota_j = sb("iota_j", [128, NSLOT])
        iota_c = sb("iota_c", [128, NG])
        before = sb("before", [128, TT])
        ones = sb("ones", [128, 128])
        restart = sb("restart", [128, E, NG])
        tot = sb("tot", [128, E, NG])
        incl = sb("incl", [128, E, NG])
        base = sb("base", [128, E, NG])
        over = sb("over", [128, E, NG])
        n_slots = sb("n_slots", [128, E])
        slot_end = sb("slot_end", [128, E])
        slot_beg = sb("slot_beg", [128, E])
        place = sb("place", [128, NG, E])
        picked = sb("picked", [128, 2, NG, E])
        row_f = sb("row_f", [128, 2, NG])
        row = sb("row", [128, 2, NG], I32)
        ended = sb("ended", [1, NSLOT, E])
        slot_e_f = sb("slot_e_f", [1, NSLOT])
        slot_e = sb("slot_e", [1, NSLOT], I32)
        zeros = sb("zeros", [128, D])
        bn6 = sb("bn6", [128, NT, 6])
        mv = sb("mv", [128, NT, 2])
        ve = sb("ve", [128, NT])
        yr = sb("yr", [128, NT])
        yt = sb("yt", [128, NT])
        negmax = sb("negmax", [128, 2])
        rowsum = sb("rowsum", [128, 2])
        rinv = sb("rinv", [128, 4])
        rinv1 = sb("rinv1", [128, 2])

        xs_dram = nc.dram_tensor("xs_dram", [NSLOT * SLOT, D], F32, kind="Internal").ap()
        ys_dram = nc.dram_tensor("ys_dram", [NSLOT * SLOT, D], F32, kind="Internal").ap()

        PS = ctx.enter_context(nc.psum_tensor("PS", [128, 8 * BANK], F32))

        def bank(i, lo=0, hi=BANK, p0=0, p1=128):
            return PS[p0:p1, i * BANK + lo:i * BANK + hi]

        x_loaded, wA_loaded = sem("x_loaded"), sem("wA_loaded")
        const_made, ident_made = sem("const_made"), sem("ident_made")
        ew_step, tok_mm, h_tok = sem("ew_step"), sem("tok_mm"), sem("h_tok")
        ln_seq, xn_ready, xn_turned, xT_ready = sem("ln_seq"), sem("xn_ready"), sem("xn_turned"), sem("xT_ready")
        qk_mm, qk_ready, v_mm, v_ready = sem("qk_mm"), sem("qk_ready"), sem("v_mm"), sem("v_ready")
        s_mm, s_masked, max_ready, probs_ready = sem("s_mm"), sem("s_masked"), sem("max_ready"), sem("probs_ready")
        p_turned, pT_ready, pv_mm, rinv_ready = sem("p_turned"), sem("pT_ready"), sem("pv_mm"), sem("rinv_ready")
        ctx_ready, ctx_turned, ctxT_ready, wo_mm = sem("ctx_ready"), sem("ctx_turned"), sem("ctxT_ready"), sem("wo_mm")
        h_biased, h_attn = sem("h_biased"), sem("h_attn")
        stored = sem("stored")
        wM_loaded, zeroed = sem("wM_loaded"), sem("zeroed")
        x_kept, router_mm, logits_ready, routed, share_exp = (sem("x_kept"), sem("router_mm"), sem("logits_ready"),
                                                              sem("routed"), sem("share_exp"))
        x_late = sem("x_late")
        gap_ready, hots_ready, rank_mm, rows_step, rows_ready = (sem("gap_ready"), sem("hots_ready"), sem("rank_mm"),
                                                                 sem("rows_step"), sem("rows_ready"))
        consts_m = sem("consts_m")
        scattered = sem("scattered")
        gu_mm, silu_s_ready, act_s_ready, down_mm, h_shared = (sem("gu_mm"), sem("silu_s_ready"), sem("act_s_ready"),
                                                               sem("down_mm"), sem("h_shared"))
        xg_loaded = [sem("xg_loaded0"), sem("xg_loaded1")]
        y_stored = [sem("y_stored0"), sem("y_stored1")]
        xg_turned, xgT_ready, fc1_mm, silu_ready, u_ready = (sem("xg_turned"), sem("xgT_ready"), sem("fc1_mm"),
                                                             sem("silu_ready"), sem("u_ready"))
        u_turned, uT_ready, fc2_mm, y_ready = sem("u_turned"), sem("uT_ready"), sem("fc2_mm"), sem("y_ready")
        gathered = [sem(f"gathered{i}") for i in range(NT)]
        h_moe, rows_scaled = sem("h_moe"), sem("rows_scaled")
        wF_loaded, absum_ready, gamma_mm, tern_step = sem("wF_loaded"), sem("absum_ready"), sem("gamma_mm"), sem("tern_step")
        bias_split, bias_mm, b_out_ready, h_biased2 = sem("bias_split"), sem("bias_mm"), sem("b_out_ready"), sem("h_biased2")
        lnx_seq, fx_ready, fx_turned, x_hi_ready, x_split = (sem("lnx_seq"), sem("fx_ready"), sem("fx_turned"),
                                                             sem("x_hi_ready"), sem("x_split"))
        fc_mm, gelu_ready, lnf_seq, norm_ready = sem("fc_mm"), sem("gelu_ready"), sem("lnf_seq"), sem("norm_ready")
        n_turned, n_hi_ready, n_split, proj_mm, h_out = (sem("n_turned"), sem("n_hi_ready"), sem("n_split"),
                                                         sem("proj_mm"), sem("h_out"))
        wC_loaded, w_mm, w_folded, w_picked = sem("wC_loaded"), sem("w_mm"), sem("w_folded"), sem("w_picked")
        kv_mm, kv_hi, kv_ready = sem("kv_mm"), sem("kv_hi"), sem("kv_ready")
        q_mm, q_hi, q_ready = sem("q_mm"), sem("q_hi"), sem("q_ready")
        s1_mm, max1_ready, probs1_ready = sem("s1_mm"), sem("max1_ready"), sem("probs1_ready")
        p1_turned, p1_hi, p1_ready, pv1_mm = sem("p1_turned"), sem("p1_hi"), sem("p1_ready"), sem("pv1_mm")
        rinv1_ready, scaled_ready, o_ready = sem("rinv1_ready"), sem("scaled_ready"), sem("o_ready")
        out1_mm, h_lat, o_zeroed = sem("out1_mm"), sem("h_lat"), sem("o_zeroed")

        START_TURN, START_KEYS, START_QUERIES = (0, 1, 2), (3, 4), (5, 6)
        C_TURNED = 2 * NG + NT
        PROJECT_AT = {HEAD_STEPS * p + i + 1: (p, i) for p in range(PAIRS) for i in range(NT)}
        QUERY_AT = {7: (1, 0), 8: (1, 1), 11: (2, 0), 12: (2, 1), 21: (3, 0), 23: (3, 1), 36: (4, 0), 43: (4, 1)}
        TURN_AT = {31: 0, 32: 2, 33: 4}
        KEYS_AT = {34: 0, 35: 1}
        VALUES_AT = 44
        STATS_AT, CHAIN_AT, NORM_AT = (10, 11, 19), range(21, 21 + LN_CHAIN // 2), (27, 28, 29)
        CUTS = ((0, HALF), (HALF, T))
        BANKS = ((0, BANK), (BANK, T))

        passed = {"dve": sem("dve_passed"), "pool": sem("pool_passed")}
        passes = {"dve": 0, "pool": 0}

        def wait_apart(eng, name, s, value, times):
            eng.wait_ge(s, value)
            eng.sem_inc(passed[name], 1)
            passes[name] += times

        def rsqrt(dve, var, y, e, t, seq, at, steps=None):
            for k in range(LN_CHAIN) if steps is None else steps:
                if k and steps is None:
                    dve.wait_ge(seq, at + k)
                if k == 0:
                    op = dve.tensor_scalar(e, var, LN_EPS, None, ALU.add)
                elif k == 1:
                    op = dve.tensor_scalar(y.bitcast(I32), e.bitcast(I32), 1, None, ALU.logical_shift_right)
                elif k == 2:
                    op = dve.tensor_scalar(y.bitcast(I32), y.bitcast(I32), -1.0, float(RSQRT_SEED), ALU.mult, ALU.add)
                elif k % 3 == 0:
                    op = dve.scalar_tensor_tensor(t, y, 0.5, y, ALU.mult, ALU.mult)
                elif k % 3 == 1:
                    op = dve.tensor_tensor(t, t, e, ALU.mult)
                else:
                    op = dve.scalar_tensor_tensor(y, t, 1.5, y, ALU.subtract, ALU.mult, reverse0=True)
                op.then_inc(seq, 1)

        LN_CALL = 2 * NT + LN_CHAIN
        R_CALL = 2 * NT + 3
        LNX_CALL = 6 + LN_CHAIN
        LNF_CALL = 9 + LN_CHAIN + 1

        def layernorm(dve, g0, at, times, n=NT, seq=ln_seq, ready=xn_ready):
            for t in range(n):
                dve.bn_stats(bn6[0:TT, t, :], h[0:TT, g0 + t, :]).then_inc(seq, 1)
            wait_apart(dve, "dve", seq, at + n, times)
            for t in range(n):
                dve.bn_aggr(mv[0:TT, t, :], bn6[0:TT, t, :]).then_inc(seq, 1)
            dve.wait_ge(seq, at + 2 * n)
            rsqrt(dve, mv[0:TT, 0:n, 1], yr[0:TT, 0:n], ve[0:TT, 0:n], yt[0:TT, 0:n], seq, at + 2 * n)
            dve.wait_ge(seq, at + 2 * n + LN_CHAIN)
            for t in range(n):
                dve.tensor_scalar(xn[0:TT, t, :], h[0:TT, g0 + t, :], mv[0:TT, t, 0:1], yr[0:TT, t:t + 1],
                                  ALU.subtract, ALU.mult).then_inc(ready, 1)

        block = ctx.enter_context(nc.Block())

        @block.sync
        def _(sp):
            sp.dma_start(x_in[:, :, :], a["x"].rearrange("b c t -> c b t")).then_inc(x_loaded, 16)
            sp.dma_start(w_tok[:, :], a["tok_wT"]).then_inc(wA_loaded, 16)
            sp.dma_start(b_tok[0:TT, :], a["tok_b"].partition_broadcast(TT)).then_inc(wA_loaded, 16)
            for w, n in ((wq0, "wq0"), (wk0, "wk0"), (wv0, "wv0"), (wo0, "wo0")):
                sp.dma_start(w[:, :, :], a[n]).then_inc(wA_loaded, 16)
            sp.dma_start(bq0[:, :], a["bq0"]).then_inc(wA_loaded, 16)
            sp.dma_start(bk0[:, :], a["bk0"]).then_inc(wA_loaded, 16)
            sp.dma_start(bv0[0:TT, :], a["bv0"].partition_broadcast(TT)).then_inc(wA_loaded, 16)
            sp.dma_start(bo0[0:TT, :], a["bo0"].partition_broadcast(TT)).then_inc(wA_loaded, 16)
            sp.dma_start(router[:, :, :], a["router"]).then_inc(wM_loaded, 16)
            for w, n in ((gate, "gate"), (up, "up"), (down, "down")):
                sp.dma_start(w[:, :, :], a[n]).then_inc(wM_loaded, 16)
            sp.dma_start(fc1[:, :, :, :], a["fc1"]).then_inc(wM_loaded, 16)
            sp.dma_start(fc2[:, :, :, :], a["fc2"]).then_inc(wM_loaded, 16)
            sp.dma_start(wf_raw[:, :], a["wfcT"].rearrange("p k n -> p (k n)")).then_inc(wF_loaded, 16)
            sp.dma_start(wp_raw[:, :], a["wprojT"].rearrange("p k n -> p (k n)")).then_inc(wF_loaded, 16)
            sp.dma_start(ln_w[:, :], a["ln_w"]).then_inc(wF_loaded, 16)
            sp.dma_start(ln_b[:, :], a["ln_b"]).then_inc(wF_loaded, 16)
            sp.wait_ge(consts_m, 8)
            for j in range(NSLOT):
                sp.dma_start(xs_dram[j * SLOT:(j + 1) * SLOT, :], zeros[:, :]).then_inc(zeroed, 16)

            def load(j, p):
                sp.dma_start(xg[:, p, :], xs_dram[bass.ds(j * SLOT, SLOT), :]).then_inc(xg_loaded[p], 16)

            sp.wait_ge(scattered, 16 * 2 * NG)
            sp.wait_ge(down_mm, NG)
            for w, n in ((wq1, "wq1"), (wk_up, "wk_up"), (wo1, "wo1")):
                sp.dma_start(w[0:HD, :, :], a[n]).then_inc(wC_loaded, 16)
            for o in range(2):
                sp.dma_start(wv_up[0:HD, :, o * LAT:(o + 1) * LAT], a["wv_up"]).then_inc(wC_loaded, 16)
            for j in range(2):
                load(j, j)
            with sp.Fori(1, NSLOT // 2) as i:
                for p in range(2):
                    sp.wait_ge(xg_turned, 2 * i + p - 1)
                    load(2 * i + p, p)
            sp.wait_ge(fc2_mm, NSLOT)
            for o in range(2):
                sp.dma_start(w_kv[:, :, o * LAT:(o + 1) * LAT], a["wkvdT"]).then_inc(wC_loaded, 16)
            with sp.Fori(0, NGR) as g:
                sp.wait_ge(h_out, 3 * g + 3)
                sp.dma_start(out.rearrange("b (t p) d -> p (b t) d", p=TT)[:, bass.ds(3 * g, 3), :],
                             h[0:TT, bass.ds(3 * g, 3), :]).then_inc(stored, 16)
            sp.wait_ge(stored, 16 * NGR)

        WA = 10 * 16

        @block.gpsimd
        def _(pool):
            pool.memset(ident[:, :], 0.0).then_inc(ident_made, 1)
            pool.memset(mask[:, :], 0.0).then_inc(ident_made, 1)
            pool.wait_ge(ident_made, 2)
            pool.affine_select(out=ident[:, :], in_=ident[:, :], compare_op=ALU.not_equal, fill=1.0, base=0,
                               pattern=[[-1, 128]], channel_multiplier=1).then_inc(ident_made, 1)
            pool.affine_select(out=mask[:, :], in_=mask[:, :], compare_op=ALU.is_ge, fill=MASKED, base=0,
                               pattern=[[-1, TT]], channel_multiplier=1).then_inc(ident_made, 1)
            pool.memset(zeros[:, :], 0.0).then_inc(consts_m, 1)
            pool.memset(ones[:, :], 1.0).then_inc(consts_m, 1)
            pool.memset(restart[:, :, :], 1.0).then_inc(consts_m, 1)
            pool.iota(iota_e[:, :], pattern=[[1, E]], base=0, channel_multiplier=0,
                      allow_small_or_imprecise_dtypes=True).then_inc(consts_m, 1)
            pool.iota(iota_j[:, :], pattern=[[1, NSLOT]], base=0, channel_multiplier=0,
                      allow_small_or_imprecise_dtypes=True).then_inc(consts_m, 1)
            pool.iota(iota_c[:, :], pattern=[[SLOT, NG]], base=0, channel_multiplier=0,
                      allow_small_or_imprecise_dtypes=True).then_inc(consts_m, 1)
            pool.wait_ge(consts_m, 6)
            pool.memset(restart[:, :, 0:1], 0.0).then_inc(consts_m, 1)
            pool.affine_select(out=before[:, :], in_=ones[:, 0:TT], compare_op=ALU.is_gt, fill=0.0, base=0,
                               pattern=[[1, TT]], channel_multiplier=-1).then_inc(consts_m, 1)
            pool.wait_ge(wA_loaded, WA)
            with pool.Fori(0, B) as b:
                for t in range(NT):
                    pool.wait_ge(xn_ready, NT * b + t + 1)
                    pool.tensor_tensor(h[0:TT, b * NT + t, :], h[0:TT, b * NT + t, :], bo0[0:TT, :], ALU.add)\
                        .then_inc(h_biased, 1)

            with pool.Fori(0, B) as b:
                for t in range(NT):
                    wait_apart(pool, "pool", xn_ready, NT * (b + 1) + NG + t + 1, B)
                    pool.tensor_copy(x_all[0:TT, b * NT + t, :], xn[0:TT, t, :]).then_inc(x_kept, 1)
            pool.wait_ge(rows_ready, 2)
            pool.wait_ge(x_kept, NG)
            pool.wait_ge(zeroed, 16 * NSLOT)
            for t in range(NG):
                for c in range(2):
                    pool.indirect_dma_start(
                        out=xs_dram[:, :], out_offset=bass.IndirectOffsetOnAxis(ap=row[0:TT, c, t:t + 1], axis=0),
                        in_=x_all[0:TT, t, :], in_offset=None).then_inc(scattered, 16)
            for p in range(2):
                pool.wait_ge(y_stored[p], 16 * (NSLOT // 2))

            def gather(b):
                for i in range(NT):
                    t = b * NT + i
                    if b:
                        pool.wait_ge(h_moe, 2 * (t - NT + 1))
                    for c in range(2):
                        pool.indirect_dma_start(
                            out=ring[0:TT, i, c, :], out_offset=None, in_=ys_dram[:, :],
                            in_offset=bass.IndirectOffsetOnAxis(ap=row[0:TT, c, t:t + 1], axis=0))\
                            .then_inc(gathered[i], 16)

            gather(0)
            pool.wait_ge(w_folded, 6)
            pool.tensor_copy(w_qp[:, :, :], w_qk[:, 0, :, :]).then_inc(w_picked, 1)
            gather(1)

            def pick(b, n):
                pool.wait_ge(q_mm, 2 * (PAIRS * b + n + 1))
                pool.tensor_copy(w_qp[:, :, :], w_qk[:, (n + 1) % PAIRS, :, :]).then_inc(w_picked, 1)

            def combine(b, i):
                t = b * NT + i
                pool.wait_ge(gathered[i], 32 * (b + 1))
                pool.tensor_tensor(ring[0:TT, i, :, :], ring[0:TT, i, :, :],
                                   share[0:TT, :, t:t + 1].to_broadcast([TT, 2, D]), ALU.mult).then_inc(rows_scaled, 1)
                pool.wait_ge(rows_scaled, t - NT + 1)
                for c in range(2):
                    if c:
                        pool.wait_ge(h_moe, 2 * t + 1)
                    pool.tensor_tensor(h[0:TT, t, :], ring[0:TT, i, c, :], h[0:TT, t, :], ALU.add).then_inc(h_moe, 1)

            for b in range(B):
                pick(b, 0)
                if b + 1 < B:
                    for i in range(NT):
                        combine(b + 1, i)
                pick(b, 1)
                pick(b, 2)
                if b + 2 < B:
                    gather(b + 2)
                pick(b, PAIRS - 1)
            pool.wait_ge(b_out_ready, 1)
            with pool.Fori(0, NG) as t:
                pool.wait_ge(fx_ready, t + 1)
                pool.tensor_tensor(h[0:TT, t, :], h[0:TT, t, :], b_out[0:TT, :], ALU.add).then_inc(h_biased2, 1)
            pool.wait_ge(passed["pool"], passes["pool"])

        @block.vector
        def _(dve):
            dve.memset(decay[:, :], 1.0 - ALPHA).then_inc(const_made, 1)
            dve.wait_ge(wA_loaded, WA)
            dve.tensor_scalar(bq0s[:, :], bq0[:, :], 1.0 / 16, None, ALU.mult).then_inc(const_made, 1)
            dve.wait_ge(const_made, 2)
            dve.wait_ge(x_loaded, 16)
            dve.wait_ge(ident_made, 4)

            def averages(b):
                ew, at = 6 * b, b % B
                dve.tensor_scalar(x_scaled[:, :], x_in[:, at, :], ALPHA / 2, None, ALU.mult).then_inc(ew_step, 1)
                dve.tensor_scalar(fwd[:, 0:1], x_in[:, at, 0:1], 0.5, None, ALU.mult).then_inc(ew_step, 1)
                dve.tensor_scalar(bwd[:, T - 1:T], x_in[:, at, T - 1:T], 0.5, None, ALU.mult).then_inc(ew_step, 1)
                dve.wait_ge(ew_step, ew + 3)
                dve.tensor_tensor_scan(fwd[:, 1:T], decay[:, 0:1].to_broadcast([128, T - 1]), x_scaled[:, 1:T],
                                       fwd[:, 0:1], ALU.mult, ALU.add).then_inc(ew_step, 1)
                dve.tensor_tensor_scan(bwd[:, T - 2::-1], decay[:, 0:1].to_broadcast([128, T - 1]),
                                       x_scaled[:, T - 2::-1], bwd[:, T - 1:T], ALU.mult, ALU.add).then_inc(ew_step, 1)
                dve.wait_ge(ew_step, ew + 5)
                dve.tensor_tensor(ewma[:, :], fwd[:, :], bwd[:, :], ALU.add).then_inc(ew_step, 1)

            def dve_tok(b, t, at):
                dve.wait_ge(tok_mm, NT * b + t + 1)
                dve.tensor_tensor(h[0:TT, b * NT + t, :], bank(at, 0, D, 0, TT), b_tok[0:TT, :], ALU.add)\
                    .then_inc(h_tok, 1)

            averages(0)
            for t in range(NT):
                dve_tok(0, t, t)
            wait_apart(dve, "dve", h_tok, NT, 1)
            layernorm(dve, 0, 0, 1)
            with dve.Fori(0, B) as b:
                averages(b + 1)
                for t in range(NT):
                    dve.wait_ge(v_mm, NT * b + t + 1)
                    dve.tensor_tensor(v0[0:TT, t, :], bank(t, 0, D, 0, TT), bv0[0:TT, :], ALU.add).then_inc(v_ready, 1)

                def dve_scores(i):
                    n, s = (i + 1) * TT, 2 * (i % 2)
                    diag = bank(s, i * TT, n, 0, TT)
                    dve.wait_ge(s_mm, NT * b + i + 1)
                    dve.tensor_tensor(diag, diag, mask[0:TT, :], ALU.add).then_inc(s_masked, 1)
                    dve.wait_ge(s_masked, NT * b + i + 1)
                    dve.tensor_reduce(negmax[0:TT, i % 2:i % 2 + 1], bank(s, 0, n, 0, TT), AX.X, ALU.max,
                                      negate=True).then_inc(max_ready, 1)

                def dve_pT(i):
                    dve.wait_ge(p_turned, NT * b + i + 1)
                    src = bank(4, 0, (i + 1) * 128, 0, TT).rearrange("p (k q) -> p k q", q=128)[:, :, 0:TT]
                    dve.tensor_copy(pT[0:TT, i % 2, 0:i + 1, :], src).then_inc(pT_ready, 1)
                    dve.reciprocal(rinv[0:TT, i % 4:i % 4 + 1], rowsum[0:TT, i % 2:i % 2 + 1]).then_inc(rinv_ready, 1)

                def dve_h(i):
                    dve.wait_ge(wo_mm, NT * b + i + 1)
                    dve.wait_ge(h_biased, NT * b + i + 1)
                    dve.tensor_tensor(h[0:TT, b * NT + i, :], bank(7, D, 2 * D, 0, TT), h[0:TT, b * NT + i, :],
                                      ALU.add).then_inc(h_attn, 1)

                dve_scores(0)
                dve_scores(1)
                for i in range(NT + 2):
                    if i < NT:
                        dve_pT(i)
                    if i + 2 < NT:
                        dve_scores(i + 2)
                    if i < 3:
                        for t in (2 * i, 2 * i + 1):
                            dve_tok(b + 1, t, 5)
                    if i >= 2:
                        dve_h(i - 2)
                    if i == 3:
                        wait_apart(dve, "dve", h_tok, NT * (b + 2), B)
                        for t in range(NT):
                            dve.bn_stats(bn6[0:TT, t, :], h[0:TT, (b + 1) * NT + t, :]).then_inc(ln_seq, 1)
                    if i == 4:
                        wait_apart(dve, "dve", ln_seq, LN_CALL * (b + 1) + NT, B)
                        for t in range(NT):
                            dve.bn_aggr(mv[0:TT, t, :], bn6[0:TT, t, :]).then_inc(ln_seq, 1)
                    if i == 5:
                        dve.wait_ge(ln_seq, LN_CALL * (b + 1) + 2 * NT)
                        rsqrt(dve, mv[0:TT, 0:NT, 1], yr[0:TT, 0:NT], ve[0:TT, 0:NT], yt[0:TT, 0:NT], ln_seq,
                              LN_CALL * (b + 1) + 2 * NT)
                        dve.wait_ge(ln_seq, LN_CALL * (b + 2))
                        for t in range(NT):
                            dve.tensor_scalar(xn[0:TT, t, :], h[0:TT, (b + 1) * NT + t, :], mv[0:TT, t, 0:1],
                                              yr[0:TT, t:t + 1], ALU.subtract, ALU.mult).then_inc(xn_ready, 1)

            MB = ISH // 128

            def dve_act_s(c, m):
                dve.wait_ge(silu_s_ready, MB * c + m + 1)
                dve.tensor_tensor(act_s[:, m, 0:HALF], silu_s[:, m % 2, :],
                                  bank(2 * (m % 3) + 1, 0, HALF), ALU.mult).then_inc(act_s_ready, 1)

            def dve_h_shared(b):
                for t in range(3):
                    dve.wait_ge(down_mm, 3 * b + t + 1)
                    hh = h[0:TT, b * NT + t, :]
                    dve.tensor_tensor(hh, bank(6 + t % 2, 0, D, 0, TT), hh, ALU.add).then_inc(h_shared, 1)

            dve.wait_ge(consts_m, 8)
            dve.wait_ge(h_attn, NG)
            layernorm(dve, 0, LN_CALL * (B + 1), 1)
            with dve.Fori(0, B) as b:
                dve.wait_ge(router_mm, b + 1)
                dve.tensor_copy(logits[0:TT, :, :], bank(6, 0, NT * E, 0, TT).rearrange("p (t e) -> p t e", e=E))\
                    .then_inc(logits_ready, 1)
                r = R_CALL * b
                wait_apart(dve, "dve", logits_ready, b + 1, B)
                for t in range(NT):
                    dve.max(top[0:TT, t, :], logits[0:TT, t, :]).then_inc(routed, 1)
                wait_apart(dve, "dve", routed, r + NT, B)
                for t in range(NT):
                    dve.max_index(top_i[0:TT, t, :], top[0:TT, t, :], logits[0:TT, t, :]).then_inc(routed, 1)
                dve.tensor_tensor(gap[0:TT, 0, bass.ds(b * NT, NT)], top[0:TT, :, 1], top[0:TT, :, 0], ALU.subtract)\
                    .then_inc(gap_ready, 1)
                dve.wait_ge(routed, r + 2 * NT)
                dve.tensor_copy(top_f[0:TT, :, :], top_i[0:TT, :, 0:2]).then_inc(routed, 1)
                dve.wait_ge(routed, r + 2 * NT + 1)
                for c in range(2):
                    dve.tensor_tensor(hot[0:TT, c, bass.ds(b * NT, NT), :],
                                      top_f[0:TT, :, c:c + 1].to_broadcast([TT, NT, E]),
                                      iota_e[0:TT, :].unsqueeze(1).to_broadcast([TT, NT, E]), ALU.is_equal)\
                        .then_inc(routed, 1)
                dve.wait_ge(routed, r + R_CALL)
                dve_act_s(b, 0)
                at, nxt = LN_CALL * (B + 2 + b), (b + 1) % B * NT
                for t in range(NT):
                    dve.bn_stats(bn6[0:TT, t, :], h[0:TT, nxt + t, :]).then_inc(ln_seq, 1)
                dve_act_s(b, 1)
                wait_apart(dve, "dve", ln_seq, at + NT, B)
                for t in range(NT):
                    dve.bn_aggr(mv[0:TT, t, :], bn6[0:TT, t, :]).then_inc(ln_seq, 1)
                dve.wait_ge(ln_seq, at + 2 * NT)
                rsqrt(dve, mv[0:TT, 0:NT, 1], yr[0:TT, 0:NT], ve[0:TT, 0:NT], yt[0:TT, 0:NT], ln_seq, at + 2 * NT)
                dve_act_s(b, 2)
                dve.wait_ge(ln_seq, at + LN_CALL)
                dve.wait_ge(x_kept, NT * b + NT)
                for t in range(NT):
                    dve.tensor_scalar(xn[0:TT, t, :], h[0:TT, nxt + t, :], mv[0:TT, t, 0:1], yr[0:TT, t:t + 1],
                                      ALU.subtract, ALU.mult).then_inc(xn_ready, 1)
                    if t == 1:
                        dve_act_s(b, 3)
                dve_h_shared(b)

            steps = [0]

            def step(ins):
                steps[0] += 1
                ins.then_inc(rows_step, 1)
                dve.wait_ge(rows_step, steps[0])

            dve.tensor_tensor(hots[0:TT, :, :], hot[0:TT, 0, :, :], hot[0:TT, 1, :, :], ALU.add)\
                .then_inc(hots_ready, 1)
            dve.wait_ge(share_exp, 1)
            step(dve.tensor_scalar(gap[0:TT, 0, :], gap[0:TT, 1, :], 1.0, None, ALU.add))
            step(dve.reciprocal(share[0:TT, 0, 0:NG], gap[0:TT, 0, :]))
            step(dve.tensor_tensor(share[0:TT, 1, 0:NG], share[0:TT, 0, 0:NG], gap[0:TT, 1, :], ALU.mult))
            dve.wait_ge(rank_mm, 1)
            step(dve.tensor_copy(tot[0:TT, :, :], bank(7, 0, NG * E, 0, TT).rearrange("p (t e) -> p e t", e=E)))
            flat = lambda v: v[0:TT, :, :].rearrange("p e t -> p (e t)")
            step(dve.tensor_tensor_scan(flat(incl), flat(restart), flat(tot), 0.0, ALU.mult, ALU.add))
            step(dve.tensor_tensor(over[0:TT, :, :], incl[0:TT, :, NG - 1:NG].to_broadcast([TT, E, NG]),
                                   iota_c[0:TT, :].unsqueeze(1).to_broadcast([TT, E, NG]), ALU.is_gt))
            step(dve.tensor_reduce(n_slots[0:TT, :], over[0:TT, :, :], AX.X, ALU.add))
            step(dve.tensor_tensor_scan(slot_end[0:TT, :], ones[0:TT, 0:E], n_slots[0:TT, :], 0.0, ALU.mult, ALU.add))
            step(dve.tensor_tensor(slot_beg[0:TT, :], slot_end[0:TT, :], n_slots[0:TT, :], ALU.subtract))
            step(dve.tensor_tensor(incl[0:TT, :, :], incl[0:TT, :, :], tot[0:TT, :, :], ALU.subtract))
            step(dve.scalar_tensor_tensor(base[0:TT, :, :], slot_beg[0:TT, :].unsqueeze(2).to_broadcast([TT, E, NG]),
                                          float(SLOT), incl[0:TT, :, :], ALU.mult, ALU.add))
            step(dve.tensor_tensor(place[0:TT, :, :], bank(6, 0, NG * E, 0, TT).rearrange("p (t e) -> p t e", e=E),
                                   base[0:TT, :, :].rearrange("p e t -> p t e"), ALU.add))
            for c in range(2):
                step(dve.tensor_tensor(picked[0:TT, c, :, :], hot[0:TT, c, :, :], place[0:TT, :, :], ALU.mult))
                step(dve.tensor_reduce(row_f[0:TT, c, :], picked[0:TT, c, :, :], AX.X, ALU.add))
            dve.tensor_copy(row[0:TT, :, :], row_f[0:TT, :, :]).then_inc(rows_ready, 1)
            step(dve.tensor_tensor(ended[:, :, :], slot_end[0:1, :].unsqueeze(1).to_broadcast([1, NSLOT, E]),
                                   iota_j[0:1, :].unsqueeze(2).to_broadcast([1, NSLOT, E]), ALU.is_le))
            step(dve.tensor_reduce(slot_e_f[:, :], ended[:, :, :], AX.X, ALU.add))
            dve.tensor_scalar(slot_e[:, :], slot_e_f[:, :], float(E - 1), None, ALU.min).then_inc(rows_ready, 1)

            def dve_h_late(b):
                for t in range(3):
                    n = 3 * b + t
                    dve.wait_ge(down_mm, 3 * B + n + 1)
                    hh = h[0:TT, b * NT + 3 + t, :]
                    dve.tensor_tensor(hh, bank(6 + n % 2, 0, D, 0, TT), hh, ALU.add).then_inc(h_shared, 1)

            for n in range(MB * B):
                b, m = divmod(n, MB)
                dve.wait_ge(silu_s_ready, MB * B + n + 1)
                dve.tensor_tensor(act_s[:, m, b % 2 * HALF:(b % 2 + 1) * HALF], silu_s[:, n % 2, :],
                                  bank(2 * (n % 3) + 1, 0, HALF), ALU.mult).then_inc(act_s_ready, 1)
                if b and m == 0:
                    dve_h_late(b - 1)
            dve_h_late(B - 1)

            def dve_expert(j, p):
                dve.wait_ge(silu_ready, j + 1)
                dve.tensor_tensor(u[:, p, :], silu[:, p, :], bank(2 + p, I, 2 * I), ALU.mult).then_inc(u_ready, 1)

            def dve_uT(j, p):
                dve.wait_ge(u_turned, j + 1)
                dve.tensor_copy(uT[:, p, :, :], bank(4 + p, 0, KD * SLOT).rearrange("p (k q) -> p k q", k=KD))\
                    .then_inc(uT_ready, 1)

            dve_expert(0, 0)
            dve_uT(0, 0)
            dve_expert(1, 1)
            with dve.Fori(1, NSLOT // 2) as i:
                for p in range(2):
                    dve_uT(2 * i + p - 1, 1 - p)
                    dve_expert(2 * i + p, p)
            dve_uT(NSLOT - 1, 1)

            dve.wait_ge(wF_loaded, 4 * 16)
            for c, w in enumerate((wf_raw, wp_raw)):
                dve.tensor_reduce(absum[:, c:c + 1], w[:, :], AX.X, ALU.add, apply_absolute_value=True)\
                    .then_inc(absum_ready, 1)
            dve.wait_ge(gamma_mm, 1)
            half = 0.5 / (FH * D)
            dve.tensor_scalar(above[:, :], bank(7, 0, 2), half, GAMMA_EPS / 2, ALU.mult, ALU.add).then_inc(tern_step, 1)
            dve.wait_ge(tern_step, 1)
            dve.tensor_scalar(below[:, :], above[:, :], -1.0, None, ALU.mult).then_inc(tern_step, 1)
            negs = probs[:, :, :].rearrange("p a t -> p (a t)")[:, 0:FH]
            flat_f = w_f[:, :, :].rearrange("p k n -> p (k n)")
            flat_p = w_p[:, :, :].rearrange("p k n -> p (k n)")
            for n in range(4):
                c, lo = n // 2, n % 2 * FH
                w, q = (wf_raw, flat_f) if c == 0 else (wp_raw, flat_p)
                dve.wait_ge(tern_step, 2 + 2 * n)
                dve.tensor_scalar(negs, w[:, lo:lo + FH], below[:, c:c + 1], -1.0, ALU.is_lt, ALU.mult)\
                    .then_inc(tern_step, 1)
                dve.wait_ge(tern_step, 3 + 2 * n)
                dve.scalar_tensor_tensor(q[:, lo:lo + FH], w[:, lo:lo + FH], above[:, c:c + 1], negs,
                                         ALU.is_gt, ALU.add).then_inc(tern_step, 1)

            for t in range(NT):
                dve.wait_ge(gathered[t], 32)
                for c in range(2):
                    if c:
                        dve.wait_ge(h_moe, 2 * t + 1)
                    dve.scalar_tensor_tensor(h[0:TT, t, :], ring[0:TT, t, c, :], share[0:TT, c, t:t + 1],
                                             h[0:TT, t, :], ALU.mult, ALU.add).then_inc(h_moe, 1)
            dve.wait_ge(h_moe, 2 * NT)

            dve.sem_inc(o_ready, 1)
            dve.memset(o_T[:, :, :], 0.0).then_inc(o_zeroed, 1)

            def dve_k(b, c, at=7):
                lo, hi = CUTS[c]
                dve.wait_ge(kv_hi, 3 * b + c + 1)
                dve.tensor_tensor(k_lo[:, b % 2, lo:hi], bank(at, 0, hi - lo), k_hi[:, b % 2, lo:hi].bitcast(F32),
                                  ALU.subtract).then_inc(kv_ready, 1)

            def dve_v(b):
                dve.wait_ge(kv_hi, 3 * b + 3)
                dve.tensor_tensor(v_st[0:TT, :, LAT:2 * LAT],
                                  bank(7, 0, NT * LAT, 0, TT).rearrange("p (t l) -> p t l", l=LAT),
                                  v_st[0:TT, :, 0:LAT].bitcast(F32), ALU.subtract).then_inc(kv_ready, 1)

            def dve_q(b, p, c, at=7):
                lo, hi = CUTS[c]
                dve.wait_ge(q_hi, 4 * (PAIRS * b + p) + 2 * c + 2)
                for n in range(2):
                    own, other = ((0, 64), (64, 128))[::1 - 2 * n]
                    q = q_st[:, 2 * (p % 2) + n, lo:hi]
                    dve.tensor_tensor(q[other[0]:other[1], :], bank(at, 0, hi - lo, own[0], own[1]),
                                      q[own[0]:own[1], :].bitcast(F32), ALU.subtract).then_inc(q_ready, 1)

            def dve_max(g):
                dve.wait_ge(s1_mm, first + g + 1)
                dve.tensor_reduce(negmax[0:TT, g % 2:g % 2 + 1], bank(2 * (g % 2), 0, T, 0, TT), AX.X, ALU.max,
                                  negate=True).then_inc(max1_ready, 1)

            def dve_rinv(g):
                dve.wait_ge(probs1_ready, first + g + 1)
                dve.reciprocal(rinv1[0:TT, g % 2:g % 2 + 1], rowsum[0:TT, g % 2:g % 2 + 1]).then_inc(rinv1_ready, 1)

            def dve_lo(g):
                for c in range(2):
                    dve.wait_ge(p1_hi, 2 * (first + g) + c + 1)
                    src = bank(4 + c, 0, 3 * TT, 0, TT).rearrange("p (k q) -> p k q", q=TT)
                    dve.tensor_tensor(pT1[0:TT, g % 2, 3 * c:3 * c + 3, 1, :], src,
                                      pT1[0:TT, g % 2, 3 * c:3 * c + 3, 0, :].bitcast(F32), ALU.subtract)\
                        .then_inc(p1_ready, 1)

            def dve_o(g):
                t, n = g % NT, g // NT % 2
                dve.wait_ge(pv1_mm, first + g + 1)
                dve.tensor_reduce(o_T[:, n, t * TT:(t + 1) * TT],
                                  bank(6, 0, 2 * TT).rearrange("p (a q) -> p q a", a=2), AX.X, ALU.add)\
                    .then_inc(o_ready, 1)

            def dve_out(slot, b, i, at=7):
                dve.wait_ge(out1_mm, NT * slot + i + 1)
                hh = h[0:TT, b * NT + i, :]
                dve.tensor_tensor(hh, bank(at, 0, D, 0, TT), hh, ALU.add).then_inc(h_lat, 1)

            def dve_ln(b, s):
                at = LN_CALL * (2 * B + 3 + b)
                nxt = (b + 1) % B * NT
                if s in STATS_AT:
                    if s == STATS_AT[0]:
                        wait_apart(dve, "dve", h_moe, 2 * NT * ((b + 1) % B + 1), B)
                    t = 2 * STATS_AT.index(s)
                    for t in (t, t + 1):
                        dve.bn_stats(bn6[0:TT, t, :], h[0:TT, nxt + t, :]).then_inc(ln_seq, 1)
                if s == STATS_AT[-1] + 1:
                    wait_apart(dve, "dve", ln_seq, at + NT, B)
                    for t in range(NT):
                        dve.bn_aggr(mv[0:TT, t, :], bn6[0:TT, t, :]).then_inc(ln_seq, 1)
                if s in CHAIN_AT:
                    for k in (2 * CHAIN_AT.index(s), 2 * CHAIN_AT.index(s) + 1):
                        dve.wait_ge(ln_seq, at + 2 * NT + k)
                        rsqrt(dve, mv[0:TT, 0:NT, 1], yr[0:TT, 0:NT], ve[0:TT, 0:NT], yt[0:TT, 0:NT], ln_seq,
                              at + 2 * NT, [k])
                if s in NORM_AT:
                    if s == NORM_AT[0]:
                        dve.wait_ge(ln_seq, at + LN_CALL)
                    t = 2 * NORM_AT.index(s)
                    for t in (t, t + 1):
                        dve.tensor_scalar(xn[0:TT, t, :], h[0:TT, nxt + t, :], mv[0:TT, t, 0:1], yr[0:TT, t:t + 1],
                                          ALU.subtract, ALU.mult).then_inc(xn_ready, 1)

            layernorm(dve, 0, LN_CALL * (2 * B + 2), 1)
            first = 0
            for c in range(2):
                dve_k(0, c, START_KEYS[c])
            for c in range(2):
                dve_q(0, 0, c, START_QUERIES[c])
            dve_v(0)
            dve_max(0)
            dve_max(1)
            dve_rinv(0)
            dve_max(2)
            dve_rinv(1)
            dve_max(3)
            dve_rinv(2)
            dve_lo(0)
            with dve.Fori(0, B) as b:
                first = STEPS * b
                for s in range(1, STEPS + 1):
                    dve_max(s + 3)
                    dve_rinv(s + 2)
                    dve_lo(s)
                    dve_o(s - 1)
                    if s in PROJECT_AT:
                        p, i = PROJECT_AT[s]
                        dve_out(PAIRS * b + p, b if p else (b + B - 1) % B, i)
                    dve_ln(b, s)
                    if s in QUERY_AT:
                        p, c = QUERY_AT[s]
                        dve_q(b, p, c)
                    if s in KEYS_AT:
                        dve_k(b + 1, KEYS_AT[s])
                dve_v(b + 1)
            for i in range(NT):
                dve_out(PAIRS * B, B - 1, i, (7, 6)[i % 2])
            dve.wait_ge(h_lat, NT * (PAIRS * B + 1))

            dve.wait_ge(bias_split, 1)
            dve.tensor_tensor(n_lo[:, :, 0:TT], ln_b[:, :].unsqueeze(2).to_broadcast([128, FB, TT]),
                              n_hi[:, :, 0:TT].bitcast(F32), ALU.subtract).then_inc(bias_split, 1)

            def rounds(g):
                return 1 if isinstance(g, int) else NGR // 2 - 1

            def dve_x(g):
                layernorm(dve, 3 * g, LNX_CALL * g, rounds(g), 3, lnx_seq, fx_ready)

            def dve_x_part(g, f):
                at = LNX_CALL * g
                if f == 0:
                    for t in range(3):
                        dve.bn_stats(bn6[0:TT, t, :], h[0:TT, 3 * g + t, :]).then_inc(lnx_seq, 1)
                elif f == 1:
                    wait_apart(dve, "dve", lnx_seq, at + 3, rounds(g))
                    for t in range(3):
                        dve.bn_aggr(mv[0:TT, t, :], bn6[0:TT, t, :]).then_inc(lnx_seq, 1)
                else:
                    for k in (2 * f - 4, 2 * f - 3):
                        dve.wait_ge(lnx_seq, at + 6 + k)
                        rsqrt(dve, mv[0:TT, 0:3, 1], yr[0:TT, 0:3], ve[0:TT, 0:3], yt[0:TT, 0:3], lnx_seq, at + 6, [k])

            def dve_x_norm(g):
                dve.wait_ge(lnx_seq, LNX_CALL * (g + 1))
                for t in range(3):
                    dve.tensor_scalar(xn[0:TT, t, :], h[0:TT, 3 * g + t, :], mv[0:TT, t, 0:1], yr[0:TT, t:t + 1],
                                      ALU.subtract, ALU.mult).then_inc(fx_ready, 1)

            def dve_x_lo(g):
                for k in range(KD):
                    dve.wait_ge(x_hi_ready, KD * g + k + 1)
                    dve.tensor_tensor(x_lo[:, k, :], bank(k, 0, GT), x_hi[:, k, :].bitcast(F32), ALU.subtract)\
                        .then_inc(x_split, 1)

            def dve_bn(g, p, t):
                wait_apart(dve, "dve", gelu_ready, 3 * g + t + 1, rounds(g))
                for c in range(2):
                    dve.bn_stats(bn_f[0:TT, t, c, :], hidden[0:TT, p, t, c * BANK:(c + 1) * BANK]).then_inc(lnf_seq, 1)

            def dve_norm(g):
                at = LNF_CALL * g
                wait_apart(dve, "dve", lnf_seq, at + 6, rounds(g))
                for t in range(3):
                    dve.bn_aggr(mv_f[0:TT, t, :], bn_f[0:TT, t, :, :].rearrange("p c s -> p (c s)")).then_inc(lnf_seq, 1)
                dve.wait_ge(lnf_seq, at + 9)
                rsqrt(dve, mv_f[0:TT, :, 1], yr_f[0:TT, :], ve_f[0:TT, :], yt_f[0:TT, :], lnf_seq, at + 9)
                dve.wait_ge(lnf_seq, at + 9 + LN_CHAIN)
                dve.scalar_tensor_tensor(nm_f[0:TT, :], mv_f[0:TT, :, 0], -1.0, yr_f[0:TT, :], ALU.mult, ALU.mult)\
                    .then_inc(lnf_seq, 1)

            def dve_n_lo(g, f):
                dve.wait_ge(n_hi_ready, FB * g + f + 1)
                dve.scalar_tensor_tensor(n_lo[:, f, :], bank(f % 2, 0, GT), ln_w[:, f:f + 1],
                                         n_hi[:, f, :].bitcast(F32), ALU.mult, ALU.subtract).then_inc(n_split, 1)

            def dve_out(g, t):
                dve.wait_ge(proj_mm, 3 * g + t + 1)
                dve.wait_ge(h_biased2, 3 * g + t + 1)
                hh = h[0:TT, 3 * g + t, :]
                dve.tensor_tensor(hh, bank(6 + t % 2, 0, D, 0, TT), hh, ALU.add).then_inc(h_out, 1)

            def dve_step(g, p, more=True, more2=True):
                for f in range(FB):
                    dve_n_lo(g, f)
                    if more2:
                        dve_x_part(g + 2, f)
                    if more and f in (2, 4, 6):
                        dve_bn(g + 1, 1 - p, f // 2 - 1)
                if more:
                    dve_norm(g + 1)
                if more2:
                    dve_x_norm(g + 2)
                dve_out(g, 0)
                dve_out(g, 1)
                if more2:
                    dve_x_lo(g + 2)
                dve_out(g, 2)

            dve_x(0)
            dve.wait_ge(bias_mm, 1)
            dve.tensor_copy(b_out[0:TT, :], bank(7, 0, D, 0, TT)).then_inc(b_out_ready, 1)
            dve_x_lo(0)
            dve_x(1)
            for t in range(3):
                dve_bn(0, 0, t)
            dve_x_lo(1)
            dve_norm(0)
            with dve.Fori(0, NGR // 2 - 1) as i:
                for p in range(2):
                    dve_step(2 * i + p, p)
            dve_step(NGR - 2, 0, True, False)
            dve_step(NGR - 1, 1, False, False)
            dve.wait_ge(passed["dve"], passes["dve"])

        @block.scalar
        def _(act):
            act.wait_ge(const_made, 2)
            act.wait_ge(wA_loaded, WA)

            def act_xT0(b):
                for t in range(NT):
                    act.wait_ge(xn_turned, NT * b + t + 1)
                    act.copy(xT[:, :, t * TT:(t + 1) * TT],
                             bank(t, 0, KD * TT).rearrange("p (k q) -> p k q", k=KD)).then_inc(xT_ready, 1)

            act_xT0(0)
            with act.Fori(0, B) as b:
                for j in range(8):
                    m, half, isk = j // 2 % 2, j % 2, j // 4
                    dst = (kT if isk else qT)[:, m, half * 375:(half + 1) * 375]
                    act.wait_ge(qk_mm, 8 * b + j + 1)
                    act.activation(dst, bank(j, 0, 375), ACT.Identity,
                                   bias=(bk0 if isk else bq0s)[:, m:m + 1], scale=1.0 if isk else 1.0 / 16)\
                        .then_inc(qk_ready, 1)

                def act_exp(i):
                    n, s = (i + 1) * TT, i % 2
                    act.wait_ge(max_ready, NT * b + i + 1)
                    act.activation(probs[0:TT, s, 0:n], bank(2 * s, 0, n, 0, TT), ACT.Exp,
                                   bias=negmax[0:TT, s:s + 1], scale=1.0, accum_out=rowsum[0:TT, s:s + 1])\
                        .then_inc(probs_ready, 1)

                def act_ctx(i):
                    act.wait_ge(pv_mm, NT * b + i + 1)
                    act.wait_ge(rinv_ready, NT * b + i + 1)
                    act.mul(ctxt[0:TT, :], bank(6, 0, D, 0, TT), rinv[0:TT, i % 4:i % 4 + 1]).then_inc(ctx_ready, 1)

                def act_ctxT(i):
                    act.wait_ge(ctx_turned, NT * b + i + 1)
                    act.copy(ctxT[:, :, :], bank(7, 0, KD * TT).rearrange("p (k q) -> p k q", k=KD))\
                        .then_inc(ctxT_ready, 1)

                act_exp(0)
                for i in range(NT + 2):
                    if i + 1 < NT:
                        act_exp(i + 1)
                    if i >= 2:
                        act_ctxT(i - 2)
                    if 1 <= i <= NT:
                        act_ctx(i - 1)
                    if i == NT:
                        act_xT0(b + 1)

            MB = ISH // 128

            def act_silu_s(c, m):
                act.wait_ge(gu_mm, MB * c + m + 1)
                if m >= 2:
                    act.wait_ge(act_s_ready, MB * c + m - 1)
                act.activation(silu_s[:, m % 2, :], bank(2 * (m % 3), 0, HALF), ACT.Silu).then_inc(silu_s_ready, 1)

            with act.Fori(0, B) as b:
                for t in range(NT):
                    act.wait_ge(xn_turned, NT * (b + 1) + NG + t + 1)
                    act.copy(xT[:, :, t * TT:(t + 1) * TT],
                             bank(t, 0, KD * TT).rearrange("p (k q) -> p k q", k=KD)).then_inc(xT_ready, 1)
                act_silu_s(b, 0)
                act.wait_ge(xT_ready, NT * (b + 1) + NG + NT)
                act.copy(xT_late[:, :, bass.ds(b * HALF, HALF)], xT[:, :, HALF:T]).then_inc(x_late, 1)
                for m in range(1, MB):
                    act_silu_s(b, m)
                act.wait_ge(x_late, b + 1)
            act.wait_ge(gap_ready, B)
            act.activation(gap[0:TT, 1, :], gap[0:TT, 0, :], ACT.Exp).then_inc(share_exp, 1)
            for n in range(MB * B):
                act.wait_ge(gu_mm, MB * B + n + 1)
                if n >= 2:
                    act.wait_ge(act_s_ready, MB * B + n - 1)
                act.activation(silu_s[:, n % 2, :], bank(2 * (n % 3), 0, HALF), ACT.Silu).then_inc(silu_s_ready, 1)

            def act_xgT(j, p):
                act.wait_ge(xg_turned, j + 1)
                act.copy(xgT[:, p, :, :], bank(p, 0, KD * SLOT).rearrange("p (k q) -> p k q", k=KD))\
                    .then_inc(xgT_ready, 1)

            def act_silu(j, p):
                act.wait_ge(fc1_mm, j + 1)
                act.activation(silu[:, p, :], bank(2 + p, 0, I), ACT.Silu).then_inc(silu_ready, 1)

            def act_y(j, p, wait):
                act.wait_ge(fc2_mm, j + 1)
                if wait:
                    act.wait_ge(y_stored[p], 8 * (j - p))
                act.copy(y_out[:, p, :], bank(6 + p, 0, D)).then_inc(y_ready, 1)

            def store_y(j, p):
                act.wait_ge(y_ready, j + 1)
                act.dma_start(ys_dram[bass.ds(j * SLOT, SLOT), :], y_out[:, p, :]).then_inc(y_stored[p], 16)

            act_xgT(0, 0)
            act_silu(0, 0)
            act_xgT(1, 1)
            act_silu(1, 1)
            act_xgT(2, 0)
            act_y(0, 0, False)
            act_silu(2, 0)
            store_y(0, 0)
            act_xgT(3, 1)
            act_y(1, 1, False)
            act_silu(3, 1)
            store_y(1, 1)
            with act.Fori(2, NSLOT // 2) as i:
                for p in range(2):
                    act_xgT(2 * i + p, p)
                    act_y(2 * i + p - 2, p, True)
                    act_silu(2 * i + p, p)
                    store_y(2 * i + p - 2, p)
            for p in range(2):
                act_y(NSLOT - 2 + p, p, True)
                store_y(NSLOT - 2 + p, p)

            act.wait_ge(w_mm, 1)
            for c in range(2):
                act.mul(w_qk[:, 2 * c:2 * c + 2, :, :],
                        bank(c).rearrange("p (n k m) -> p n k m", n=2, k=KD), HD ** -0.5).then_inc(w_folded, 1)
            for c in range(4):
                act.copy(w_vo[:, 2 * c:2 * c + 2, :], bank(2 + c).rearrange("p (n m) -> p n m", n=2))\
                    .then_inc(w_folded, 1)

            def act_xT1(b, t, at=7):
                act.wait_ge(xn_turned, NT * b + C_TURNED + t + 2)
                act.copy(xT[:, :, t * TT:(t + 2) * TT],
                         bank(at, 0, KD * 2 * TT).rearrange("p (k q) -> p k q", k=KD)).then_inc(xT_ready, 2)

            def act_k(b, c, at=7):
                lo, hi = CUTS[c]
                act.wait_ge(kv_mm, 3 * b + c + 1)
                act.copy(k_hi[:, b % 2, lo:hi], bank(at, 0, hi - lo)).then_inc(kv_hi, 1)

            def act_v(b):
                act.wait_ge(kv_mm, 3 * b + 3)
                act.copy(v_st[0:TT, :, 0:LAT], bank(7, 0, NT * LAT, 0, TT).rearrange("p (t l) -> p t l", l=LAT))\
                    .then_inc(kv_hi, 1)

            def act_q(b, p, c, at=7):
                lo, hi = CUTS[c]
                act.wait_ge(q_mm, 2 * (PAIRS * b + p) + c + 1)
                for n, (p0, p1) in enumerate(((0, 64), (64, 128))):
                    act.copy(q_st[p0:p1, 2 * (p % 2) + n, lo:hi], bank(at, 0, hi - lo, p0, p1)).then_inc(q_hi, 1)

            def act_exp1(g):
                act.wait_ge(max1_ready, first + g + 1)
                act.activation(probs1[0:TT, g % 3, :], bank(2 * (g % 2), 0, T, 0, TT), ACT.Exp,
                               bias=negmax[0:TT, g % 2:g % 2 + 1], scale=1.0,
                               accum_out=rowsum[0:TT, g % 2:g % 2 + 1]).then_inc(probs1_ready, 1)

            def act_scale(g):
                act.wait_ge(rinv1_ready, first + g + 1)
                act.mul(probs1[0:TT, g % 3, :], probs1[0:TT, g % 3, :], rinv1[0:TT, g % 2:g % 2 + 1])\
                    .then_inc(scaled_ready, 1)

            def act_hi(g):
                for c in range(2):
                    act.wait_ge(p1_turned, 2 * (first + g) + c + 1)
                    src = bank(4 + c, 0, 3 * TT, 0, TT).rearrange("p (k q) -> p k q", q=TT)
                    act.copy(pT1[0:TT, g % 2, 3 * c:3 * c + 3, 0, :], src).then_inc(p1_hi, 1)

            for t in range(0, NT, 2):
                act_xT1(0, t, START_TURN[t // 2])
            first = 0
            for c in range(2):
                act_k(0, c, START_KEYS[c])
            for c in range(2):
                act_q(0, 0, c, START_QUERIES[c])
            act_v(0)
            act_exp1(0)
            act_exp1(1)
            act_scale(0)
            act_exp1(2)
            act_scale(1)
            act_hi(0)
            with act.Fori(0, B) as b:
                first = STEPS * b
                for s in range(1, STEPS + 1):
                    act_exp1(s + 2)
                    act_scale(s + 1)
                    act_hi(s)
                    if s in QUERY_AT:
                        p, c = QUERY_AT[s]
                        act_q(b, p, c)
                    if s in TURN_AT:
                        act_xT1(b + 1, TURN_AT[s])
                    if s in KEYS_AT:
                        act_k(b + 1, KEYS_AT[s])
                act.wait_ge(pv1_mm, STEPS * (b + 1))
                act_v(b + 1)

            act.wait_ge(h_lat, NT * (PAIRS * B + 1))
            act.wait_ge(w_picked, PAIRS * B + 1)
            act.copy(n_hi[:, :, 0:TT], ln_b[:, :].unsqueeze(2).to_broadcast([128, FB, TT])).then_inc(bias_split, 1)

            def act_x_hi(g):
                for k in range(KD):
                    act.wait_ge(fx_turned, KD * g + k + 1)
                    act.copy(x_hi[:, k, :], bank(k, 0, GT)).then_inc(x_hi_ready, 1)

            def act_gelu(g, p, t):
                s = 2 + 2 * ((3 * p + t) % 2)
                act.wait_ge(fc_mm, 3 * g + t + 1)
                act.activation(hidden[0:TT, p, t, :], bank(s, 0, FH, 0, TT), ACT.Gelu).then_inc(gelu_ready, 1)

            def act_norm(g, p):
                act.wait_ge(lnf_seq, LNF_CALL * (g + 1))
                for t in range(3):
                    act.activation(hidden[0:TT, p, t, :], hidden[0:TT, p, t, :], ACT.Identity,
                                   bias=nm_f[0:TT, t:t + 1], scale=yr_f[0:TT, t:t + 1]).then_inc(norm_ready, 1)

            def act_n_hi(g, f):
                act.wait_ge(n_turned, FB * g + f + 1)
                act.mul(n_hi[:, f, :], bank(f % 2, 0, GT), ln_w[:, f:f + 1]).then_inc(n_hi_ready, 1)

            def act_step(g, p, more=True, more2=True):
                for f in range(FB):
                    act_n_hi(g, f)
                    if more and f in (2, 4, 6):
                        act_gelu(g + 1, 1 - p, f // 2 - 1)
                if more:
                    act_norm(g + 1, 1 - p)
                if more2:
                    act_x_hi(g + 2)

            act_x_hi(0)
            for t in range(3):
                act_gelu(0, 0, t)
            act_x_hi(1)
            act_norm(0, 0)
            with act.Fori(0, NGR // 2 - 1) as i:
                for p in range(2):
                    act_step(2 * i + p, p)
            act_step(NGR - 2, 0, True, False)
            act_step(NGR - 1, 1, False, False)

        @block.tensor
        def _(pe):
            pe.wait_ge(wA_loaded, WA)
            pe.wait_ge(ident_made, 4)

            def embed(t, at):
                pe.matmul(bank(at, 0, D, 0, TT), ewma[:, t * TT:(t + 1) * TT], w_tok[:, :],
                          start=True, stop=True).then_inc(tok_mm, 1)

            pe.wait_ge(ew_step, 6)
            for t in range(NT):
                embed(t, t)

            def turn_x0(b):
                for t in range(NT):
                    pe.wait_ge(xn_ready, NT * b + t + 1)
                    for k in range(KD):
                        mm = pe.transpose(bank(t, k * TT, (k + 1) * TT), xn[0:TT, t, k * 128:(k + 1) * 128],
                                          ident[0:TT, 0:TT])
                    mm.then_inc(xn_turned, 1)

            turn_x0(0)
            with pe.Fori(0, B) as b:
                pe.wait_ge(xT_ready, NT * b + NT)
                for j in range(8):
                    m, half, w = j // 2 % 2, j % 2, (wk0 if j // 4 else wq0)
                    for k in range(KD):
                        mm = pe.matmul(bank(j, 0, 375), w[:, k, m * 128:(m + 1) * 128],
                                       xT[:, k, half * 375:(half + 1) * 375], start=k == 0, stop=k == KD - 1)
                    mm.then_inc(qk_mm, 1)
                for t in range(NT):
                    pe.wait_ge(qk_ready, 8 * b + t + 1)
                    for k in range(KD):
                        mm = pe.matmul(bank(t, 0, D, 0, TT), xT[:, k, t * TT:(t + 1) * TT], wv0[:, k, :],
                                       start=k == 0, stop=k == KD - 1)
                    mm.then_inc(v_mm, 1)
                pe.wait_ge(qk_ready, 8 * b + 8)
                pe.wait_ge(v_ready, NT * b + NT)

                def scores(i):
                    n, s = (i + 1) * TT, 2 * (i % 2)
                    if i >= 2:
                        pe.wait_ge(probs_ready, NT * b + i - 1)
                    for lo in range(0, n, BANK):
                        hi = min(n, lo + BANK)
                        for k in range(KD):
                            mm = pe.matmul(bank(s, lo, hi, 0, TT), qT[:, k, i * TT:(i + 1) * TT], kT[:, k, lo:hi],
                                           start=k == 0, stop=k == KD - 1)
                    mm.then_inc(s_mm, 1)

                def turn_probs(i):
                    pe.wait_ge(probs_ready, NT * b + i + 1)
                    if i >= 1:
                        pe.wait_ge(pT_ready, NT * b + i)
                    for k in range(i + 1):
                        mm = pe.transpose(bank(4, k * 128, k * 128 + TT, 0, TT),
                                          probs[0:TT, i % 2, k * TT:(k + 1) * TT], ident[0:TT, 0:TT])
                    mm.then_inc(p_turned, 1)

                def weigh_values(i):
                    pe.wait_ge(pT_ready, NT * b + i + 1)
                    for k in range(i + 1):
                        mm = pe.matmul(bank(6, 0, D, 0, TT), pT[0:TT, i % 2, k, :], v0[0:TT, k, :],
                                       start=k == 0, stop=k == i)
                    mm.then_inc(pv_mm, 1)

                def turn_ctx(i):
                    pe.wait_ge(ctx_ready, NT * b + i + 1)
                    if i >= 1:
                        pe.wait_ge(h_attn, NT * b + i)
                    for k in range(KD):
                        mm = pe.transpose(bank(7, k * TT, (k + 1) * TT), ctxt[0:TT, k * 128:(k + 1) * 128],
                                          ident[0:TT, 0:TT])
                    mm.then_inc(ctx_turned, 1)

                def project(i):
                    pe.wait_ge(ctxT_ready, NT * b + i + 1)
                    for k in range(KD):
                        mm = pe.matmul(bank(7, D, 2 * D, 0, TT), ctxT[:, k, :], wo0[:, k, :],
                                       start=k == 0, stop=k == KD - 1)
                    mm.then_inc(wo_mm, 1)

                scores(0)
                scores(1)
                for i in range(NT + 2):
                    if i < NT:
                        turn_probs(i)
                    if i + 2 < NT:
                        scores(i + 2)
                    if i >= 2:
                        turn_ctx(i - 2)
                    if 1 <= i <= NT:
                        weigh_values(i - 1)
                    if i < 3:
                        pe.wait_ge(ew_step, 6 * (b + 2))
                        for t in (2 * i, 2 * i + 1):
                            if t:
                                pe.wait_ge(h_tok, NT * (b + 1) + t)
                            embed(t, 5)
                    if i >= 2:
                        project(i - 2)
                    if i == NT:
                        turn_x0(b + 1)
                pe.wait_ge(h_attn, NT * b + NT)

            MB = ISH // 128

            def gate_up(c):
                for m in range(MB):
                    if m >= 3:
                        pe.wait_ge(act_s_ready, MB * c + m - 2)
                    for w, o in ((gate, 0), (up, 1)):
                        for k in range(KD):
                            mm = pe.matmul(bank(2 * (m % 3) + o, 0, HALF), w[:, k, m * 128:(m + 1) * 128],
                                           xT[:, k, 0:HALF], start=k == 0, stop=k == KD - 1)
                    mm.then_inc(gu_mm, 1)

            def down_s(c):
                pe.wait_ge(act_s_ready, MB * c + MB)
                for t in range(3):
                    if t == 2:
                        pe.wait_ge(h_shared, 3 * c + 1)
                    for m in range(MB):
                        mm = pe.matmul(bank(6 + t % 2, 0, D, 0, TT),
                                       act_s[:, m, t * TT:(t + 1) * TT], down[:, m, :],
                                       start=m == 0, stop=m == MB - 1)
                    mm.then_inc(down_mm, 1)
                pe.wait_ge(h_shared, 3 * c + 3)

            pe.wait_ge(wM_loaded, 6 * 16)
            pe.wait_ge(h_attn, NG)
            with pe.Fori(0, B) as b:
                for t in range(NT):
                    pe.wait_ge(xn_ready, NT * (b + 1) + NG + t + 1)
                    for k in range(KD):
                        mm = pe.transpose(bank(t, k * TT, (k + 1) * TT), xn[0:TT, t, k * 128:(k + 1) * 128],
                                          ident[0:TT, 0:TT])
                    mm.then_inc(xn_turned, 1)
                pe.wait_ge(xT_ready, NT * (b + 1) + NG + NT)
                for t in range(NT):
                    for k in range(KD):
                        mm = pe.matmul(bank(6, t * E, (t + 1) * E, 0, TT), xT[:, k, t * TT:(t + 1) * TT],
                                       router[:, k, :], start=k == 0, stop=k == KD - 1)
                mm.then_inc(router_mm, 1)
                gate_up(b)
                pe.wait_ge(logits_ready, b + 1)
                down_s(b)

            pe.wait_ge(hots_ready, 1)
            pe.wait_ge(consts_m, 8)
            flat = hots[0:TT, :, :].rearrange("p t e -> p (t e)")
            pe.matmul(bank(6, 0, NG * E, 0, TT), before[0:TT, :], flat, start=True, stop=True)
            pe.matmul(bank(7, 0, NG * E, 0, TT), ones[0:TT, 0:TT], flat, start=True, stop=True).then_inc(rank_mm, 1)

            def down_late(b):
                pe.wait_ge(act_s_ready, MB * (B + b + 1))
                for t in range(3):
                    n = 3 * b + t
                    if n >= 2:
                        pe.wait_ge(h_shared, 3 * B + n - 1)
                    at = b % 2 * HALF + t * TT
                    for m in range(MB):
                        mm = pe.matmul(bank(6 + n % 2, 0, D, 0, TT), act_s[:, m, at:at + TT], down[:, m, :],
                                       start=m == 0, stop=m == MB - 1)
                    mm.then_inc(down_mm, 1)

            pe.wait_ge(rows_ready, 1)
            pe.wait_ge(x_late, B)
            for n in range(MB * B):
                b, m = divmod(n, MB)
                if n >= 3:
                    pe.wait_ge(act_s_ready, MB * B + n - 2)
                for w, o in ((gate, 0), (up, 1)):
                    for k in range(KD):
                        mm = pe.matmul(bank(2 * (n % 3) + o, 0, HALF), w[:, k, m * 128:(m + 1) * 128],
                                       xT_late[:, k, b * HALF:(b + 1) * HALF], start=k == 0, stop=k == KD - 1)
                mm.then_inc(gu_mm, 1)
                if b and m == 0:
                    down_late(b - 1)
            down_late(B - 1)
            pe.wait_ge(h_shared, 6 * B)

            def turn_x(j, p):
                pe.wait_ge(xg_loaded[p], 8 * (j - p) + 16)
                for k in range(KD):
                    mm = pe.transpose(bank(p, k * SLOT, (k + 1) * SLOT), xg[:, p, k * 128:(k + 1) * 128], ident[:, :])
                mm.then_inc(xg_turned, 1)

            def turn_u(j, p):
                pe.wait_ge(u_ready, j + 1)
                for k in range(KD):
                    mm = pe.transpose(bank(4 + p, k * SLOT, (k + 1) * SLOT), u[:, p, k * 128:(k + 1) * 128], ident[:, :])
                mm.then_inc(u_turned, 1)

            def first(j, p, e):
                pe.wait_ge(xgT_ready, j + 1)
                for k in range(KD):
                    mm = pe.matmul(bank(2 + p, 0, 2 * I), xgT[:, p, k, :], fc1[:, e, k, :],
                                   start=k == 0, stop=k == KD - 1)
                mm.then_inc(fc1_mm, 1)

            def second(j, p, e, wait=True):
                pe.wait_ge(uT_ready, j + 1)
                if wait:
                    pe.wait_ge(y_ready, j - 1)
                for k in range(KD):
                    mm = pe.matmul(bank(6 + p, 0, D), uT[:, p, k, :], fc2[:, e, k, :],
                                   start=k == 0, stop=k == KD - 1)
                mm.then_inc(fc2_mm, 1)

            def expert_of(j):
                return pe.value_load(slot_e[0:1, bass.ds(j, 1)], min_val=0, max_val=E - 1)

            pe.wait_ge(rows_ready, 2)
            turn_x(0, 0)
            first(0, 0, expert_of(0))
            turn_x(1, 1)
            turn_u(0, 0)
            first(1, 1, expert_of(1))
            turn_x(2, 0)
            second(0, 0, expert_of(0), False)
            turn_u(1, 1)
            first(2, 0, expert_of(2))
            turn_x(3, 1)
            second(1, 1, expert_of(1), False)
            turn_u(2, 0)
            first(3, 1, expert_of(3))
            with pe.Fori(2, NSLOT // 2) as i:
                for p in range(2):
                    j = 2 * i + p
                    e_second, e_first = expert_of(j - 2), expert_of(j)
                    turn_x(j, p)
                    second(j - 2, p, e_second)
                    turn_u(j - 1, 1 - p)
                    first(j, p, e_first)
            second(NSLOT - 2, 0, expert_of(NSLOT - 2))
            turn_u(NSLOT - 1, 1)
            second(NSLOT - 1, 1, expert_of(NSLOT - 1))
            pe.wait_ge(absum_ready, 2)
            pe.wait_ge(y_ready, NSLOT)
            pe.matmul(bank(7, 0, 2), ones[:, :], absum[:, :], start=True, stop=True).then_inc(gamma_mm, 1)
            pe.wait_ge(tern_step, 1)

            pe.wait_ge(wC_loaded, 7 * 16)
            pe.wait_ge(y_ready, NSLOT)
            for n in range(LH):
                for k in range(KD):
                    col = (n // 2 * KD + k) * 128 + n % 2 * LAT
                    pe.matmul(bank(0, col, col + LAT), wq1[0:HD, n, k * 128:(k + 1) * 128], wk_up[0:HD, n, :],
                              start=True, stop=True)
                mm = pe.matmul(bank(2 + n // 2, n % 2 * D, (n % 2 + 1) * D), wv_up[0:HD, n, :], wo1[0:HD, n, :],
                               start=True, stop=True)
            mm.then_inc(w_mm, 1)
            pe.wait_ge(w_folded, 6)

            def turn_x1(b, t, at=7):
                pe.wait_ge(xn_ready, NT * b + 2 * NG + 2 * NT + t + 2)
                for k in range(KD):
                    for i in range(2):
                        mm = pe.transpose(bank(at, (2 * k + i) * TT, (2 * k + i + 1) * TT),
                                          xn[0:TT, t + i, k * 128:(k + 1) * 128], ident[0:TT, 0:TT])
                mm.then_inc(xn_turned, 2)

            def keys(b, c, at=7):
                lo, hi = CUTS[c]
                for k in range(KD):
                    mm = pe.matmul(bank(at, 0, hi - lo), w_kv[:, k, :], xT[:, k, lo:hi], start=k == 0, stop=k == KD - 1)
                mm.then_inc(kv_mm, 1)

            def values():
                for t in range(NT):
                    for k in range(KD):
                        mm = pe.matmul(bank(7, t * LAT, (t + 1) * LAT, 0, TT), xT[:, k, t * TT:(t + 1) * TT],
                                       w_kv[:, k, 0:LAT], start=k == 0, stop=k == KD - 1)
                mm.then_inc(kv_mm, 1)

            def queries(b, p, c, at=7):
                lo, hi = CUTS[c]
                if c == 0:
                    pe.wait_ge(w_picked, PAIRS * b + p + 1)
                for k in range(KD):
                    mm = pe.matmul(bank(at, 0, hi - lo), w_qp[:, k, :], xT[:, k, lo:hi], start=k == 0, stop=k == KD - 1)
                mm.then_inc(q_mm, 1)

            def scores1(g, kv):
                p, n, t = g // HEAD_STEPS, g // NT % 2, g % NT
                q = q_st[:, 2 * (p % 2) + n, t * TT:(t + 1) * TT]
                if g >= 2:
                    pe.wait_ge(probs1_ready, first + g - 1)
                for kh in (k_hi, k_lo):
                    for lo, hi in BANKS:
                        mm = pe.matmul(bank(2 * (g % 2), lo, hi, 0, TT), q, kh[:, kv % 2, lo:hi],
                                       start=kh is k_hi, stop=kh is k_lo)
                mm.then_inc(s1_mm, 1)

            def turn_probs1(g):
                pe.wait_ge(scaled_ready, first + g + 1)
                for c in range(2):
                    if g:
                        pe.wait_ge(p1_ready, 2 * (first + g) - 1 + c)
                    for k in range(3):
                        mm = pe.transpose(bank(4 + c, k * TT, (k + 1) * TT, 0, TT),
                                          probs1[0:TT, g % 3, (3 * c + k) * TT:(3 * c + k + 1) * TT],
                                          ident[0:TT, 0:TT])
                    mm.then_inc(p1_turned, 1)

            def weigh1(g):
                pe.wait_ge(p1_ready, 2 * (first + g) + 2)
                pe.wait_ge(o_ready, first + g + 1)
                for k in range(NT):
                    mm = pe.matmul(bank(6, 0, 2 * TT), v_st[0:TT, k, :],
                                   pT1[0:TT, g % 2, k, :, :].rearrange("p a q -> p (a q)"),
                                   start=k == 0, stop=k == NT - 1)
                mm.then_inc(pv1_mm, 1)

            def project1(p, i, at=7):
                for n in range(2):
                    mm = pe.matmul(bank(at, 0, D, 0, TT), o_T[:, n, i * TT:(i + 1) * TT],
                                   w_vo[:, 2 * p + n, :], start=n == 0, stop=n == 1)
                mm.then_inc(out1_mm, 1)

            def bank7_free(b, s):
                made = max(x for x in (*PROJECT_AT, *QUERY_AT, *TURN_AT, *KEYS_AT, VALUES_AT, 0) if x < s)
                if made in PROJECT_AT:
                    p, i = PROJECT_AT[made]
                    pe.wait_ge(h_lat, NT * (PAIRS * b + p) + i + 1)
                elif made in QUERY_AT:
                    p, c = QUERY_AT[made]
                    pe.wait_ge(q_ready, 4 * (PAIRS * b + p) + 2 * c + 2)
                elif made in TURN_AT:
                    pe.wait_ge(xT_ready, NT * (b + 1) + C_TURNED + TURN_AT[made] + 2)
                elif made in KEYS_AT:
                    pe.wait_ge(kv_ready, 3 * (b + 1) + KEYS_AT[made] + 1)
                else:
                    pe.wait_ge(kv_ready, 3 * b + 3)

            pe.wait_ge(o_zeroed, 1)
            for t in range(0, NT, 2):
                turn_x1(0, t, START_TURN[t // 2])
            pe.wait_ge(xT_ready, C_TURNED + NT)
            for c in range(2):
                keys(0, c, START_KEYS[c])
            for c in range(2):
                queries(0, 0, c, START_QUERIES[c])
            values()
            pe.wait_ge(kv_ready, 2)
            pe.wait_ge(q_ready, 4)
            first = 0
            for g in range(3):
                scores1(g, 0)
            turn_probs1(0)
            scores1(3, 0)
            with pe.Fori(0, B) as b:
                first = STEPS * b
                for s in range(1, STEPS + 1):
                    if s + 3 in range(HEAD_STEPS, STEPS + 1, HEAD_STEPS):
                        pe.wait_ge(q_ready, 4 * (PAIRS * b + (s + 3) // HEAD_STEPS + 1))
                    if s + 3 == STEPS:
                        pe.wait_ge(kv_ready, 3 * (b + 1) + 2)
                    scores1(s + 3, b if s + 3 < STEPS else b + 1)
                    turn_probs1(s)
                    if s in PROJECT_AT:
                        p, i = PROJECT_AT[s]
                        bank7_free(b, s)
                        project1((p - 1) % PAIRS, i)
                    if s in QUERY_AT:
                        bank7_free(b, s)
                        queries(b, *QUERY_AT[s])
                    if s in TURN_AT:
                        bank7_free(b, s)
                        turn_x1(b + 1, TURN_AT[s])
                    if s in KEYS_AT:
                        bank7_free(b, s)
                        pe.wait_ge(xT_ready, NT * (b + 1) + C_TURNED + NT)
                        keys(b + 1, KEYS_AT[s])
                    if s == VALUES_AT:
                        bank7_free(b, s)
                        values()
                    if s == 1:
                        pe.wait_ge(kv_ready, 3 * b + 3)
                    weigh1(s - 1)
            pe.wait_ge(kv_ready, 3 * B + 3)
            pe.wait_ge(o_ready, STEPS * B + 1)
            for i in range(NT):
                if i >= 2:
                    pe.wait_ge(h_lat, NT * PAIRS * B + i - 1)
                project1(PAIRS - 1, i, (7, 6)[i % 2])
            pe.wait_ge(h_lat, NT * (PAIRS * B + 1))
            pe.wait_ge(max1_ready, STEPS * B + 4)
            pe.wait_ge(p1_ready, 2 * (STEPS * B + 1))
            pe.wait_ge(scaled_ready, STEPS * B + 2)
            pe.wait_ge(rinv1_ready, STEPS * B + 3)
            pe.wait_ge(q_ready, 4 * (PAIRS * B + 1))

            pe.wait_ge(bias_split, 2)
            for f in range(FB):
                for half, nt in enumerate((n_hi, n_lo)):
                    mm = pe.matmul(bank(7, 0, D, 0, TT), nt[:, f, 0:TT], w_p[:, f, :],
                                   start=f == 0 and half == 0, stop=f == FB - 1 and half == 1)
            mm.then_inc(bias_mm, 1)

            def turn_x3(g):
                pe.wait_ge(fx_ready, 3 * g + 3)
                for k in range(KD):
                    for t in range(3):
                        mm = pe.transpose(bank(k, t * TT, (t + 1) * TT), xn[0:TT, t, k * 128:(k + 1) * 128],
                                          ident[0:TT, 0:TT])
                    mm.then_inc(fx_turned, 1)

            def fc(g, p, t, half, wait=True):
                s = 2 + 2 * ((3 * p + t) % 2) + half
                if half == 0:
                    pe.wait_ge(x_split, KD * g + KD)
                    if wait:
                        pe.wait_ge(gelu_ready, 3 * g + t - 1)
                for k in range(KD):
                    for part, xt in enumerate((x_hi, x_lo)):
                        mm = pe.matmul(bank(s, 0, BANK, 0, TT), xt[:, k, t * TT:(t + 1) * TT],
                                       w_f[:, k, half * BANK:(half + 1) * BANK],
                                       start=k == 0 and part == 0, stop=k == KD - 1 and part == 1)
                if half:
                    mm.then_inc(fc_mm, 1)

            def turn_n(g, p, f):
                if f == 0:
                    pe.wait_ge(norm_ready, 3 * g + 3)
                if f >= 2:
                    pe.wait_ge(n_split, FB * g + f - 1)
                for t in range(3):
                    mm = pe.transpose(bank(f % 2, t * TT, (t + 1) * TT), hidden[0:TT, p, t, f * 128:(f + 1) * 128],
                                      ident[0:TT, 0:TT])
                mm.then_inc(n_turned, 1)

            def proj(g, t, first=False):
                pe.wait_ge(n_split, FB * g + FB)
                if not first or t == 2:
                    pe.wait_ge(h_out, 3 * g + t - 1)
                for f in range(FB):
                    for half, nt in enumerate((n_hi, n_lo)):
                        mm = pe.matmul(bank(6 + t % 2, 0, D, 0, TT), nt[:, f, t * TT:(t + 1) * TT], w_p[:, f, :],
                                       start=f == 0 and half == 0, stop=f == FB - 1 and half == 1)
                mm.then_inc(proj_mm, 1)

            def step3(g, p, more=True, more2=True, first=False):
                if more:
                    pe.wait_ge(x_split, KD * g + 2 * KD)
                for f in range(FB):
                    turn_n(g, p, f)
                    if more and f < 6:
                        fc(g + 1, 1 - p, *divmod(f, 2))
                proj(g, 0, first)
                proj(g, 1, first)
                if more2:
                    turn_x3(g + 2)
                proj(g, 2, first)

            turn_x3(0)
            pe.wait_ge(b_out_ready, 1)
            for t in range(3):
                for half in range(2):
                    fc(0, 0, t, half, t == 2)
            turn_x3(1)
            step3(0, 0, first=True)
            step3(1, 1)
            with pe.Fori(1, NGR // 2 - 1) as i:
                for p in range(2):
                    step3(2 * i + p, p)
            step3(NGR - 2, 0, True, False)
            step3(NGR - 1, 1, False, False)


def layout(x, L0_tok_W, L0_tok_b, L0_attn_Wq, L0_attn_bq, L0_attn_Wk, L0_attn_bk, L0_attn_Wv, L0_attn_bv, L0_attn_Wo,
           L0_attn_bo, L0_ffn_w_router, L0_ffn_fc1_w, L0_ffn_fc2_w, L0_ffn_gate_w, L0_ffn_up_w, L0_ffn_down_w,
           L1_attn_Wq, L1_attn_Wkv_down, L1_attn_Wk_up, L1_attn_Wv_up, L1_attn_Wo, L1_ffn_W_fc, L1_ffn_ln_w,
           L1_ffn_ln_b, L1_ffn_W_proj):
    kp = lambda w: np.moveaxis(np.asarray(w).reshape(*w.shape[:-2], -1, 128, w.shape[-1]), -2, 0)
    cols = lambda v: np.asarray(v).reshape(-1, 128).T
    heads = lambda w: np.asarray(w).reshape(LH, HD, -1).transpose(1, 0, 2)
    arrays = dict(
        x=x, tok_wT=np.asarray(L0_tok_W).T, tok_b=L0_tok_b, wq0=kp(L0_attn_Wq), wk0=kp(L0_attn_Wk), wv0=kp(L0_attn_Wv),
        wo0=kp(L0_attn_Wo), bq0=cols(L0_attn_bq), bk0=cols(L0_attn_bk), bv0=L0_attn_bv, bo0=L0_attn_bo,
        router=kp(L0_ffn_w_router), fc1=kp(L0_ffn_fc1_w), fc2=kp(L0_ffn_fc2_w), gate=kp(L0_ffn_gate_w), up=kp(L0_ffn_up_w),
        down=kp(L0_ffn_down_w), wq1=heads(L1_attn_Wq), wkvdT=kp(np.asarray(L1_attn_Wkv_down).T), wk_up=heads(L1_attn_Wk_up),
        wv_up=heads(L1_attn_Wv_up), wo1=heads(np.asarray(L1_attn_Wo).T), wfcT=kp(np.asarray(L1_ffn_W_fc).T),
        ln_w=cols(L1_ffn_ln_w), ln_b=cols(L1_ffn_ln_b), wprojT=kp(np.asarray(L1_ffn_W_proj).T))
    return {n: np.ascontiguousarray(v) for n, v in arrays.items()}


def kernel(**inputs):
    import concourse.bacc as bacc
    from concourse.bass_utils import run_bass_kernel_spmd

    nc = bacc.Bacc("TRN2", target_bir_lowering=False, num_devices=1)
    arrays = layout(**inputs)
    a = {n: nc.dram_tensor(f"in_{n}", v.shape, mybir.dt.from_np(v.dtype), kind="ExternalInput").ap()
         for n, v in arrays.items()}
    out = nc.dram_tensor("out", (B, T, D), F32, kind="ExternalOutput").ap()
    build(nc, a, out)
    r = run_bass_kernel_spmd(nc, [{f"in_{n}": v for n, v in arrays.items()}], core_ids=[0])
    return r.results[0]["out"]
```
